# Optimizing a Trainium2 kernel written in Bass

```python
import numpy as np
import jax
import jax.numpy as jnp

def _softmax(x, axis=-1):
    return jax.nn.softmax(x, axis=axis)

def _gelu(x):
    return jax.nn.gelu(x, approximate=True)

def _silu(x):
    return jax.nn.silu(x)

def _sigmoid(x):
    return jax.nn.sigmoid(x)

def _layernorm(x, axis=-1, eps=1e-05):
    m = jnp.mean(x, axis=axis, keepdims=True)
    v = jnp.var(x, axis=axis, keepdims=True)
    return (x - m) / jnp.sqrt(v + eps)

def _scatter_add(tgt, idx, src, axis=0):
    return tgt.at[idx].add(src)

def _segment_sum(src, seg, n):
    return jax.ops.segment_sum(src, seg, n)
kernel_name = 'mk_seq_postln_d1_jaxref_r8_155d25'

def setup_inputs(seed: int=0):
    np.random.seed(seed)
    _w = jnp.asarray

    def _L0_attn_setup():
        import jax, jax.numpy as jnp
        import numpy as np
        import math
        N_EMBD = 128
        N_HEAD = 16
        BLOCK_SIZE = 128
        B, T = (4, 128)
        key = jax.random.key(seed)
        ks = jax.random.split(key, 7)
        C = N_EMBD
        return {'x': jax.random.normal(ks[0], (B, T, C), dtype=jnp.float32), 'Wqk': jax.random.normal(ks[1], (C, 2 * C), dtype=jnp.float32) * 0.02, 'bqk': jnp.zeros((2 * C,), dtype=jnp.float32), 'Wgate': jax.random.normal(ks[2], (C, N_HEAD), dtype=jnp.float32) * 0.02, 'bgate': jnp.zeros((N_HEAD,), dtype=jnp.float32), 'Wproj': jax.random.normal(ks[3], (C, C), dtype=jnp.float32) * 0.02, 'bproj': jnp.zeros((C,), dtype=jnp.float32)}
    _L0_attn_in = _L0_attn_setup()

    def _L0_ffn_setup():
        import jax, jax.numpy as jnp
        import numpy as np
        TOP_K = 2
        key = jax.random.key(seed)
        ks = jax.random.split(key, 6)
        B, T, H, E, F = (2, 256, 128, 8, 512)
        s = 0.02
        return {'hidden_states': jax.random.normal(ks[0], (B, T, H), dtype=jnp.float32), 'router_w': jax.random.normal(ks[1], (E, H), dtype=jnp.float32) * s, 'w1': jax.random.normal(ks[2], (E, F, H), dtype=jnp.float32) * s, 'b1': jax.random.normal(ks[3], (E, F), dtype=jnp.float32) * s, 'w2': jax.random.normal(ks[4], (E, H, F), dtype=jnp.float32) * s, 'b2': jax.random.normal(ks[5], (E, H), dtype=jnp.float32) * s}
    _L0_ffn_in = _L0_ffn_setup()
    _d = {'L0_attn_x': _L0_attn_in['x'], 'L0_attn_Wqk': _L0_attn_in['Wqk'], 'L0_attn_bqk': _L0_attn_in['bqk'], 'L0_attn_Wgate': _L0_attn_in['Wgate'], 'L0_attn_bgate': _L0_attn_in['bgate'], 'L0_attn_Wproj': _L0_attn_in['Wproj'], 'L0_attn_bproj': _L0_attn_in['bproj'], 'L0_ffn_router_w': _L0_ffn_in['router_w'], 'L0_ffn_w1': _L0_ffn_in['w1'], 'L0_ffn_b1': _L0_ffn_in['b1'], 'L0_ffn_w2': _L0_ffn_in['w2'], 'L0_ffn_b2': _L0_ffn_in['b2']}
    _x0 = _d['L0_attn_x']
    _d['L0_attn_x'] = jax.random.normal(jax.random.fold_in(jax.random.key(seed), 1), (8, 512, 128), dtype=_x0.dtype)
    del _x0
    return _d

def reference(L0_attn_x, L0_attn_Wqk, L0_attn_bqk, L0_attn_Wgate, L0_attn_bgate, L0_attn_Wproj, L0_attn_bproj, L0_ffn_router_w, L0_ffn_w1, L0_ffn_b1, L0_ffn_w2, L0_ffn_b2):

    def _L0_attn_ref(x, Wqk, bqk, Wgate, bgate, Wproj, bproj):
        import jax, jax.numpy as jnp
        import numpy as np
        import math
        N_EMBD = 128
        N_HEAD = 16
        BLOCK_SIZE = 128
        B, T = (4, 128)
        Bx, Tx, C = x.shape
        H = N_HEAD
        D = C // H
        windows = jnp.array([max(4, BLOCK_SIZE // 2 ** h) for h in range(H)], dtype=jnp.int32)
        qk = x @ Wqk + bqk
        q, k = jnp.split(qk, 2, axis=-1)
        v = k
        q = q.reshape(Bx, Tx, H, D).transpose(0, 2, 1, 3)
        k = k.reshape(Bx, Tx, H, D).transpose(0, 2, 1, 3)
        v = v.reshape(Bx, Tx, H, D).transpose(0, 2, 1, 3)
        i = jnp.arange(Tx)[:, None]
        j = jnp.arange(Tx)[None, :]
        mask = (j <= i)[None] & (j > i - windows[:, None, None])
        att = jnp.einsum('bhtd,bhsd->bhts', q, k) * (1.0 / math.sqrt(D))
        att = jnp.where(mask[None], att, -jnp.inf)
        att = jax.nn.softmax(att, axis=-1)
        out = jnp.einsum('bhts,bhsd->bhtd', att, v)
        combined = out.transpose(0, 2, 1, 3)
        gates = jax.nn.softmax(x @ Wgate + bgate, axis=-1)
        gated = (combined * gates[..., None]).reshape(Bx, Tx, C)
        return gated @ Wproj + bproj

    def _L0_ffn_ref(hidden_states, router_w, w1, b1, w2, b2):
        import jax, jax.numpy as jnp
        import numpy as np
        TOP_K = 2
        x = hidden_states
        router_logits = jnp.einsum('bth,eh->bte', x, router_w)
        topk_values, topk_indices = jax.lax.top_k(router_logits, TOP_K)
        topk_weights = jax.nn.softmax(topk_values.astype(jnp.float32), axis=-1).astype(x.dtype)
        h1 = jnp.einsum('bth,efh->btef', x, w1) + b1
        h1 = jax.nn.gelu(h1, approximate=False)
        expert_outputs = jnp.einsum('btef,ehf->bteh', h1, w2) + b2
        gather_idx = topk_indices[..., None]
        topk_expert_outputs = jnp.take_along_axis(expert_outputs, gather_idx, axis=2)
        mixed_output = jnp.sum(topk_expert_outputs * topk_weights[..., None], axis=2)
        return mixed_output
    x = L0_attn_x
    x = _layernorm(x + _L0_attn_ref(x, L0_attn_Wqk, L0_attn_bqk, L0_attn_Wgate, L0_attn_bgate, L0_attn_Wproj, L0_attn_bproj), axis=-1)
    x = _layernorm(x + _L0_ffn_ref(x, L0_ffn_router_w, L0_ffn_w1, L0_ffn_b1, L0_ffn_w2, L0_ffn_b2), axis=-1)
    return x

_drawn_inputs = setup_inputs


def setup_inputs(seed=0):
    import zlib

    import numpy as np

    out = dict(_drawn_inputs(seed))
    spreads = {'L0_attn_bqk': (0.0, 0.8), 'L0_attn_bgate': (0.0, 0.8), 'L0_attn_bproj': (0.0, 0.1)}
    factors = {'L0_attn_Wqk': 8.0,
     'L0_attn_Wgate': 8.0,
     'L0_attn_Wproj': 8.0,
     'L0_ffn_b1': 8.0,
     'L0_ffn_b2': 3.923}
    for name, (base, spread) in spreads.items():
        noise = np.random.default_rng([zlib.crc32(name.encode()), seed]).standard_normal(out[name].shape)
        drawn = base * np.exp(spread * noise) if base else spread * noise
        out[name] = jnp.asarray(drawn.astype(out[name].dtype))
    for name, factor in factors.items():
        out[name] = (out[name] * factor).astype(out[name].dtype)
    return out
```

```python
from contextlib import ExitStack

import concourse.bass as bass
from concourse import mybir

F32 = mybir.dt.float32
F32R = mybir.dt.float32r
BF16 = mybir.dt.bfloat16
I32 = mybir.dt.int32
U32 = mybir.dt.uint32
ALU = mybir.AluOpType
ACT = mybir.ActivationFunctionType
X_AXIS = mybir.AxisListType.X

P = 128
SEQS, T, C = 8, 512, 128
TILES = T // P
HEADS, D = 16, 8
SCALE = float(D) ** -0.5
EPS = 1e-5
LOW = -3.0e38

WIDE = 4
WINDOWS = [128, 64, 32, 16]
KEYS = [w + P for w in WINDOWS]
KEY_AT = [sum(KEYS[:h]) for h in range(WIDE)]
ALL_KEYS = sum(KEYS)
NARROW = HEADS - WIDE
OFFS = 4
NW = NARROW * D
PAIRS = OFFS * NARROW + OFFS
PK = PAIRS * D
KT = WIDE * D + PK

W_KREP, W_QREP, W_K, W_QG, W_PROJ, W_R = 0, 128, 256, 384, 496, 624
W_COLS = 632
B_KREP, B_QREP, B_KT, B_QG, B_PROJ = 0, 128, 256, 256 + KT, 256 + KT + 112
B_COLS = B_PROJ + 128
QG = NW + HEADS

EXPERTS, F, TOP = 8, 512, 2
FC = F // P
CAP = SEQS * T + P
ZERO_ROW = EXPERTS * CAP
ROWS = ZERO_ROW + P
ROW = C + 2
PLACES = TOP * SEQS * T
NOWHERE = 1 << 20
BLOCKS = PLACES // P + EXPERTS

K_ID, K_MN = 0, 128
K_SM = K_MN + ALL_KEYS
K_NK, K_NQ, K_NB = K_SM + PAIRS, K_SM + PAIRS + 1, K_SM + PAIRS + 2
K_I8 = K_NB + 1
K_EC = K_I8 + EXPERTS
K_TRI = K_EC + EXPERTS
K_COLS = K_TRI + P
R_B, R_E, R_M, R_TRI, R_EB = 0, BLOCKS, BLOCKS + 8, BLOCKS + 8 + 32, BLOCKS + 8 + 32 + 64
R_COLS = R_EB + 8


class Seq:

    def __init__(self, n, half, odd):
        self.n, self.half, self.u = n, half, odd


class Chain:

    def __init__(self, eng, sem, per, base=0):
        self.eng, self.sem, self.per, self.start, self.base, self.k = eng, sem, per, base, base, 0

    def round(self, n):
        assert self.k in (0, self.per), (self.k, self.per)
        self.base, self.k = n * self.per + self.start, 0

    def mark(self, ins):
        ins.then_inc(self.sem, 1)
        self.k += 1
        return ins

    def wait(self):
        self.eng.wait_ge(self.sem, self.base + self.k)

    def value(self):
        return self.base + self.k


def program(nc, x, xt, w_att, b_att, w12, b12, consts, rowc, places, out):
    ctx = ExitStack()
    with ctx:
        stage_a_only = ExitStack()
        place = [ctx]

        def sb(name, shape, dt=F32):
            return place[-1].enter_context(nc.sbuf_tensor(name, shape, dt))

        def sem(name):
            return ctx.enter_context(nc.semaphore(name))

        rows = nc.dram_tensor("expert_rows", (ROWS, ROW), F32, kind="Internal").ap()
        x1 = nc.dram_tensor("x1", (SEQS * T, C), F32, kind="Internal").ap()
        res = nc.dram_tensor("expert_results", (PLACES, C), F32, kind="Internal").ap()

        bank = [ctx.enter_context(nc.psum_tensor(f"bank{i}", [P, 512], F32)) for i in range(8)]

        kc = sb("kc", [P, K_COLS])
        rc = sb("rc", [1, R_COLS])
        place_c = sb("place_c", [P, TOP * SEQS * TILES], I32)
        tri = sb("tri", [P, P], BF16)
        ones_b = sb("ones_b", [P, P], BF16)
        ones2 = sb("ones2", [2, T], F32R)
        wah = sb("wah", [P, W_COLS], F32R)
        wal = sb("wal", [P, W_COLS], F32R)
        bas = sb("bas", [2, B_COLS], F32R)
        rowb = [[sb(f"row{k}_{u}", [P, TILES, ROW]) for k in range(TOP)] for u in range(2)]
        slot = [sb(f"slot{u}", [P, TILES, TOP], I32) for u in range(2)]
        fill = sb("fill", [P, ROW])
        mtot = [sb(f"mtot{u}", [P, EXPERTS], BF16) for u in range(2)]
        stat = sb("stat", [P, TILES, 6])
        mv = sb("mv", [P, TILES, 2])
        va = sb("va", [P, TILES])
        nwt = [sb(f"nwt{i}", [P, TILES]) for i in range(10)]
        w12h = sb("w12h", [P, EXPERTS * 2 * F], F32R)
        w12l = sb("w12l", [P, EXPERTS * 2 * F], F32R)
        b12s = sb("b12s", [2, EXPERTS * (F + C)], F32R)

        place.append(ctx.enter_context(stage_a_only))
        w12f = sb("w12f", [P, 2 * F])
        b12f = sb("b12f", [2, F + C])
        b12h = sb("b12h", [2, F + C], F32R)
        xtf = [sb(f"xtf{u}", [P, T]) for u in range(2)]
        xres = [sb(f"xres{u}", [P, TILES, C]) for u in range(2)]
        xth = [sb(f"xth{u}", [P, D + T], F32R) for u in range(2)]
        xtl = [sb(f"xtl{u}", [P, D + T], F32R) for u in range(2)]
        hi_k = sb("hi_k", [P, T], F32R)
        hi_q = sb("hi_q", [P, T], F32R)
        kst = sb("kst", [P, T], F32R)
        qst = sb("qst", [P, T], F32R)
        qg = [sb(f"qg{u}", [P, TILES, QG]) for u in range(2)]
        kt = [sb(f"kt{u}", [P, TILES, KT]) for u in range(2)]
        scored = [sb(f"scored{u}", [P, ALL_KEYS]) for u in range(2)]
        top = sb("top", [P, 2, WIDE])
        ntop = sb("ntop", [P, 2, WIDE])
        prob = [sb(f"prob{u}", [P, WIDE, 2 * P]) for u in range(2)]
        setup_only = ExitStack()
        place.append(ctx.enter_context(setup_only))
        wa = sb("wa", [P, W_COLS])
        ba = sb("ba", [2, B_COLS])
        bah = sb("bah", [2, B_COLS], F32R)
        setup_only.close()
        place.pop()
        pta = [sb(f"pta{u}", [P, WIDE, P]) for u in range(2)]
        ptb = [sb(f"ptb{u}", [P, WIDE, P]) for u in range(2)]
        sums = [sb(f"sums{u}", [P, TILES, HEADS]) for u in range(2)]
        prod = sb("prod", [P, TILES, PK])
        sc = sb("sc", [P, TILES, PAIRS])
        nmax = sb("nmax", [P, TILES, NARROW])
        nmax2 = sb("nmax2", [P, TILES])
        nmax3 = sb("nmax3", [P, TILES])
        scd = sb("scd", [P, TILES, PAIRS])
        ex = sb("ex", [P, TILES, PAIRS])
        gmax = sb("gmax", [P, TILES])
        gd = sb("gd", [P, TILES, HEADS])
        ge = sb("ge", [P, TILES, HEADS])
        gsum = sb("gsum", [P, TILES])
        xsum = sb("xsum", [P, TILES])
        xsum2 = sb("xsum2", [P, TILES])
        den = sb("den", [P, TILES, HEADS])
        rden = sb("rden", [P, TILES, HEADS])
        gn = sb("gn", [P, TILES, HEADS])
        raw = sb("raw", [P, TILES, NW])
        raw4 = sb("raw4", [P, TILES, D])
        raw5 = sb("raw5", [P, TILES, D])
        att = sb("att", [P, TILES, C])
        atth = sb("atth", [P, T], F32R)
        attl = sb("attl", [P, T], F32R)
        hid = sb("hid", [P, TILES, C])
        best = sb("best", [P, TILES, 8])
        logit = sb("logit", [P, TILES, EXPERTS])
        ibest = sb("ibest", [P, TILES, 8], U32)
        ibf = sb("ibf", [P, TILES, 8])
        diff = sb("diff", [P, TILES])
        edif = sb("edif", [P, TILES])
        edif1 = sb("edif1", [P, TILES])
        wtop = sb("wtop", [P, TILES])
        wtop2 = sb("wtop2", [P, TILES])
        oh = sb("oh", [P, TILES, TOP, EXPERTS])
        mem = sb("mem", [P, TILES, EXPERTS], BF16)
        memf = sb("memf", [P, EXPERTS])
        rank = sb("rank", [P, TILES, EXPERTS])
        slotf = sb("slotf", [P, TILES, TOP])
        pick = sb("pick", [P, TILES, TOP, EXPERTS])

        stage_a_only.close()
        place.pop()

        cnt = sb("cnt", [1, EXPERTS])
        cmp32 = sb("cmp32", [1, EXPERTS, 32])
        nblk = sb("nblk", [1, EXPERTS])
        cum3 = sb("cum3", [1, EXPERTS, EXPERTS])
        cend = sb("cend", [1, EXPERTS])
        shift = sb("shift", [1, EXPERTS])
        shift2 = sb("shift2", [1, EXPERTS])
        bge = sb("bge", [1, BLOCKS, EXPERTS])
        bexp = sb("bexp", [1, BLOCKS])
        boh = sb("boh", [1, BLOCKS, EXPERTS])
        boh2 = sb("boh2", [1, BLOCKS, EXPERTS])
        bsh = sb("bsh", [1, BLOCKS])
        bun = sb("bun", [1, BLOCKS])
        bun2 = sb("bun2", [1, BLOCKS])
        bun3 = sb("bun3", [1, BLOCKS])
        brow = sb("brow", [1, BLOCKS])
        brow2 = sb("brow2", [1, BLOCKS])
        t_row = sb("t_row", [1, BLOCKS], I32)
        t_exp = sb("t_exp", [1, BLOCKS], I32)
        t_fill = sb("t_fill", [1, EXPERTS], I32)

        RING = 4
        xb = [sb(f"xb{i}", [P, ROW]) for i in range(RING)]
        wd = [sb(f"wd{i}", [P, 2]) for i in range(RING)]
        xbh = [sb(f"xbh{i}", [P, P], F32R) for i in range(2)]
        xbl = [sb(f"xbl{i}", [P, P], F32R) for i in range(2)]
        g = [sb(f"g{i}", [P, F]) for i in range(2)]
        gth = [sb(f"gth{i}", [P, F], F32R) for i in range(2)]
        gtl = [sb(f"gtl{i}", [P, F], F32R) for i in range(2)]
        yb = [sb(f"yb{i}", [P, C]) for i in range(RING)]
        ya = [[sb(f"ya{k}_{u}", [P, TILES, C]) for k in range(TOP)] for u in range(2)]
        x1c = [sb(f"x1c{u}", [P, TILES, C]) for u in range(2)]
        ysum = sb("ysum", [P, TILES, C])
        h2 = [sb(f"h2_{u}", [P, TILES, C]) for u in range(2)]
        o2 = [sb(f"o2_{u}", [P, TILES, C]) for u in range(2)]

        names = """const_in weights_in ffn_weights_in const_ready weights_ready acredit
            x_hi x_lo kproj qproj qgproj khi qhi kst_ready qst_ready qg_copied
            ktok kt_free scores score_free ntop_ready p_ready turned pta_out ptb_out pv pv_free
            prod_ready sc_ready ex_ready pk_ready att_ready
            att_turned att_hi att_lo projected hid_ready rows_x x1_kept x1_turned x1_hi x1_lo
            logits_ready tail_free diff_ready edif_ready mem_ready ranks slots_ready
            dve_a dve_t act_a pool_a w_hi w_lo totals plan_ready fill_ready rows_filled b12_hi
            b12_ready
            x_turned xb_hi xb_lo wd_ready h_ready g_ready g_turned gt_hi gt_lo y_done y_ready
            issued dve_c c_ready rows_free setup_dve ones_ready w_used psx""".split()
        S = {n: sem(n) for n in names}
        xt_in = [sem(f"xt_in{u}") for u in range(2)]
        xres_in = [sem(f"xres_in{u}") for u in range(2)]
        expert_in = sem("expert_in")
        x1_out = [sem(f"x1_out{u}") for u in range(2)]
        scattered = [sem(f"scattered{u}") for u in range(2)]
        block_in = [sem(f"block_in{i}") for i in range(RING)]
        y_out = [sem(f"y_out{i}") for i in range(RING)]
        c_in = [sem(f"c_in{u}") for u in range(2)]
        c_out = [sem(f"c_out{u}") for u in range(2)]

        ident = kc[:, K_ID:K_ID + P]
        b_k, b_q, b_c, b_pv, b_tail = bank[4], bank[5], bank[6], bank[7], bank[3]
        score_at = [bank[0][:, 0:KEYS[0]], bank[1][:, 0:KEYS[1]], bank[2][:, 0:KEYS[2]],
                    bank[2][:, 256:256 + KEYS[3]]]

        def wait_alone(eng, semaphore, value):
            if not isinstance(value, int):
                eng.reg_mov(carrier[eng.engine], value)
                eng.wait_ge(S["const_in"], 48)
                value = carrier[eng.engine]
            eng.wait_ge(semaphore, value)

        carrier = {}

        def prepare_carrier(eng):
            carrier[eng.engine] = eng.alloc_register("carrier")
            eng.reg_mov(carrier[eng.engine], 0)

        def stage_a(eng, step):
            step(Seq(0, 0, 0), None)
            step(Seq(1, 0, 1), Seq(0, 0, 0))
            with eng.Fori(0, (SEQS - 2) // 2) as j:
                step(Seq(2 * j + 2, j + 1, 0), Seq(2 * j + 1, j, 1))
                step(Seq(2 * j + 3, j + 1, 1), Seq(2 * j + 2, j + 1, 0))
            step(None, Seq(SEQS - 1, SEQS // 2 - 1, 1))

        def b_loop(eng, b_step):
            for b in range(RING):
                b_step(b, 0, b)
            with eng.Fori(1, BLOCKS // RING - 1) as r:
                for i in range(RING):
                    b_step(r * RING + i, r, i)
            for b in range(BLOCKS - RING, BLOCKS + 2):
                b_step(b, b // RING, b % RING)

        block = ctx.enter_context(nc.Block())

        @block.sync
        def _(sp):
            sp.dma_start(xtf[0][:], xt[:, 0:T]).then_inc(xt_in[0], 16)
            sp.dma_start(wa[:], w_att).then_inc(S["weights_in"], 16)
            sp.dma_start(ba[:], b_att).then_inc(S["weights_in"], 16)
            sp.dma_start(kc[:], consts).then_inc(S["const_in"], 16)
            sp.dma_start(rc[:], rowc).then_inc(S["const_in"], 16)
            sp.dma_start(place_c[:], places).then_inc(S["const_in"], 16)
            sp.dma_start(xres[0][:], x[0:T, :].rearrange("(i p) c -> p i c", p=P)).then_inc(xres_in[0], 16)
            sp.dma_start(xtf[1][:], xt[:, T:2 * T]).then_inc(xt_in[1], 16)
            sp.dma_start(xres[1][:], x[T:2 * T, :].rearrange("(i p) c -> p i c", p=P)).then_inc(xres_in[1], 16)

            def load_expert(e):
                sp.dma_start(w12f[:], w12[:, bass.ds(e * 2 * F, 2 * F)]).then_inc(expert_in, 16)
                sp.dma_start(b12f[:], b12[:, bass.ds(e * (F + C), F + C)]).then_inc(expert_in, 16)

            load_expert(0)

            def load_x(n, s):
                sp.wait_ge(S["x_lo"], s.n + 1)
                sp.dma_start(xtf[s.u][:], xt[:, bass.ds(n * T, T)]).then_inc(xt_in[s.u], 16)

            def prefetch(s):
                load_x(s.n + 2, s)
                sp.wait_ge(S["w_lo"], s.n + 1)
                load_expert(s.n + 1)
                sp.wait_ge(S["hid_ready"], s.n + 1)
                sp.dma_start(xres[s.u][:], x[bass.ds((s.n + 2) * T, T), :].rearrange("(i p) c -> p i c", p=P)).then_inc(xres_in[s.u], 16)

            def keep_x1(s):
                sp.wait_ge(S["rows_x"], s.n + 1)
                sp.dma_start(x1[bass.ds(s.n * T, T), :].rearrange("(i p) c -> p i c", p=P),
                             rowb[s.u][0][:, :, 0:C]).then_inc(x1_out[s.u], 16)

            with sp.Fori(0, (SEQS - 2) // 2) as j:
                for s in (Seq(2 * j, j, 0), Seq(2 * j + 1, j, 1)):
                    prefetch(s)
                    keep_x1(s)
            load_x(0, Seq(SEQS - 2, SEQS // 2 - 1, 0))
            sp.wait_ge(S["w_lo"], SEQS - 1)
            load_expert(SEQS - 1)
            keep_x1(Seq(SEQS - 2, SEQS // 2 - 1, 0))
            keep_x1(Seq(SEQS - 1, SEQS // 2 - 1, 1))

            sp.wait_ge(S["fill_ready"], 1)
            sp.dma_start(rows[ZERO_ROW:ROWS, :], fill[:]).then_inc(S["rows_filled"], 16)
            sp.wait_ge(S["plan_ready"], 1)
            for e in range(EXPERTS):
                at = sp.value_load(t_fill[0:1, e:e + 1], min_val=0, max_val=ZERO_ROW - P)
                sp.dma_start(rows[bass.ds(at, P), :], fill[:]).then_inc(S["rows_filled"], 16)
            sp.wait_ge(S["rows_filled"], 16 * (EXPERTS + 1))
            for u in range(2):
                sp.wait_ge(scattered[u], 16 * TOP * TILES * SEQS // 2)

            def load_block(b, i, first):
                if not first:
                    sp.wait_ge(S["x_turned"], b - RING + 1)
                    sp.wait_ge(S["wd_ready"], b - RING + 1)
                at = sp.value_load(t_row[0:1, bass.ds(b, 1)], min_val=0, max_val=ZERO_ROW)
                sp.dma_start(xb[i][:], rows[bass.ds(at, P), :]).then_inc(block_in[i], 16)

            for b in range(RING):
                load_block(b, b, True)
            with sp.Fori(1, BLOCKS // RING) as r:
                for i in range(RING):
                    load_block(r * RING + i, i, False)

            for i in range(RING):
                sp.wait_ge(y_out[i], 16 * (BLOCKS // RING))

            for u in range(2):
                sp.wait_ge(x1_out[u], 16 * SEQS // 2)

            def load_c(n, u, half, first):
                if not first:
                    sp.wait_ge(S["c_ready"], n - 1)
                sp.dma_start(x1c[u][:], x1[bass.ds(n * T, T), :].rearrange("(i p) c -> p i c", p=P)).then_inc(c_in[u], 16)
                for k in range(TOP):
                    sp.dma_start(ya[u][k][:], res[bass.ds(n * T + k * SEQS * T, T), :].rearrange("(i p) c -> p i c", p=P)).then_inc(c_in[u], 16)

            def store_c(n, u, half):
                sp.wait_ge(S["c_ready"], n + 1)
                sp.dma_start(out[bass.ds(n * T, T), :].rearrange("(i p) c -> p i c", p=P), o2[u][:]).then_inc(c_out[u], 16)

            load_c(0, 0, 0, True)
            load_c(1, 1, 0, True)
            with sp.Fori(0, (SEQS - 2) // 2) as j:
                store_c(2 * j, 0, j)
                load_c(2 * j + 2, 0, j + 1, False)
                store_c(2 * j + 1, 1, j)
                load_c(2 * j + 3, 1, j + 1, False)
            store_c(SEQS - 2, 0, 3)
            store_c(SEQS - 1, 1, 3)
            for u in range(2):
                sp.wait_ge(c_out[u], 16 * SEQS // 2)

        @block.tensor
        def _(pe):
            def three(out_ap, lh, ll, rh, rl, last_start=False, stop=True):
                pe.matmul(out_ap, lh, rh, start=last_start, stop=False, skip_group_check=True)
                pe.matmul(out_ap, lh, rl, start=False, stop=False, skip_group_check=True)
                return pe.matmul(out_ap, ll, rh, start=False, stop=stop, skip_group_check=True)

            def bias(out_ap, lhs, rhs):
                return pe.matmul(out_ap, lhs, rhs, start=True, stop=False, skip_group_check=True)

            def scores(s, i, h):
                pe.wait_ge(S["score_free"], 4 * (4 * s.n + i) + (h + 1 if h < 2 else WIDE))
                r = slice(32 * h, 32 * h + 32)
                at = P + P * i
                at -= P
                w = WINDOWS[h] if i else 0
                return pe.matmul(score_at[h][:, WINDOWS[h] - w:], qst[r, P * i:P * i + P], kst[r, at - w:at + P],
                                 start=True, stop=True, skip_group_check=True)

            def token_keys(s, i):
                xh, xl = xth[s.u], xtl[s.u]
                pe.wait_ge(S["kt_free"], 4 * s.n + i + 1)
                bias(b_c[:, 0:KT], ones2[:, 0:P], bas[:, B_KT:B_KT + KT])
                for o in range(2 * OFFS):
                    lo = D + P * i - o
                    if o == 0:
                        a, w, cols = 0, W_K, WIDE * D + NW
                    elif o < OFFS:
                        a, w, cols = WIDE * D + NW * o, W_K + WIDE * D, NW
                    else:
                        a, w, cols = WIDE * D + NW * OFFS + D * (o - OFFS), W_K + WIDE * D, D
                    mm = three(b_c[:, a:a + cols], xh[:, lo:lo + P], xl[:, lo:lo + P],
                               wah[:, w:w + cols], wal[:, w:w + cols])
                mm.then_inc(S["ktok"], 1)

            def turn(s, i):
                pe.wait_ge(S["p_ready"], 4 * s.n + i + 1)
                if i >= 1:
                    pe.wait_ge(S["pta_out"], 4 * s.n + i + 1)
                if i >= 2:
                    pe.wait_ge(S["ptb_out"], 3 * s.n + i)
                pr = prob[i % 2]
                for h in range(WIDE):
                    mm = pe.transpose(b_k[:, P * h:P * h + P], pr[:, h, P:2 * P], ident)
                if i >= 1:
                    for h in range(WIDE):
                        mm = pe.transpose(b_q[:, P * h:P * h + P], pr[:, h, 0:P], ident)
                mm.then_inc(S["turned"], 1)

            def pv(s, i):
                pe.wait_ge(S["pta_out"], 4 * s.n + i + 2)
                pe.wait_ge(S["kt_free"], 4 * s.n + i + 2)
                if i == 0:
                    pe.wait_ge(S["qg_copied"], s.n + 1)
                if i >= 1:
                    pe.wait_ge(S["ptb_out"], 3 * s.n + i + 1)
                for h in range(WIDE):
                    o = b_pv[:, WIDE * D * i + D * h:WIDE * D * i + D * h + D]
                    mm = pe.matmul(o, pta[i % 2][:, h, :], kt[s.u][:, i, D * h:D * h + D],
                                   start=True, stop=i == 0, skip_group_check=True)
                    if i >= 1:
                        mm = pe.matmul(o, ptb[i % 2][:, h, :], kt[s.u][:, i - 1, D * h:D * h + D],
                                       start=False, stop=True, skip_group_check=True)
                mm.then_inc(S["pv"], 1)

            def end0(s):
                pe.wait_ge(S["att_ready"], s.n + 1)
                pe.wait_ge(S["tail_free"], s.n + 1)
                for i in range(TILES):
                    mm = pe.transpose(b_tail[:, P * i:P * i + P], att[:, i, :], ident)
                mm.then_inc(S["att_turned"], 1)

            def end1(s):
                pe.wait_ge(S["att_lo"], s.n + 1)
                for i in range(TILES):
                    t = slice(P * i, P * i + P)
                    bias(b_tail[:, t], ones2[:, 0:P], bas[:, B_PROJ:B_PROJ + C])
                    mm = three(b_tail[:, t], atth[:, t], attl[:, t], wah[:, W_PROJ:W_PROJ + C],
                               wal[:, W_PROJ:W_PROJ + C])
                mm.then_inc(S["projected"], 1)

            def end2(s):
                pe.wait_ge(S["rows_x"], s.n + 1)
                for i in range(TILES):
                    mm = pe.transpose(b_tail[:, P * i:P * i + P], rowb[s.u][0][:, i, 0:C], ident)
                mm.then_inc(S["x1_turned"], 1)

            def end3(s):
                pe.wait_ge(S["x1_lo"], s.n + 1)
                for i in range(TILES):
                    t = slice(P * i, P * i + P)
                    mm = three(b_tail[:, EXPERTS * i:EXPERTS * i + EXPERTS], atth[:, t], attl[:, t],
                               wah[:, W_R:W_R + EXPERTS], wal[:, W_R:W_R + EXPERTS], last_start=True)
                mm.then_inc(S["logits_ready"], 1)

            def end4(s):
                pe.wait_ge(S["mem_ready"], s.n + 1)
                for i in range(TILES):
                    o = b_tail[:, 64 + EXPERTS * i:64 + EXPERTS * i + EXPERTS]
                    pe.matmul(o, tri[:], mem[:, i, :], start=True, stop=False, skip_group_check=True)
                    for i2 in range(i):
                        pe.matmul(o, ones_b[:], mem[:, i2, :], start=False, stop=False, skip_group_check=True)
                    mm = pe.matmul(o, ones_b[:], mtot[s.u][:], start=False, stop=True, skip_group_check=True)
                mm.then_inc(S["ranks"], 1)

            def step(s, t):
                if s:
                    u = s.u
                    pe.wait_ge(S["x_lo"], s.n + 1)
                    pe.wait_ge(S["pta_out"], 4 * s.n + 1)
                    pe.wait_ge(S["ptb_out"], 3 * s.n + 1)
                    for b, wc, bc, done in ((b_k, W_KREP, B_KREP, "kproj"), (b_q, W_QREP, B_QREP, "qproj")):
                        bias(b[:], bas[:, bc:bc + P], ones2[:])
                        three(b[:], wah[:, wc:wc + P], wal[:, wc:wc + P], xth[u][:, D:],
                              xtl[u][:, D:]).then_inc(S[done], 1)
                    pe.wait_ge(S["pv_free"], s.n + 1)
                    for i in range(TILES):
                        lo = D + P * i
                        o = b_pv[:, QG * i:QG * i + QG]
                        bias(o, ones2[:, 0:P], bas[:, B_QG:B_QG + QG])
                        mm = three(o, xth[u][:, lo:lo + P], xtl[u][:, lo:lo + P],
                                   wah[:, W_QG:W_QG + QG], wal[:, W_QG:W_QG + QG])
                    mm.then_inc(S["qgproj"], 1)
                for i in range(TILES):
                    if s:
                        if i == 0:
                            pe.wait_ge(S["kst_ready"], s.n + 1)
                            pe.wait_ge(S["qst_ready"], s.n + 1)
                        for h in range(WIDE - 1):
                            scores(s, i, h).then_inc(S["scores"], 1)
                        token_keys(s, i)
                        pe.wait_ge(S["scores"], 4 * (4 * s.n + i) + 3)
                        scores(s, i, WIDE - 1).then_inc(S["scores"], 1)
                        if i >= 2:
                            pv(s, i - 2)
                        if i >= 1:
                            turn(s, i - 1)
                    if t:
                        (end0, end1, end2, end3)[i](t)
                if s:
                    turn(s, TILES - 1)
                    pv(s, TILES - 2)
                if t:
                    end4(t)
                if s:
                    pv(s, TILES - 1)

            pe.wait_ge(S["weights_ready"], 1)
            stage_a(pe, step)

            pe.wait_ge(S["tail_free"], SEQS + 1)
            pe.matmul(b_tail[:, 0:EXPERTS], ones_b[:], mtot[0][:], start=True, stop=True).then_inc(S["totals"], 1)

            ph, pt, px, py = bank[0:2], bank[2:4], bank[4], bank[5:7]

            def turn_x(b, q, i):
                pe.wait_ge(block_in[i], 16 * (q + 1))
                pe.wait_ge(S["psx"], b + 1)
                pe.transpose(px[:, 0:P], xb[i][:, 0:C], ident).then_inc(S["x_turned"], 1)

            def first_product(b, i):
                e = pe.value_load(t_exp[0:1, bass.ds(b, 1)], min_val=0, max_val=EXPERTS - 1)
                pe.wait_ge(S["xb_lo"], b + 1)
                pe.wait_ge(S["g_ready"], b + 1)
                o = ph[i % 2][:]
                pe.matmul(o, ones2[:, 0:P], b12s[:, bass.ds(e * (F + C), F)], start=True, stop=False, skip_group_check=True)
                three(o, xbh[i % 2][:], xbl[i % 2][:], w12h[:, bass.ds(e * 2 * F, F)],
                      w12l[:, bass.ds(e * 2 * F, F)]).then_inc(S["h_ready"], 1)

            def turn_g(b, i):
                pe.wait_ge(S["g_ready"], b + 3)
                pe.wait_ge(S["gt_lo"], b + 1)
                for c in range(FC):
                    mm = pe.transpose(pt[i % 2][:, P * c:P * c + P], g[i % 2][:, P * c:P * c + P], ident)
                mm.then_inc(S["g_turned"], 1)

            def second_product(b, i):
                e = pe.value_load(t_exp[0:1, bass.ds(b, 1)], min_val=0, max_val=EXPERTS - 1)
                pe.wait_ge(S["gt_lo"], b + 3)
                pe.wait_ge(S["y_ready"], b + 1)
                o = py[i % 2][:, 0:C]
                pe.matmul(o, ones2[:, 0:P], b12s[:, bass.ds(e * (F + C) + F, C)], start=True, stop=False, skip_group_check=True)
                for c in range(FC):
                    t = slice(P * c, P * c + P)
                    mm = three(o, gth[i % 2][:, t], gtl[i % 2][:, t], w12h[:, bass.ds(e * 2 * F + F + P * c, C)],
                               w12l[:, bass.ds(e * 2 * F + F + P * c, C)], stop=c == FC - 1)
                mm.then_inc(S["y_done"], 1)

            def b_step(b, q, i):
                static = isinstance(b, int)
                if not static or b + 1 < BLOCKS:
                    turn_x(b + 1, q + (i + 1) // RING, (i + 1) % RING)
                if not static or b < BLOCKS:
                    first_product(b, i)
                if not static or 1 <= b <= BLOCKS:
                    turn_g(b - 1, i - 1)
                if not static or b >= 2:
                    second_product(b - 2, i - 2)

            pe.wait_ge(S["w_lo"], SEQS)
            pe.wait_ge(S["plan_ready"], 1)
            turn_x(0, 0, 0)
            b_loop(pe, b_step)

        @block.scalar
        def _(act):
            act.sem_inc(S["kt_free"], 1)
            act.sem_inc(S["pta_out"], 1)
            act.sem_inc(S["ptb_out"], 1)
            act.sem_inc(S["g_ready"], 2)
            act.wait_ge(S["weights_in"], 32)
            act.copy(wah[:], wa[:]).then_inc(S["w_hi"], 1)
            act.copy(bah[:], ba[:]).then_inc(S["w_hi"], 1)

            def split_x(n, half, u):
                act.wait_ge(xt_in[u], 16 * (half + 1))
                act.copy(xth[u][:, D:], xtf[u][:]).then_inc(S["x_hi"], 1)

            split_x(0, 0, 0)

            def wide_exp(s, i):
                act.wait_ge(S["ntop_ready"], 4 * s.n + i + 1)
                for h in range(WIDE):
                    w = WINDOWS[h] if i else 0
                    a = act.activation(prob[i % 2][:, h, P - w:2 * P],
                                       scored[i % 2][:, KEY_AT[h] + WINDOWS[h] - w:KEY_AT[h] + KEYS[h]], ACT.Exp,
                                       bias=ntop[:, i % 2, h:h + 1], scale=SCALE,
                                       accum_out=sums[s.u][:, i, h:h + 1])
                a.then_inc(S["p_ready"], 1)

            def copy_turned(s, i):
                act.wait_ge(S["turned"], 4 * s.n + i + 1)
                act.copy(pta[i % 2][:].rearrange("p h q -> p (h q)"), b_k[:]).then_inc(S["pta_out"], 1)
                if i >= 1:
                    act.copy(ptb[i % 2][:].rearrange("p h q -> p (h q)"), b_q[:]).then_inc(S["ptb_out"], 1)

            def end(t, i):
                if i == 0:
                    act.wait_ge(S["att_turned"], t.n + 1)
                    act.copy(atth[:], b_tail[:]).then_inc(S["att_hi"], 1)
                if i == 2:
                    act.wait_ge(S["x1_turned"], t.n + 1)
                    act.copy(atth[:], b_tail[:]).then_inc(S["x1_hi"], 1)
                    if_free(t)
                    act.copy(rowb[t.u][1][:, :, 0:C], rowb[t.u][0][:, :, 0:C]).then_inc(S["x1_kept"], 1)
                if i == 3:
                    act.wait_ge(S["diff_ready"], t.n + 1)
                    act.activation(edif[:], diff[:], ACT.Exp).then_inc(S["edif_ready"], 1)

            def if_free(t):
                act.wait_ge(S["rows_free"], t.n + 1)

            def step(s, t):
                if s:
                    act.wait_ge(S["kproj"], s.n + 1)
                    act.copy(hi_k[:], b_k[:]).then_inc(S["khi"], 1)
                    act.wait_ge(S["qproj"], s.n + 1)
                    act.copy(hi_q[:], b_q[:]).then_inc(S["qhi"], 1)
                    act.wait_ge(S["qgproj"], s.n + 1)
                    act.copy(qg[s.u][:].rearrange("p i c -> p (i c)"), b_pv[:, 0:TILES * QG]).then_inc(S["qg_copied"], 1)
                for i in range(TILES):
                    if s:
                        act.wait_ge(S["ktok"], 4 * s.n + i + 1)
                        act.copy(kt[s.u][:, i, :], b_c[:, 0:KT]).then_inc(S["kt_free"], 1)
                        wide_exp(s, i)
                        if i >= 1:
                            copy_turned(s, i - 1)
                    if t:
                        end(t, i)
                if s:
                    act.wait_ge(S["sc_ready"], s.n + 1)
                    act.activation(ex[:].rearrange("p i c -> p (i c)"), scd[:].rearrange("p i c -> p (i c)"), ACT.Exp, scale=SCALE)
                    act.activation(ge[:].rearrange("p i c -> p (i c)"), gd[:].rearrange("p i c -> p (i c)"), ACT.Exp).then_inc(S["ex_ready"], 1)
                    copy_turned(s, TILES - 1)
                    act.wait_ge(expert_in, 32 * (s.n + 1))
                    act.copy(w12h[:, bass.ds(s.n * 2 * F, 2 * F)], w12f[:]).then_inc(S["w_hi"], 1)
                    if not (isinstance(s.n, int) and s.n == 0):
                        act.wait_ge(S["w_lo"], s.n)
                    act.copy(b12h[:], b12f[:]).then_inc(S["w_hi"], 1)
                    split_x(s.n + 1, s.half + s.u, 1 - s.u)

            stage_a(act, step)

            ph, pt, px = bank[0:2], bank[2:4], bank[4]

            def x_hi(b, i):
                act.wait_ge(S["x_turned"], b + 1)
                act.copy(xbh[i % 2][:], px[:, 0:P]).then_inc(S["xb_hi"], 1)

            def b_step(b, q, i):
                static = isinstance(b, int)
                if not static or b + 1 < BLOCKS:
                    x_hi(b + 1, i + 1)
                if not static or b < BLOCKS:
                    act.wait_ge(S["h_ready"], b + 1)
                    act.activation(g[i % 2][:], ph[i % 2][:], ACT.Gelu).then_inc(S["g_ready"], 1)
                if not static or 1 <= b <= BLOCKS:
                    act.wait_ge(S["g_turned"], b)
                    act.copy(gth[(i - 1) % 2][:], pt[(i - 1) % 2][:]).then_inc(S["gt_hi"], 1)

            x_hi(0, 0)
            b_loop(act, b_step)


        @block.gpsimd
        def _(pool):
            prepare_carrier(pool)
            pool.memset(fill[:], 0.0).then_inc(S["pool_a"], 1)
            pool.wait_ge(S["pool_a"], 1)
            pool.memset(fill[:, C + 1:C + 2].bitcast(I32), NOWHERE).then_inc(S["fill_ready"], 1)
            pool.sem_inc(S["rows_free"], 2)

            def step(s, t):
                if s:
                    pool.wait_ge(S["qg_copied"], s.n + 1)
                    for i in range(TILES):
                        pool.wait_ge(S["kt_free"], 4 * s.n + i + 2)
                        if i == 0:
                            pool.wait_ge(S["pv_free"], s.n + 1)
                        k, q = kt[s.u][:, i, WIDE * D:KT], qg[s.u][:, i, 0:NW]
                        pool.tensor_tensor(prod[:, i, 0:OFFS * NW].rearrange("p (o c) -> p o c", o=OFFS),
                                           k[:, 0:OFFS * NW].rearrange("p (o c) -> p o c", o=OFFS),
                                           q.unsqueeze(1).broadcast_to([P, OFFS, NW]), ALU.mult)
                        pool.tensor_tensor(prod[:, i, OFFS * NW:PK].rearrange("p (o c) -> p o c", o=OFFS),
                                           k[:, OFFS * NW:PK].rearrange("p (o c) -> p o c", o=OFFS),
                                           q[:, 0:D].unsqueeze(1).broadcast_to([P, OFFS, D]), ALU.mult).then_inc(S["prod_ready"], 1)
                    pool.wait_ge(S["ex_ready"], s.n + 1)
                    for i in range(TILES):
                        pool.tensor_tensor(prod[:, i, :].rearrange("p (c d) -> p c d", d=D),
                                           kt[s.u][:, i, WIDE * D:KT].rearrange("p (c d) -> p c d", d=D),
                                           ex[:, i, :].unsqueeze(2).broadcast_to([P, PAIRS, D]), ALU.mult).then_inc(S["pk_ready"], 1)
                if t:
                    wait_alone(pool, S["slots_ready"], t.n + 1)
                    for i in range(TILES):
                        for k in range(TOP):
                            pool.indirect_dma_start(rows, bass.IndirectOffsetOnAxis(ap=slot[t.u][:, i, k:k + 1], axis=0),
                                                    rowb[t.u][k][:, i, :], None, bounds_check=ZERO_ROW - 1,
                                                    oob_is_err=False).then_inc(scattered[t.u], 16)

            def step_and_free(s, t):
                if t and not (isinstance(t.n, int) and t.n == 0):
                    half = t.half if t.u else t.half - 1
                    pool.wait_ge(scattered[1 - t.u], 16 * TOP * TILES * (half + 1))
                    pool.wait_ge(x1_out[1 - t.u], 16 * (half + 1))
                    pool.sem_inc(S["rows_free"], 1)
                step(s, t)

            stage_a(pool, step_and_free)

            def scatter(b, q, i):
                wait_alone(pool, S["y_ready"], b + 3)
                pool.indirect_dma_start(res, bass.IndirectOffsetOnAxis(ap=wd[i][:, 1:2].bitcast(I32), axis=0),
                                        yb[i][:], None, bounds_check=PLACES - 1,
                                        oob_is_err=False).then_inc(y_out[i], 16)
                pool.sem_inc(S["issued"], 1)

            with pool.Fori(0, BLOCKS // RING) as r:
                for i in range(RING):
                    scatter(r * RING + i, r, i)

        @block.vector
        def _(dve):
            prepare_carrier(dve)
            dve.sem_inc(S["score_free"], WIDE)
            dve.sem_inc(S["pv_free"], 1)
            dve.sem_inc(S["tail_free"], 1)
            dve.sem_inc(S["psx"], 1)
            dve.sem_inc(S["gt_lo"], 2)
            dve.sem_inc(S["y_ready"], 2)
            for u in range(2):
                dve.memset(xth[u][:, 0:D].bitcast(F32), 0.0)
                dve.memset(xtl[u][:, 0:D].bitcast(F32), 0.0)
                dve.memset(prob[u][:], 0.0)
            dve.memset(mtot[0][:], 0.0)
            dve.memset(ones_b[:], 1.0)
            dve.memset(ones2[:].bitcast(F32), 1.0)
            dve.wait_ge(S["const_in"], 48)
            dve.tensor_copy(tri[:], kc[:, K_TRI:K_TRI + P])
            dve.wait_ge(S["w_hi"], 2)
            dve.tensor_tensor(wal[:], wa[:], wah[:].bitcast(F32), ALU.subtract)
            dve.scalar_tensor_tensor(bas[:], bah[:].bitcast(F32), kc[0:2, K_NB:K_NB + 1], ba[:],
                                     ALU.mult, ALU.add).then_inc(S["weights_ready"], 1)

            def x_lo(n, u):
                dve.wait_ge(S["x_hi"], n + 1)
                dve.tensor_tensor(xtl[u][:, D:], xtf[u][:], xth[u][:, D:].bitcast(F32), ALU.subtract).then_inc(S["x_lo"], 1)

            x_lo(0, 0)
            own = Chain(dve, S["dve_a"], 22)
            tail = Chain(dve, S["dve_t"], 27)

            def rstd(chain, v):
                y = nwt[0]
                chain.mark(dve.tensor_scalar(y[:].bitcast(I32), v[:].bitcast(I32), -0.5, 1597463007.0, ALU.mult, ALU.add))
                for i in range(3):
                    a, b, y2 = nwt[3 * i + 1], nwt[3 * i + 2], nwt[3 * i + 3]
                    chain.wait()
                    chain.mark(dve.tensor_tensor(a[:], y[:], y[:], ALU.mult))
                    chain.wait()
                    chain.mark(dve.scalar_tensor_tensor(b[:], a[:], -0.5, v[:], ALU.mult, ALU.mult))
                    chain.wait()
                    chain.mark(dve.scalar_tensor_tensor(y2[:], b[:], 1.5, y[:], ALU.add, ALU.mult))
                    y = y2
                chain.wait()
                return y

            def statistics(chain, h):
                for i in range(TILES):
                    ins = dve.bn_stats(stat[:, i, :], h[:, i, :])
                chain.mark(ins)
                wait_alone(dve, chain.sem, chain.value())
                for i in range(TILES):
                    ins = dve.bn_aggr(mv[:, i, :], stat[:, i, :])
                chain.mark(ins)
                chain.wait()
                chain.mark(dve.tensor_scalar(va[:], mv[:, :, 1], EPS, None, ALU.add))
                chain.wait()
                return rstd(chain, va)

            def window(s, i):
                for h in range(WIDE):
                    wait_alone(dve, S["scores"], 4 * (4 * s.n + i) + (h + 1 if h < 2 else WIDE))
                    if i >= 2 and h == 0:
                        dve.wait_ge(S["p_ready"], 4 * s.n + i - 1)
                    a = WINDOWS[h] if i == 0 else 0
                    dve.tensor_tensor_reduce(
                        scored[i % 2][:, KEY_AT[h] + a:KEY_AT[h] + KEYS[h]], score_at[h][:, a:],
                        kc[:, K_MN + KEY_AT[h] + a:K_MN + KEY_AT[h] + KEYS[h]], 1.0, LOW, ALU.add, ALU.max,
                        top[:, i % 2, h:h + 1]).then_inc(S["score_free"], 1)
                dve.wait_ge(S["score_free"], 4 * (4 * s.n + i) + 2 * WIDE)
                dve.tensor_scalar(ntop[:, i % 2, :], top[:, i % 2, :], -SCALE, None, ALU.mult).then_inc(S["ntop_ready"], 1)

            def narrow_scores(s, i):
                dve.wait_ge(S["prod_ready"], 4 * s.n + i + 1)
                own.mark(dve.tensor_reduce(sc[:, i, :], prod[:, i, :].rearrange("p (c d) -> p c d", d=D), X_AXIS, ALU.add))

            def end(t, i):
                u = t.u
                if i == 0:
                    dve.wait_ge(S["att_hi"], t.n + 1)
                    dve.tensor_tensor(attl[:], b_tail[:], atth[:].bitcast(F32), ALU.subtract).then_inc(S["att_lo"], 1)
                if i == 1:
                    dve.wait_ge(S["projected"], t.n + 1)
                    dve.wait_ge(xres_in[u], 16 * (t.half + 1))
                    dve.tensor_tensor(hid[:].rearrange("p i c -> p (i c)"), b_tail[:],
                                      xres[u][:].rearrange("p i c -> p (i c)"), ALU.add).then_inc(S["hid_ready"], 1)
                    dve.wait_ge(S["hid_ready"], t.n + 1)
                    y = statistics(tail, hid)
                    dve.wait_ge(S["rows_free"], t.n + 1)
                    for k in range(TILES):
                        ins = dve.tensor_scalar(rowb[u][0][:, k, 0:C], hid[:, k, :], mv[:, k, 0:1], y[:, k:k + 1],
                                                ALU.subtract, ALU.mult)
                    ins.then_inc(S["rows_x"], 1)
                    for k in range(TOP):
                        ins = dve.tensor_copy(rowb[u][k][:, :, C + 1:C + 2].bitcast(I32),
                                              place_c[:, bass.ds(4 * t.n + k * SEQS * TILES, TILES)].unsqueeze(2))
                    tail.mark(ins)
                if i == 2:
                    dve.wait_ge(S["x1_hi"], t.n + 1)
                    dve.tensor_tensor(attl[:], b_tail[:], atth[:].bitcast(F32), ALU.subtract).then_inc(S["x1_lo"], 1)
                if i == 3:
                    dve.wait_ge(S["logits_ready"], t.n + 1)
                    tail.mark(dve.tensor_copy(logit[:].rearrange("p i e -> p (i e)"), b_tail[:, 0:TILES * EXPERTS]))
                    wait_alone(dve, tail.sem, tail.value())
                    for k in range(TILES):
                        ins = dve.max(best[:, k, :], logit[:, k, :])
                    tail.mark(ins)
                    wait_alone(dve, tail.sem, tail.value())
                    for k in range(TILES):
                        ins = dve.max_index(ibest[:, k, :], best[:, k, :], logit[:, k, :])
                    tail.mark(ins)
                    dve.tensor_tensor(diff[:], best[:, :, 1], best[:, :, 0], ALU.subtract).then_inc(S["diff_ready"], 1)
                    tail.wait()
                    tail.mark(dve.tensor_copy(ibf[:], ibest[:]))
                    tail.wait()
                    tail.mark(dve.tensor_tensor(oh[:], ibf[:, :, 0:TOP].unsqueeze(3).broadcast_to([P, TILES, TOP, EXPERTS]),
                                                kc[:, K_I8:K_I8 + EXPERTS].unsqueeze(1).unsqueeze(1).broadcast_to([P, TILES, TOP, EXPERTS]),
                                                ALU.is_equal))
                    tail.wait()
                    dve.tensor_tensor(mem[:], oh[:, :, 0, :], oh[:, :, 1, :], ALU.add).then_inc(S["mem_ready"], 1)
                    dve.wait_ge(S["edif_ready"], t.n + 1)
                    tail.mark(dve.tensor_scalar(edif1[:], edif[:], 1.0, None, ALU.add))
                    tail.wait()
                    tail.mark(dve.reciprocal(wtop[:], edif1[:]))
                    tail.wait()
                    tail.mark(dve.tensor_copy(rowb[u][0][:, :, C:C + 1], wtop[:].unsqueeze(2)))
                    tail.mark(dve.tensor_tensor(rowb[u][1][:, :, C:C + 1], wtop[:].unsqueeze(2), edif[:].unsqueeze(2), ALU.mult))
                    dve.wait_ge(S["mem_ready"], t.n + 1)
                    tail.mark(dve.tensor_reduce(memf[:], mem[:].rearrange("p i e -> p e i"), X_AXIS, ALU.add))
                    tail.wait()
                    tail.mark(dve.tensor_tensor(mtot[1 - u][:], mtot[u][:], memf[:], ALU.add))
                if i == 4:
                    dve.wait_ge(S["ranks"], t.n + 1)
                    dve.tensor_tensor(rank[:], b_tail[:, 64:64 + TILES * EXPERTS].rearrange("p (i e) -> p i e", e=EXPERTS),
                                      kc[:, K_EC:K_EC + EXPERTS].unsqueeze(1).broadcast_to([P, TILES, EXPERTS]),
                                      ALU.add).then_inc(S["tail_free"], 1)
                    dve.wait_ge(S["tail_free"], t.n + 2)
                    tail.mark(dve.tensor_tensor(pick[:], oh[:], rank[:].unsqueeze(2).broadcast_to([P, TILES, TOP, EXPERTS]), ALU.mult))
                    tail.wait()
                    dve.wait_ge(S["x1_kept"], t.n + 1)
                    tail.mark(dve.tensor_reduce(slotf[:], pick[:], X_AXIS, ALU.add))
                    tail.wait()
                    dve.tensor_copy(slot[u][:], slotf[:]).then_inc(S["slots_ready"], 1)

            def step(s, t):
                if s:
                    own.round(s.n)
                    dve.wait_ge(S["khi"], s.n + 1)
                    dve.scalar_tensor_tensor(kst[:], hi_k[:].bitcast(F32), kc[:, K_NK:K_NK + 1], b_k[:],
                                             ALU.mult, ALU.add).then_inc(S["kst_ready"], 1)
                    dve.wait_ge(S["qhi"], s.n + 1)
                    dve.scalar_tensor_tensor(qst[:], hi_q[:].bitcast(F32), kc[:, K_NQ:K_NQ + 1], b_q[:],
                                             ALU.mult, ALU.add).then_inc(S["qst_ready"], 1)
                if t:
                    tail.round(t.n)
                for i in range(TILES):
                    if s:
                        window(s, i)
                        if i >= 1:
                            narrow_scores(s, i - 1)
                    if t:
                        end(t, i)
                if s:
                    u = s.u
                    narrow_scores(s, TILES - 1)
                    own.wait()
                    own.mark(dve.tensor_tensor(sc[:, 0, :], sc[:, 0, :], kc[:, K_SM:K_SM + PAIRS], ALU.add))
                    gl = qg[u][:, :, NW:QG]
                    own.mark(dve.tensor_reduce(gmax[:], gl, X_AXIS, ALU.max))
                    own.wait()
                    n4 = OFFS * NARROW
                    by_head = sc[:, :, 0:n4].rearrange("p i (o h) -> p i h o", o=OFFS)
                    own.mark(dve.tensor_reduce(nmax[:], by_head, X_AXIS, ALU.max))
                    own.mark(dve.tensor_reduce(nmax2[:], sc[:, :, n4:PAIRS], X_AXIS, ALU.max))
                    own.mark(dve.tensor_tensor(gd[:], gl, gmax[:].unsqueeze(2).broadcast_to([P, TILES, HEADS]), ALU.subtract))
                    own.wait()
                    own.mark(dve.tensor_tensor(nmax3[:], nmax2[:], nmax[:, :, 0], ALU.max))
                    own.wait()
                    own.mark(dve.tensor_copy(nmax[:, :, 0], nmax3[:]))
                    own.mark(dve.tensor_tensor(scd[:, :, n4:PAIRS], sc[:, :, n4:PAIRS],
                                               nmax3[:].unsqueeze(2).broadcast_to([P, TILES, OFFS]), ALU.subtract))
                    own.wait()
                    for i in range(TILES):
                        ins = dve.tensor_tensor(scd[:, i, 0:n4].rearrange("p (o h) -> p o h", o=OFFS),
                                                sc[:, i, 0:n4].rearrange("p (o h) -> p o h", o=OFFS),
                                                nmax[:, i, :].unsqueeze(1).broadcast_to([P, OFFS, NARROW]), ALU.subtract)
                    ins.then_inc(S["sc_ready"], 1)
                if t:
                    end(t, 4)
                if s:
                    dve.wait_ge(S["ex_ready"], s.n + 1)
                    dve.wait_ge(S["p_ready"], 4 * s.n + 4)
                    own.mark(dve.tensor_reduce(sums[u][:, :, WIDE:HEADS], ex[:, :, 0:n4].rearrange("p i (o h) -> p i h o", o=OFFS), X_AXIS, ALU.add))
                    own.mark(dve.tensor_reduce(xsum[:], ex[:, :, n4:PAIRS], X_AXIS, ALU.add))
                    own.mark(dve.tensor_reduce(gsum[:], ge[:], X_AXIS, ALU.add))
                    own.wait()
                    own.mark(dve.tensor_tensor(xsum2[:], xsum[:], sums[u][:, :, WIDE], ALU.add))
                    own.wait()
                    own.mark(dve.tensor_copy(sums[u][:, :, WIDE], xsum2[:]))
                    own.wait()
                    own.mark(dve.tensor_tensor(den[:], sums[u][:], gsum[:].unsqueeze(2).broadcast_to([P, TILES, HEADS]), ALU.mult))
                    own.wait()
                    own.mark(dve.reciprocal(rden[:], den[:]))
                    own.wait()
                    own.mark(dve.tensor_tensor(gn[:], ge[:], rden[:], ALU.mult))
                    dve.wait_ge(S["pk_ready"], 4 * s.n + 4)
                    dve.tensor_reduce(raw[:], prod[:, :, 0:OFFS * NW].rearrange("p i (o c) -> p i c o", o=OFFS), X_AXIS, ALU.add)
                    own.mark(dve.tensor_reduce(raw4[:], prod[:, :, OFFS * NW:PK].rearrange("p i (o c) -> p i c o", o=OFFS), X_AXIS, ALU.add))
                    own.wait()
                    ins = dve.tensor_tensor(raw5[:], raw4[:], raw[:, :, 0:D], ALU.add)
                    own_last(ins)
                    dve.tensor_tensor(att[:, :, WIDE * D + D:C].rearrange("p i (h d) -> p i h d", d=D),
                                      raw[:, :, D:NW].rearrange("p i (h d) -> p i h d", d=D),
                                      gn[:, :, WIDE + 1:HEADS].unsqueeze(3).broadcast_to([P, TILES, NARROW - 1, D]), ALU.mult)
                    dve.tensor_tensor(att[:, :, WIDE * D:WIDE * D + D], raw5[:],
                                      gn[:, :, WIDE:WIDE + 1].broadcast_to([P, TILES, D]), ALU.mult)
                    dve.wait_ge(S["pv"], 4 * s.n + 4)
                    dve.tensor_tensor(att[:, :, 0:WIDE * D].rearrange("p i (h d) -> p i h d", d=D),
                                      b_pv[:, 0:TILES * WIDE * D].rearrange("p (i h d) -> p i h d", i=TILES, d=D),
                                      gn[:, :, 0:WIDE].unsqueeze(3).broadcast_to([P, TILES, WIDE, D]), ALU.mult).then_inc(S["att_ready"], 1)
                    dve.wait_ge(S["att_ready"], s.n + 1)
                    dve.sem_inc(S["pv_free"], 1)
                    dve.wait_ge(S["w_hi"], 2 * s.n + 4)
                    e = bass.ds(s.n * 2 * F, 2 * F)
                    dve.tensor_tensor(w12l[:, e], w12f[:], w12h[:, e].bitcast(F32), ALU.subtract)
                    dve.scalar_tensor_tensor(b12s[:, bass.ds(s.n * (F + C), F + C)], b12h[:].bitcast(F32),
                                             kc[0:2, K_NB:K_NB + 1], b12f[:], ALU.mult, ALU.add).then_inc(S["w_lo"], 1)
                    x_lo(s.n + 1, 1 - u)

            def own_last(ins):
                own.mark(ins)
                own.wait()

            stage_a(dve, step)

            plan = Chain(dve, S["setup_dve"], 0)
            n = EXPERTS
            dve.wait_ge(S["totals"], 1)
            row = lambda a, k: rc[0:1, a:a + k]

            def then(ins):
                plan.mark(ins)
                plan.wait()

            then(dve.tensor_copy(cnt[:], b_tail[0:1, 0:n]))
            then(dve.tensor_tensor(t_fill[:], cnt[:], row(R_EB, n), ALU.add))
            then(dve.tensor_tensor(cmp32[:], cnt[:].unsqueeze(2).broadcast_to([1, n, 32]),
                                   row(R_M, 32).unsqueeze(1).broadcast_to([1, n, 32]), ALU.is_gt))
            then(dve.tensor_reduce(nblk[:], cmp32[:], X_AXIS, ALU.add))
            then(dve.tensor_tensor(cum3[:], nblk[:].unsqueeze(1).broadcast_to([1, n, n]),
                                   row(R_TRI, n * n).rearrange("p (a b) -> p a b", b=n), ALU.mult))
            then(dve.tensor_reduce(cend[:], cum3[:], X_AXIS, ALU.add))
            then(dve.tensor_tensor(shift[:], nblk[:], cend[:], ALU.subtract))
            then(dve.scalar_tensor_tensor(shift2[:], row(R_EB, n), 1.0 / P, shift[:], ALU.mult, ALU.add))
            wide = [1, BLOCKS, n]
            then(dve.tensor_tensor(bge[:], row(R_B, BLOCKS).unsqueeze(2).broadcast_to(wide),
                                   cend[:].unsqueeze(1).broadcast_to(wide), ALU.is_ge))
            then(dve.tensor_reduce(bexp[:], bge[:], X_AXIS, ALU.add))
            then(dve.tensor_tensor(boh[:], bexp[:].unsqueeze(2).broadcast_to(wide),
                                   row(R_E, n).unsqueeze(1).broadcast_to(wide), ALU.is_equal))
            then(dve.tensor_tensor(boh2[:], boh[:], shift2[:].unsqueeze(1).broadcast_to(wide), ALU.mult))
            then(dve.tensor_reduce(bsh[:], boh2[:], X_AXIS, ALU.add))
            then(dve.tensor_tensor(brow[:], bsh[:], row(R_B, BLOCKS), ALU.add))
            then(dve.tensor_scalar(bun[:], bexp[:], float(n), None, ALU.is_ge))
            then(dve.tensor_scalar(bun2[:], brow[:], -1.0, float(ZERO_ROW // P), ALU.mult, ALU.add))
            then(dve.tensor_tensor(bun3[:], bun2[:], bun[:], ALU.mult))
            then(dve.tensor_tensor(brow2[:], brow[:], bun3[:], ALU.add))
            then(dve.tensor_scalar(t_row[:], brow2[:], float(P), None, ALU.mult))
            dve.tensor_scalar(t_exp[:], bexp[:], float(n - 1), None, ALU.min).then_inc(S["plan_ready"], 1)

            pt, px, py = bank[2:4], bank[4], bank[5:7]

            def x_part(b, q, i):
                dve.wait_ge(S["xb_hi"], b + 1)
                dve.tensor_tensor(xbl[i % 2][:], px[:, 0:P], xbh[i % 2][:].bitcast(F32), ALU.subtract).then_inc(S["xb_lo"], 1)
                dve.wait_ge(S["xb_lo"], b + 1)
                dve.sem_inc(S["psx"], 1)
                if not (isinstance(b, int) and b < RING):
                    dve.wait_ge(S["issued"], b - RING + 1)
                    dve.wait_ge(y_out[i], 16 * q)
                dve.tensor_copy(wd[i][:], xb[i][:, C:ROW]).then_inc(S["wd_ready"], 1)

            def b_step(b, q, i):
                static = isinstance(b, int)
                if not static or b + 1 < BLOCKS:
                    x_part(b + 1, q + (i + 1) // RING, (i + 1) % RING)
                if not static or 1 <= b <= BLOCKS:
                    j = (i - 1) % 2
                    dve.wait_ge(S["gt_hi"], b)
                    dve.tensor_tensor(gtl[j][:], pt[j][:], gth[j][:].bitcast(F32), ALU.subtract).then_inc(S["gt_lo"], 1)
                if not static or b >= 2:
                    k = (i - 2) % RING
                    dve.wait_ge(S["y_done"], b - 1)
                    dve.wait_ge(S["wd_ready"], b - 1)
                    dve.tensor_scalar(yb[k][:], py[i % 2][:, 0:C], wd[k][:, 0:1], None, ALU.mult).then_inc(S["y_ready"], 1)

            x_part(0, 0, 0)
            b_loop(dve, b_step)

            fin = Chain(dve, S["dve_c"], 15)

            def last(n, u, half):
                fin.round(n)
                flat = lambda a: a.rearrange("p i c -> p (i c)")
                dve.wait_ge(c_in[u], 16 * (TOP + 1) * (half + 1))
                fin.mark(dve.tensor_tensor(ysum[:], ya[u][0][:], ya[u][1][:], ALU.add))
                fin.wait()
                fin.mark(dve.tensor_tensor(h2[u][:], ysum[:], x1c[u][:], ALU.add))
                fin.wait()
                y = statistics(fin, h2[u])
                if not (isinstance(n, int) and n < 2):
                    dve.wait_ge(c_out[u], 16 * half)
                for k in range(TILES):
                    ins = dve.tensor_scalar(o2[u][:, k, :], h2[u][:, k, :], mv[:, k, 0:1], y[:, k:k + 1],
                                            ALU.subtract, ALU.mult)
                ins.then_inc(S["c_ready"], 1)
                dve.wait_ge(S["c_ready"], n + 1)

            last(0, 0, 0)
            last(1, 1, 0)
            with dve.Fori(1, SEQS // 2) as j:
                last(2 * j, 0, j)
                last(2 * j + 1, 1, j)


def kernel(L0_attn_x, L0_attn_Wqk, L0_attn_bqk, L0_attn_Wgate, L0_attn_bgate, L0_attn_Wproj,
           L0_attn_bproj, L0_ffn_router_w, L0_ffn_w1, L0_ffn_b1, L0_ffn_w2, L0_ffn_b2):
    import numpy as np
    import concourse.bacc as bacc
    from concourse.bass_utils import run_bass_kernel_spmd

    f4 = np.float32
    x = np.asarray(L0_attn_x).reshape(SEQS * T, C)
    wqk, bqk = np.asarray(L0_attn_Wqk), np.asarray(L0_attn_bqk)
    rep = np.array([D * h + d for h in range(WIDE) for _ in range(4) for d in range(D)])
    w_att = np.concatenate([wqk[:, C + rep], wqk[:, rep], wqk[:, C:2 * C], wqk[:, WIDE * D:C],
                            np.asarray(L0_attn_Wgate), np.asarray(L0_attn_Wproj),
                            np.asarray(L0_ffn_router_w).T], axis=1)
    bk = bqk[C:2 * C]
    nk = bk[WIDE * D:]
    b_att = np.concatenate([bk[rep], bqk[rep], bk, nk, nk, nk] + [nk[:D]] * OFFS
                           + [bqk[WIDE * D:C], np.asarray(L0_attn_bgate), np.asarray(L0_attn_bproj)])
    b_att = np.stack([b_att, b_att])
    w1 = np.asarray(L0_ffn_w1).transpose(2, 0, 1).reshape(C, EXPERTS * F)
    w2 = np.asarray(L0_ffn_w2).reshape(EXPERTS, C, FC, P).transpose(3, 0, 2, 1).reshape(P, EXPERTS * F)
    w12 = np.concatenate([w1.reshape(P, EXPERTS, F), w2.reshape(P, EXPERTS, F)], axis=2).reshape(P, EXPERTS * 2 * F)
    b12 = np.concatenate([np.asarray(L0_ffn_b1), np.asarray(L0_ffn_b2)], axis=1).reshape(-1)
    b12 = np.stack([b12, b12])

    k = np.zeros((P, K_COLS), f4)
    k[:, K_ID:K_ID + P] = np.eye(P)
    q = np.arange(P)[:, None]
    for h, w in enumerate(WINDOWS):
        key = np.arange(KEYS[h])[None, :] - w
        ok = (key <= q) & (key > q - w)
        k[:, K_MN + KEY_AT[h]:K_MN + KEY_AT[h] + KEYS[h]] = np.where(ok, 0.0, LOW)
    off = np.concatenate([np.repeat(np.arange(OFFS), NARROW), np.arange(OFFS, 2 * OFFS)])[None, :]
    k[:, K_SM:K_SM + PAIRS] = np.where(off <= q, 0.0, LOW)
    part = (np.arange(P) // D) % 4
    k[:, K_NK] = -(part % 2)
    k[:, K_NQ] = -(part // 2)
    k[1, K_NB] = -1.0
    k[:, K_I8:K_I8 + EXPERTS] = np.arange(EXPERTS)
    k[:, K_EC:K_EC + EXPERTS] = np.arange(EXPERTS) * CAP
    k[:, K_TRI:K_TRI + P] = np.triu(np.ones((P, P)), 1)
    r = np.zeros((1, R_COLS), f4)
    r[0, R_B:R_B + BLOCKS] = np.arange(BLOCKS)
    r[0, R_E:R_E + 8] = np.arange(8)
    r[0, R_M:R_M + 32] = np.arange(32) * P
    r[0, R_TRI:R_TRI + 64] = np.tril(np.ones((8, 8))).reshape(-1)
    r[0, R_EB:R_EB + 8] = np.arange(8) * CAP
    places = np.arange(PLACES).reshape(TOP * SEQS * TILES, P).T.astype(np.int32)

    nc = bacc.Bacc("TRN2", target_bir_lowering=False, num_devices=1)
    arrays, args = {}, []
    for name, a in (("x", x), ("xt", x.T), ("w_att", w_att), ("b_att", b_att), ("w12", w12),
                    ("b12", b12), ("consts", k), ("rowc", r), ("places", places)):
        a = np.ascontiguousarray(a)
        arrays[name] = a
        args.append(nc.dram_tensor(name, a.shape, mybir.dt.from_np(a.dtype), kind="ExternalInput").ap())
    args.append(nc.dram_tensor("out", (SEQS * T, C), F32, kind="ExternalOutput").ap())
    program(nc, *args)
    got = run_bass_kernel_spmd(nc, [arrays], core_ids=[0])
    return got.results[0]["out"].reshape(SEQS, T, C)
```

```python
from contextlib import ExitStack

import concourse.bass as bass
from concourse import mybir

F32 = mybir.dt.float32
F32R = mybir.dt.float32r
BF16 = mybir.dt.bfloat16
I32 = mybir.dt.int32
U32 = mybir.dt.uint32
ALU = mybir.AluOpType
ACT = mybir.ActivationFunctionType
X_AXIS = mybir.AxisListType.X

P = 128
SEQS, T, C = 8, 512, 128
TILES = T // P
HEADS, D = 16, 8
SCALE = float(D) ** -0.5
EPS = 1e-5
LOW = -3.0e38

WIDE = 4
WINDOWS = [128, 64, 32, 16]
KEYS = [w + P for w in WINDOWS]
KEY_AT = [sum(KEYS[:h]) for h in range(WIDE)]
ALL_KEYS = sum(KEYS)
NARROW = HEADS - WIDE
OFFS = 4
NW = NARROW * D
PAIRS = OFFS * NARROW + OFFS
PK = PAIRS * D
EMPTY = 2 * OFFS

W_KREP, W_QREP, W_K, W_QG, W_PROJ, W_R = 0, 128, 256, 384, 496, 624
W_COLS = 632
B_KREP, B_QREP, B_KQ, B_PROJ = 0, 128, 256, 496
B_COLS = B_PROJ + 128
QG = NW + HEADS
KQ = C + QG

EXPERTS, F, TOP = 8, 512, 2
FC = F // P
BR = 2 * P
CAP = SEQS * T + BR
ZERO_ROW = EXPERTS * CAP
ROWS = ZERO_ROW + BR
MOST = SEQS * T // BR
ROW = C + 2
PLACES = TOP * SEQS * T
NOWHERE = 1 << 20
BLOCKS = PLACES // BR + EXPERTS

K_ID, K_MN = 0, 128
K_SM = K_MN + ALL_KEYS
K_NK, K_NQ, K_NB = K_SM + PAIRS, K_SM + PAIRS + 1, K_SM + PAIRS + 2
K_I8 = K_NB + 1
K_EC = K_I8 + EXPERTS
K_TRI = K_EC + EXPERTS
K_COLS = K_TRI + P
R_B, R_E, R_M = 0, BLOCKS, BLOCKS + 8
R_TRI, R_EB = R_M + MOST, R_M + MOST + 64
R_COLS = R_EB + 8


class Seq:

    def __init__(self, n, half, odd):
        self.n, self.half, self.u = n, half, odd


class Chain:

    def __init__(self, eng, sem, per, base=0):
        self.eng, self.sem, self.per, self.start, self.base, self.k = eng, sem, per, base, base, 0

    def round(self, n):
        assert self.k in (0, self.per), (self.k, self.per)
        self.base, self.k = n * self.per + self.start, 0

    def mark(self, ins):
        ins.then_inc(self.sem, 1)
        self.k += 1
        return ins

    def wait(self):
        self.eng.wait_ge(self.sem, self.base + self.k)

    def value(self):
        return self.base + self.k


def program(nc, x, xt, w_att, b_att, w12, b12, consts, rowc, places, out):
    ctx = ExitStack()
    with ctx:
        stage_a_only = ExitStack()
        place = [ctx]

        def sb(name, shape, dt=F32):
            return place[-1].enter_context(nc.sbuf_tensor(name, shape, dt))

        def sem(name):
            return ctx.enter_context(nc.semaphore(name))

        rows = nc.dram_tensor("expert_rows", (ROWS, ROW), F32, kind="Internal").ap()
        x1 = nc.dram_tensor("x1", (SEQS * T, C), F32, kind="Internal").ap()
        res = nc.dram_tensor("expert_results", (PLACES, C), F32, kind="Internal").ap()

        keys = [nc.dram_tensor(f"keys{u}", (EMPTY + T, NW), F32, kind="Internal").ap() for u in range(2)]
        keys4 = [nc.dram_tensor(f"keys4_{u}", (EMPTY + T, D), F32, kind="Internal").ap() for u in range(2)]

        psum = [ctx.enter_context(nc.psum_tensor(f"banks{i}", [P, 1024], F32)) for i in range(4)]
        bank = [psum[i // 2][:, 512 * (i % 2):512 * (i % 2) + 512] for i in range(8)]

        kc = sb("kc", [P, K_COLS])
        rc = sb("rc", [1, R_COLS])
        place_c = sb("place_c", [P, TOP * SEQS * TILES], I32)
        tri = sb("tri", [P, P], BF16)
        ones_b = sb("ones_b", [P, P], BF16)
        ones2 = sb("ones2", [2, T], F32R)
        wah = sb("wah", [P, W_COLS], F32R)
        wal = sb("wal", [P, W_COLS], F32R)
        bas = sb("bas", [2, B_COLS], F32R)
        rowb = [[sb(f"row{k}_{u}", [P, TILES, ROW]) for k in range(TOP)] for u in range(2)]
        slot = [sb(f"slot{u}", [P, TILES, TOP], I32) for u in range(2)]
        zeros = sb("zeros", [EMPTY, NW])
        fill = sb("fill", [P, BR // P, ROW])
        mtot = [sb(f"mtot{u}", [P, EXPERTS], BF16) for u in range(2)]
        stat = sb("stat", [P, TILES, 6])
        mv = sb("mv", [P, TILES, 2])
        va = sb("va", [P, TILES])
        nwt = [sb(f"nwt{i}", [P, TILES]) for i in range(10)]
        w12s = sb("w12s", [P, EXPERTS, 2, 2, F], F32R)
        b12c = sb("b12c", [P, EXPERTS * (FC + 1)])

        place.append(ctx.enter_context(stage_a_only))
        w12f = sb("w12f", [P, 2 * F])
        xtf = sb("xtf", [P, T])
        xres = [sb(f"xres{u}", [P, TILES, C]) for u in range(2)]
        xth = sb("xth", [P, T], F32R)
        xtl = sb("xtl", [P, T], F32R)
        hi_k = sb("hi_k", [P, T], F32R)
        hi_q = sb("hi_q", [P, T], F32R)
        kst = sb("kst", [P, T], F32R)
        qst = sb("qst", [P, T], F32R)
        qg = [sb(f"qg{u}", [P, TILES, QG]) for u in range(2)]
        key = [sb(f"key{u}", [P, TILES, C]) for u in range(2)]
        kt = [sb(f"kt{u}", [P, TILES, PK]) for u in range(2)]
        scored = [sb(f"scored{u}", [P, ALL_KEYS]) for u in range(2)]
        top = sb("top", [P, 2, WIDE])
        ntop = sb("ntop", [P, 2, WIDE])
        prob = [sb(f"prob{u}", [P, WIDE, 2 * P]) for u in range(2)]
        setup_only = ExitStack()
        place.append(ctx.enter_context(setup_only))
        wa = sb("wa", [P, W_COLS])
        ba = sb("ba", [2, B_COLS])
        bah = sb("bah", [2, B_COLS], F32R)
        setup_only.close()
        place.pop()
        pta = [sb(f"pta{u}", [P, WIDE, P]) for u in range(2)]
        ptb = [sb(f"ptb{u}", [P, WIDE, P]) for u in range(2)]
        sums = [sb(f"sums{u}", [P, TILES, HEADS]) for u in range(2)]
        prod = sb("prod", [P, TILES, PK])
        sc = sb("sc", [P, TILES, PAIRS])
        nmax = sb("nmax", [P, TILES, NARROW])
        nmax2 = sb("nmax2", [P, TILES])
        nmax3 = sb("nmax3", [P, TILES])
        scd = sb("scd", [P, TILES, PAIRS])
        ex = sb("ex", [P, TILES, PAIRS])
        gmax = sb("gmax", [P, TILES])
        gd = sb("gd", [P, TILES, HEADS])
        ge = sb("ge", [P, TILES, HEADS])
        gsum = sb("gsum", [P, TILES])
        xsum = sb("xsum", [P, TILES])
        xsum2 = sb("xsum2", [P, TILES])
        den = sb("den", [P, TILES, HEADS])
        rden = sb("rden", [P, TILES, HEADS])
        gn = sb("gn", [P, TILES, HEADS])
        raw = sb("raw", [P, TILES, NW])
        raw4 = sb("raw4", [P, TILES, D])
        raw5 = sb("raw5", [P, TILES, D])
        att = sb("att", [P, TILES, C])
        atth = sb("atth", [P, T], F32R)
        attl = sb("attl", [P, T], F32R)
        hid = sb("hid", [P, TILES, C])
        best = sb("best", [P, TILES, 8])
        logit = sb("logit", [P, TILES, EXPERTS])
        ibest = sb("ibest", [P, TILES, 8], U32)
        ibf = sb("ibf", [P, TILES, 8])
        diff = sb("diff", [P, TILES])
        edif = sb("edif", [P, TILES])
        edif1 = sb("edif1", [P, TILES])
        wtop = sb("wtop", [P, TILES])
        wtop2 = sb("wtop2", [P, TILES])
        oh = sb("oh", [P, TILES, TOP, EXPERTS])
        mem = sb("mem", [P, TILES, EXPERTS], BF16)
        memf = sb("memf", [P, EXPERTS])
        rank = sb("rank", [P, TILES, EXPERTS])
        slotf = sb("slotf", [P, TILES, TOP])
        pick = sb("pick", [P, TILES, TOP, EXPERTS])

        stage_a_only.close()
        place.pop()

        cnt = sb("cnt", [1, EXPERTS])
        cmp32 = sb("cmp32", [1, EXPERTS, MOST])
        nblk = sb("nblk", [1, EXPERTS])
        cum3 = sb("cum3", [1, EXPERTS, EXPERTS])
        cend = sb("cend", [1, EXPERTS])
        shift = sb("shift", [1, EXPERTS])
        shift2 = sb("shift2", [1, EXPERTS])
        bge = sb("bge", [1, BLOCKS, EXPERTS])
        bexp = sb("bexp", [1, BLOCKS])
        boh = sb("boh", [1, BLOCKS, EXPERTS])
        boh2 = sb("boh2", [1, BLOCKS, EXPERTS])
        bsh = sb("bsh", [1, BLOCKS])
        bun = sb("bun", [1, BLOCKS])
        bun2 = sb("bun2", [1, BLOCKS])
        bun3 = sb("bun3", [1, BLOCKS])
        brow = sb("brow", [1, BLOCKS])
        brow2 = sb("brow2", [1, BLOCKS])
        t_row = sb("t_row", [1, BLOCKS], I32)
        t_exp = sb("t_exp", [1, BLOCKS], I32)
        t_fill = sb("t_fill", [1, EXPERTS], I32)

        RING = 4
        xb = [sb(f"xb{i}", [P, BR // P, ROW]) for i in range(RING)]
        wd = [sb(f"wd{i}", [P, BR // P, 2]) for i in range(RING)]
        w1s = [sb(f"w1s{i}", [P, 2, F], F32R) for i in range(2)]
        w2s = [sb(f"w2s{i}", [P, 2, F], F32R) for i in range(2)]
        xbh = [sb(f"xbh{i}", [P, BR], F32R) for i in range(2)]
        xbl = [sb(f"xbl{i}", [P, BR], F32R) for i in range(2)]
        g = [sb(f"g{i}", [P, FC * BR]) for i in range(2)]
        gh = [sb(f"gh{i}", [P, FC * BR], F32R) for i in range(2)]
        gl = [sb(f"gl{i}", [P, FC * BR], F32R) for i in range(2)]
        yt = [sb(f"yt{i}", [P, BR]) for i in range(2)]
        yb = [sb(f"yb{i}", [P, BR // P, C]) for i in range(RING)]
        ya = [[sb(f"ya{k}_{u}", [P, TILES, C]) for k in range(TOP)] for u in range(2)]
        x1c = [sb(f"x1c{u}", [P, TILES, C]) for u in range(2)]
        ysum = sb("ysum", [P, TILES, C])
        h2 = [sb(f"h2_{u}", [P, TILES, C]) for u in range(2)]
        o2 = [sb(f"o2_{u}", [P, TILES, C]) for u in range(2)]

        names = """const_in weights_in biases_in const_ready weights_ready acredit
            x_hi x_lo kproj qproj kq_done kq_copied keys_out khi qhi kst_ready qst_ready scores score_free ntop_ready p_ready turned pta_out ptb_out pv pv_free
            prod_ready sc_ready ex_ready pk_ready att_ready
            att_turned att_hi att_lo projected hid_ready rows_x x1_kept x1_turned x1_hi x1_lo
            logits_ready tail_free diff_ready edif_ready mem_ready ranks slots_ready
            dve_a dve_t act_a pool_a w_hi w_lo totals plan_ready fill_ready rows_filled b12_hi
            b12_ready
            x_turned xb_hi xb_lo wd_ready h_ready w1_ready w2_ready g_ready g_hi g_lo y_done y_copied y_turned
            y_ready zeros_ready dve_c c_ready rows_free setup_dve ones_ready w_used""".split()
        S = {n: sem(n) for n in names}
        xt_in = sem("xt_in")
        keys_in = [sem(f"keys_in{u}") for u in range(2)]
        xres_in = [sem(f"xres_in{u}") for u in range(2)]
        expert_in = sem("expert_in")
        x1_out = [sem(f"x1_out{u}") for u in range(2)]
        scattered = [sem(f"scattered{u}") for u in range(2)]
        block_in = [sem(f"block_in{i}") for i in range(RING)]
        y_out = [sem(f"y_out{i}") for i in range(RING)]
        c_in = [sem(f"c_in{u}") for u in range(2)]
        c_out = [sem(f"c_out{u}") for u in range(2)]

        ident = kc[:, K_ID:K_ID + P]
        b_k, b_q, b_c, b_pv, b_tail = bank[4], bank[5], bank[6], bank[7], bank[3]
        score_at = [bank[0][:, 0:KEYS[0]], bank[1][:, 0:KEYS[1]], bank[2][:, 0:KEYS[2]],
                    bank[2][:, 256:256 + KEYS[3]]]

        def wait_alone(eng, semaphore, value):
            if not isinstance(value, int):
                eng.reg_mov(carrier[eng.engine], value)
                eng.wait_ge(S["const_in"], 48)
                value = carrier[eng.engine]
            eng.wait_ge(semaphore, value)

        carrier = {}

        def prepare_carrier(eng):
            carrier[eng.engine] = eng.alloc_register("carrier")
            eng.reg_mov(carrier[eng.engine], 0)

        def stage_a(eng, step):
            step(Seq(0, 0, 0), None, Seq(1, 0, 1))
            with eng.Fori(0, (SEQS - 2) // 2) as j:
                a, b, c, d = Seq(2 * j, j, 0), Seq(2 * j + 1, j, 1), Seq(2 * j + 2, j + 1, 0), Seq(2 * j + 3, j + 1, 1)
                step(b, a, c)
                step(c, b, d)
            last = Seq(SEQS - 1, SEQS // 2 - 1, 1)
            step(last, Seq(SEQS - 2, SEQS // 2 - 1, 0), None)
            step(None, last, None)

        LAST = 3

        def b_loop(eng, b_step):
            for b in range(RING):
                b_step(b, 0, b)
            with eng.Fori(1, BLOCKS // RING - 1) as r:
                for i in range(RING):
                    b_step(r * RING + i, r, i)
            for b in range(BLOCKS - RING, BLOCKS + LAST):
                b_step(b, b // RING, b % RING)

        block = ctx.enter_context(nc.Block())

        @block.sync
        def _(sp):
            sp.dma_start(xtf[:], xt[:, 0:T]).then_inc(xt_in, 16)
            sp.dma_start(wa[:], w_att).then_inc(S["weights_in"], 16)
            sp.dma_start(ba[:], b_att).then_inc(S["weights_in"], 16)
            sp.dma_start(kc[:], consts).then_inc(S["const_in"], 16)
            sp.dma_start(rc[:], rowc).then_inc(S["const_in"], 16)
            sp.dma_start(place_c[:], places).then_inc(S["const_in"], 16)
            sp.dma_start(xres[0][:], x[0:T, :].rearrange("(i p) c -> p i c", p=P)).then_inc(xres_in[0], 16)
            sp.dma_start(b12c[:], b12).then_inc(S["biases_in"], 16)
            sp.wait_ge(S["zeros_ready"], 1)
            for u in range(2):
                sp.dma_start(keys[u][0:EMPTY, :], zeros[:]).then_inc(S["keys_out"], 16)
                sp.dma_start(keys4[u][0:EMPTY, :], zeros[:, 0:D]).then_inc(S["keys_out"], 16)

            def windows(n):
                sp.wait_ge(S["kq_copied"], 2 * n.n + 3)
                for to, cols in ((keys, NW), (keys4, D)):
                    sp.dma_start(to[n.u][EMPTY:EMPTY + T, :].rearrange("(i p) c -> p i c", p=P),
                                 key[n.u][:, :, WIDE * D:WIDE * D + cols]).then_inc(S["keys_out"], 16)
                sp.wait_ge(S["keys_out"], 32 * n.n + 96)
                w, w4 = OFFS * NW, OFFS * D
                sp.dma_start(kt[n.u][:, :, 0:w],
                             bass.AP(keys[n.u].tensor, (EMPTY - OFFS + 1) * NW, [[NW, P], [NW * P, TILES], [1, w]])).then_inc(keys_in[n.u], 16)
                sp.dma_start(kt[n.u][:, :, w:PK],
                             bass.AP(keys4[n.u].tensor, (EMPTY - 2 * OFFS + 1) * D, [[D, P], [D * P, TILES], [1, w4]])).then_inc(keys_in[n.u], 16)

            windows(Seq(0, 0, 0))

            def step(s, t, n):
                if n:
                    sp.wait_ge(S["x_lo"], s.n + 1)
                    sp.dma_start(xtf[:], xt[:, bass.ds(n.n * T, T)]).then_inc(xt_in, 16)
                if s:
                    if t:
                        sp.wait_ge(S["w_lo"], s.n)
                    sp.dma_start(w12f[:], w12[:, bass.ds(s.n * 2 * F, 2 * F)]).then_inc(expert_in, 16)
                if n:
                    if t:
                        sp.wait_ge(S["hid_ready"], t.n + 1)
                    sp.dma_start(xres[n.u][:], x[bass.ds(n.n * T, T), :].rearrange("(i p) c -> p i c", p=P)).then_inc(xres_in[n.u], 16)
                if t:
                    sp.wait_ge(S["rows_x"], t.n + 1)
                    sp.dma_start(x1[bass.ds(t.n * T, T), :].rearrange("(i p) c -> p i c", p=P),
                                 rowb[t.u][0][:, :, 0:C]).then_inc(x1_out[t.u], 16)
                if n:
                    windows(n)

            stage_a(sp, step)

            sp.wait_ge(S["fill_ready"], 1)
            sp.dma_start(rows[ZERO_ROW:ROWS, :].rearrange("(j p) c -> p j c", p=P), fill[:]).then_inc(S["rows_filled"], 16)
            sp.wait_ge(S["plan_ready"], 1)
            for e in range(EXPERTS):
                at = sp.value_load(t_fill[0:1, e:e + 1], min_val=0, max_val=ZERO_ROW - BR)
                sp.dma_start(rows[bass.ds(at, BR), :].rearrange("(j p) c -> p j c", p=P), fill[:]).then_inc(S["rows_filled"], 16)
            sp.wait_ge(S["rows_filled"], 16 * (EXPERTS + 1))
            for u in range(2):
                sp.wait_ge(scattered[u], 16 * TOP * TILES * SEQS // 2)

            def load_block(b, i, first):
                if not first:
                    sp.wait_ge(S["x_turned"], b - RING + 1)
                    sp.wait_ge(S["wd_ready"], b - RING + 1)
                at = sp.value_load(t_row[0:1, bass.ds(b, 1)], min_val=0, max_val=ZERO_ROW)
                sp.dma_start(xb[i][:], rows[bass.ds(at, BR), :].rearrange("(j p) c -> p j c", p=P)).then_inc(block_in[i], 16)

            for b in range(RING):
                load_block(b, b, True)
            with sp.Fori(1, BLOCKS // RING) as r:
                for i in range(RING):
                    load_block(r * RING + i, i, False)

            for i in range(RING):
                sp.wait_ge(y_out[i], 16 * (BR // P) * (BLOCKS // RING))

            for u in range(2):
                sp.wait_ge(x1_out[u], 16 * SEQS // 2)

            def load_c(n, u, half, first):
                if not first:
                    sp.wait_ge(S["c_ready"], n - 1)
                sp.dma_start(x1c[u][:], x1[bass.ds(n * T, T), :].rearrange("(i p) c -> p i c", p=P)).then_inc(c_in[u], 16)
                for k in range(TOP):
                    sp.dma_start(ya[u][k][:], res[bass.ds(n * T + k * SEQS * T, T), :].rearrange("(i p) c -> p i c", p=P)).then_inc(c_in[u], 16)

            def store_c(n, u, half):
                sp.wait_ge(S["c_ready"], n + 1)
                sp.dma_start(out[bass.ds(n * T, T), :].rearrange("(i p) c -> p i c", p=P), o2[u][:]).then_inc(c_out[u], 16)

            load_c(0, 0, 0, True)
            load_c(1, 1, 0, True)
            with sp.Fori(0, (SEQS - 2) // 2) as j:
                store_c(2 * j, 0, j)
                load_c(2 * j + 2, 0, j + 1, False)
                store_c(2 * j + 1, 1, j)
                load_c(2 * j + 3, 1, j + 1, False)
            store_c(SEQS - 2, 0, 3)
            store_c(SEQS - 1, 1, 3)
            for u in range(2):
                sp.wait_ge(c_out[u], 16 * SEQS // 2)

        @block.tensor
        def _(pe):
            def three(out_ap, lh, ll, rh, rl, last_start=False, stop=True):
                pe.matmul(out_ap, lh, rh, start=last_start, stop=False, skip_group_check=True)
                pe.matmul(out_ap, lh, rl, start=False, stop=False, skip_group_check=True)
                return pe.matmul(out_ap, ll, rh, start=False, stop=stop, skip_group_check=True)

            def bias(out_ap, lhs, rhs):
                return pe.matmul(out_ap, lhs, rhs, start=True, stop=False, skip_group_check=True)

            def scores(s, i, h):
                pe.wait_ge(S["score_free"], 4 * (4 * s.n + i) + (h + 1 if h < 2 else WIDE))
                r = slice(32 * h, 32 * h + 32)
                at = P * i
                w = WINDOWS[h] if i else 0
                return pe.matmul(score_at[h][:, WINDOWS[h] - w:], qst[r, P * i:P * i + P], kst[r, at - w:at + P],
                                 start=True, stop=True, skip_group_check=True)

            def tokens(n, a):
                pe.wait_ge(S["kq_copied"], 2 * n.n + a + 1)
                for i in range(2):
                    t = slice(P * (2 * a + i), P * (2 * a + i) + P)
                    o = b_c[:, KQ * i:KQ * i + KQ]
                    bias(o, ones2[:, 0:P], bas[:, B_KQ:B_KQ + KQ])
                    mm = three(o, xth[:, t], xtl[:, t], wah[:, W_K:W_K + KQ], wal[:, W_K:W_K + KQ])
                mm.then_inc(S["kq_done"], 1)

            def project(n, b, wc, bc, done):
                bias(b[:], bas[:, bc:bc + P], ones2[:])
                three(b[:], wah[:, wc:wc + P], wal[:, wc:wc + P], xth[:], xtl[:]).then_inc(done, 1)

            def project_keys(n):
                pe.wait_ge(S["pta_out"], 4 * n.n + 1)
                project(n, b_k, W_KREP, B_KREP, S["kproj"])

            def project_queries(n):
                pe.wait_ge(S["ptb_out"], 3 * n.n + 1)
                project(n, b_q, W_QREP, B_QREP, S["qproj"])

            def turn(s, i):
                pe.wait_ge(S["p_ready"], 4 * s.n + i + 1)
                if i >= 1:
                    pe.wait_ge(S["pta_out"], 4 * s.n + i + 1)
                if i >= 2:
                    pe.wait_ge(S["ptb_out"], 3 * s.n + i)
                pr = prob[i % 2]
                for h in range(WIDE):
                    mm = pe.transpose(b_k[:, P * h:P * h + P], pr[:, h, P:2 * P], ident)
                if i >= 1:
                    for h in range(WIDE):
                        mm = pe.transpose(b_q[:, P * h:P * h + P], pr[:, h, 0:P], ident)
                mm.then_inc(S["turned"], 1)

            def pv(s, i):
                pe.wait_ge(S["pta_out"], 4 * s.n + i + 2)
                if i == 0:
                    pe.wait_ge(S["pv_free"], s.n + 1)
                    pe.wait_ge(S["kq_copied"], 2 * s.n + 3)
                if i >= 1:
                    pe.wait_ge(S["ptb_out"], 3 * s.n + i + 1)
                for h in range(WIDE):
                    o = b_pv[:, WIDE * D * i + D * h:WIDE * D * i + D * h + D]
                    mm = pe.matmul(o, pta[i % 2][:, h, :], key[s.u][:, i, D * h:D * h + D],
                                   start=True, stop=i == 0, skip_group_check=True)
                    if i >= 1:
                        mm = pe.matmul(o, ptb[i % 2][:, h, :], key[s.u][:, i - 1, D * h:D * h + D],
                                       start=False, stop=True, skip_group_check=True)
                mm.then_inc(S["pv"], 1)

            def end0(s):
                pe.wait_ge(S["att_ready"], s.n + 1)
                pe.wait_ge(S["tail_free"], s.n + 1)
                for i in range(TILES):
                    mm = pe.transpose(b_tail[:, P * i:P * i + P], att[:, i, :], ident)
                mm.then_inc(S["att_turned"], 1)

            def end1(s):
                pe.wait_ge(S["att_lo"], s.n + 1)
                for i in range(TILES):
                    t = slice(P * i, P * i + P)
                    bias(b_tail[:, t], ones2[:, 0:P], bas[:, B_PROJ:B_PROJ + C])
                    mm = three(b_tail[:, t], atth[:, t], attl[:, t], wah[:, W_PROJ:W_PROJ + C],
                               wal[:, W_PROJ:W_PROJ + C])
                mm.then_inc(S["projected"], 1)

            def end2(s):
                pe.wait_ge(S["rows_x"], s.n + 1)
                for i in range(TILES):
                    mm = pe.transpose(b_tail[:, P * i:P * i + P], rowb[s.u][0][:, i, 0:C], ident)
                mm.then_inc(S["x1_turned"], 1)

            def end3(s):
                pe.wait_ge(S["x1_lo"], s.n + 1)
                for i in range(TILES):
                    t = slice(P * i, P * i + P)
                    mm = three(b_tail[:, EXPERTS * i:EXPERTS * i + EXPERTS], atth[:, t], attl[:, t],
                               wah[:, W_R:W_R + EXPERTS], wal[:, W_R:W_R + EXPERTS], last_start=True)
                mm.then_inc(S["logits_ready"], 1)

            def end4(s):
                pe.wait_ge(S["mem_ready"], s.n + 1)
                for i in range(TILES):
                    o = b_tail[:, 64 + EXPERTS * i:64 + EXPERTS * i + EXPERTS]
                    pe.matmul(o, tri[:], mem[:, i, :], start=True, stop=False, skip_group_check=True)
                    for i2 in range(i):
                        pe.matmul(o, ones_b[:], mem[:, i2, :], start=False, stop=False, skip_group_check=True)
                    mm = pe.matmul(o, ones_b[:], mtot[s.u][:], start=False, stop=True, skip_group_check=True)
                mm.then_inc(S["ranks"], 1)

            def step(s, t, n):
                for i in range(TILES):
                    if s:
                        if i == 0:
                            pe.wait_ge(S["kst_ready"], s.n + 1)
                            pe.wait_ge(S["qst_ready"], s.n + 1)
                        for h in range(WIDE - 1):
                            scores(s, i, h).then_inc(S["scores"], 1)
                        if i >= 2:
                            pv(s, i - 2)
                        if i >= 1:
                            turn(s, i - 1)
                        pe.wait_ge(S["scores"], 4 * (4 * s.n + i) + 3)
                        scores(s, i, WIDE - 1).then_inc(S["scores"], 1)
                    if t:
                        (end0, end1, end2, end3)[i](t)
                    if n and i >= 2:
                        if i == 2:
                            pe.wait_ge(S["x_lo"], n.n + 1)
                        tokens(n, i - 2)
                if s:
                    turn(s, TILES - 1)
                    pv(s, TILES - 2)
                if n:
                    project_keys(n)
                    project_queries(n)
                if t:
                    end4(t)
                if s:
                    pv(s, TILES - 1)

            pe.wait_ge(S["weights_ready"], 1)
            pe.wait_ge(S["x_lo"], 1)
            first = Seq(0, 0, 0)
            tokens(first, 0)
            project_keys(first)
            tokens(first, 1)
            project_queries(first)
            stage_a(pe, step)

            pe.wait_ge(S["tail_free"], SEQS + 1)
            pe.matmul(b_tail[:, 0:EXPERTS], ones_b[:], mtot[0][:], start=True, stop=True).then_inc(S["totals"], 1)

            ph, px, py, pyt = psum[0:2], bank[4], bank[5:7], bank[7]
            pe.sem_inc(S["y_done"], 2)
            pe.sem_inc(S["y_turned"], 2)

            def turn_x(b, q, i):
                pe.wait_ge(block_in[i], 16 * (q + 1))
                if not (isinstance(b, int) and b == 0):
                    pe.wait_ge(S["xb_lo"], b)
                for j in range(BR // P):
                    mm = pe.transpose(px[:, P * j:P * j + P], xb[i][:, j, 0:C], ident)
                mm.then_inc(S["x_turned"], 1)

            def first_product(b, i):
                pe.wait_ge(S["w1_ready"], b + 1)
                pe.wait_ge(S["xb_lo"], b + 1)
                pe.wait_ge(S["g_ready"], b + 1)
                for c in range(FC):
                    w = w1s[i % 2][:, :, P * c:P * c + P]
                    mm = three(ph[i % 2][:, BR * c:BR * c + BR], w[:, 0], w[:, 1],
                               xbh[i % 2][:], xbl[i % 2][:], last_start=True)
                mm.then_inc(S["h_ready"], 1)

            def second_product(b, i):
                pe.wait_ge(S["w2_ready"], b + 1)
                pe.wait_ge(S["g_lo"], b + 3)
                pe.wait_ge(S["y_copied"], b + 1)
                for c in range(FC):
                    w, r = w2s[i % 2][:, :, C * c:C * c + C], slice(BR * c, BR * c + BR)
                    mm = three(py[i % 2][:, 0:BR], w[:, 0], w[:, 1], gh[i % 2][:, r], gl[i % 2][:, r],
                               last_start=c == 0, stop=c == FC - 1)
                mm.then_inc(S["y_done"], 1)

            def turn_y(b, i):
                pe.wait_ge(S["y_copied"], b + 3)
                pe.wait_ge(S["y_ready"], b + 1)
                for j in range(BR // P):
                    mm = pe.transpose(pyt[:, C * j:C * j + C], yt[i % 2][:, P * j:P * j + P], ident)
                mm.then_inc(S["y_turned"], 1)

            def b_step(b, q, i):
                static = isinstance(b, int)
                if not static or b + 1 < BLOCKS:
                    turn_x(b + 1, q + (i + 1) // RING, (i + 1) % RING)
                if not static or b < BLOCKS:
                    first_product(b, i)
                if not static or b >= 3:
                    turn_y(b - 3, i - 3)
                if not static or 2 <= b < BLOCKS + 2:
                    second_product(b - 2, i - 2)

            pe.wait_ge(S["w_lo"], SEQS)
            pe.wait_ge(S["plan_ready"], 1)
            turn_x(0, 0, 0)
            b_loop(pe, b_step)

        @block.scalar
        def _(act):
            act.sem_inc(S["kq_copied"], 1)
            act.sem_inc(S["pta_out"], 1)
            act.sem_inc(S["ptb_out"], 1)
            act.sem_inc(S["g_ready"], 2)
            act.sem_inc(S["y_copied"], 2)
            act.wait_ge(S["weights_in"], 32)
            act.copy(wah[:], wa[:]).then_inc(S["w_hi"], 1)
            act.copy(bah[:], ba[:]).then_inc(S["w_hi"], 1)

            def split_x(n):
                act.wait_ge(xt_in, 16 * (n.n + 1))
                if not (isinstance(n.n, int) and n.n == 0):
                    act.wait_ge(S["qproj"], n.n)
                act.copy(xth[:], xtf[:]).then_inc(S["x_hi"], 1)

            def copy_tokens(n, a):
                act.wait_ge(S["kq_done"], 2 * n.n + a + 1)
                both = b_c[:, 0:2 * KQ].rearrange("p (i c) -> p i c", i=2)
                act.copy(key[n.u][:, 2 * a:2 * a + 2, :], both[:, :, 0:C])
                act.copy(qg[n.u][:, 2 * a:2 * a + 2, :], both[:, :, C:KQ]).then_inc(S["kq_copied"], 1)

            def keys_hi(n):
                act.wait_ge(S["kproj"], n.n + 1)
                act.copy(hi_k[:], b_k[:]).then_inc(S["khi"], 1)

            def queries_hi(n):
                act.wait_ge(S["qproj"], n.n + 1)
                act.copy(hi_q[:], b_q[:]).then_inc(S["qhi"], 1)

            split_x(Seq(0, 0, 0))

            def wide_exp(s, i):
                act.wait_ge(S["ntop_ready"], 4 * s.n + i + 1)
                for h in range(WIDE):
                    w = WINDOWS[h] if i else 0
                    a = act.activation(prob[i % 2][:, h, P - w:2 * P],
                                       scored[i % 2][:, KEY_AT[h] + WINDOWS[h] - w:KEY_AT[h] + KEYS[h]], ACT.Exp,
                                       bias=ntop[:, i % 2, h:h + 1], scale=SCALE,
                                       accum_out=sums[s.u][:, i, h:h + 1])
                a.then_inc(S["p_ready"], 1)

            def copy_turned(s, i):
                act.wait_ge(S["turned"], 4 * s.n + i + 1)
                act.copy(pta[i % 2][:].rearrange("p h q -> p (h q)"), b_k[:]).then_inc(S["pta_out"], 1)
                if i >= 1:
                    act.copy(ptb[i % 2][:].rearrange("p h q -> p (h q)"), b_q[:]).then_inc(S["ptb_out"], 1)

            def end(t, i):
                if i == 0:
                    act.wait_ge(S["att_turned"], t.n + 1)
                    act.copy(atth[:], b_tail[:]).then_inc(S["att_hi"], 1)
                if i == 2:
                    act.wait_ge(S["x1_turned"], t.n + 1)
                    act.copy(atth[:], b_tail[:]).then_inc(S["x1_hi"], 1)
                    if_free(t)
                    act.copy(rowb[t.u][1][:, :, 0:C], rowb[t.u][0][:, :, 0:C]).then_inc(S["x1_kept"], 1)
                if i == 3:
                    act.wait_ge(S["diff_ready"], t.n + 1)
                    act.activation(edif[:], diff[:], ACT.Exp).then_inc(S["edif_ready"], 1)

            def if_free(t):
                act.wait_ge(S["rows_free"], t.n + 1)

            def step(s, t, n):
                for i in range(TILES):
                    if s:
                        wide_exp(s, i)
                        if i >= 1:
                            copy_turned(s, i - 1)
                    if t and i < 3:
                        end(t, i)
                    if n:
                        if i == 0:
                            split_x(n)
                        if i >= 2:
                            copy_tokens(n, i - 2)
                if s:
                    copy_turned(s, TILES - 1)
                    act.wait_ge(S["sc_ready"], s.n + 1)
                    act.activation(ex[:].rearrange("p i c -> p (i c)"), scd[:].rearrange("p i c -> p (i c)"), ACT.Exp, scale=SCALE)
                    act.activation(ge[:].rearrange("p i c -> p (i c)"), gd[:].rearrange("p i c -> p (i c)"), ACT.Exp).then_inc(S["ex_ready"], 1)
                if n:
                    keys_hi(n)
                    queries_hi(n)
                if t:
                    end(t, 3)
                if s:
                    act.wait_ge(expert_in, 16 * (s.n + 1))
                    act.copy(w12s[:, bass.ds(s.n, 1), :, 0, :], w12f[:].rearrange("p (a k f) -> p a k f", a=1, k=2)).then_inc(S["w_hi"], 1)

            first = Seq(0, 0, 0)
            copy_tokens(first, 0)
            keys_hi(first)
            copy_tokens(first, 1)
            queries_hi(first)
            stage_a(act, step)

            ph, px, py = psum[0:2], bank[4], bank[5:7]
            act.wait_ge(S["biases_in"], 16)

            def expert_of(b):
                return act.value_load(t_exp[0:1, bass.ds(b, 1)], min_val=0, max_val=EXPERTS - 1)

            def x_hi(b, i):
                act.wait_ge(S["x_turned"], b + 1)
                act.copy(xbh[i % 2][:], px[:, 0:BR]).then_inc(S["xb_hi"], 1)

            def gelu(b, i):
                e = expert_of(b)
                act.wait_ge(S["h_ready"], b + 1)
                act.wait_ge(S["g_lo"], b + 1)
                for c in range(FC):
                    r = slice(BR * c, BR * c + BR)
                    a = act.activation(g[i % 2][:, r], ph[i % 2][:, r], ACT.Gelu,
                                       bias=b12c[:, bass.ds(e * (FC + 1) + c, 1)])
                a.then_inc(S["g_ready"], 1)

            def g_hi(b, i):
                act.wait_ge(S["g_ready"], b + 3)
                act.wait_ge(S["y_done"], b + 1)
                act.copy(gh[i % 2][:], g[i % 2][:]).then_inc(S["g_hi"], 1)

            def y_copy(b, i):
                e = expert_of(b)
                act.wait_ge(S["y_done"], b + 3)
                act.wait_ge(S["y_turned"], b + 1)
                act.activation(yt[i % 2][:], py[i % 2][:, 0:BR], ACT.Identity,
                               bias=b12c[:, bass.ds(e * (FC + 1) + FC, 1)]).then_inc(S["y_copied"], 1)

            def b_step(b, q, i):
                static = isinstance(b, int)
                if not static or b >= 3:
                    y_copy(b - 3, i - 3)
                if not static or b + 1 < BLOCKS:
                    x_hi(b + 1, i + 1)
                if not static or b < BLOCKS:
                    gelu(b, i)
                    g_hi(b, i)

            x_hi(0, 0)
            b_loop(act, b_step)

        @block.gpsimd
        def _(pool):
            prepare_carrier(pool)
            pool.memset(zeros[:], 0.0).then_inc(S["zeros_ready"], 1)
            pool.memset(fill[:], 0.0).then_inc(S["pool_a"], 1)
            pool.wait_ge(S["pool_a"], 1)
            pool.memset(fill[:, :, C + 1:C + 2].bitcast(I32), NOWHERE).then_inc(S["fill_ready"], 1)
            pool.sem_inc(S["rows_free"], 2)

            def step(s, t, n):
                if s:
                    pool.wait_ge(keys_in[s.u], 32 * (s.half + 1))
                    for i in range(TILES):
                        k, q = kt[s.u][:, i, :], qg[s.u][:, i, 0:NW]
                        pool.tensor_tensor(prod[:, i, 0:OFFS * NW].rearrange("p (o c) -> p o c", o=OFFS),
                                           k[:, 0:OFFS * NW].rearrange("p (o c) -> p o c", o=OFFS),
                                           q.unsqueeze(1).broadcast_to([P, OFFS, NW]), ALU.mult)
                        pool.tensor_tensor(prod[:, i, OFFS * NW:PK].rearrange("p (o c) -> p o c", o=OFFS),
                                           k[:, OFFS * NW:PK].rearrange("p (o c) -> p o c", o=OFFS),
                                           q[:, 0:D].unsqueeze(1).broadcast_to([P, OFFS, D]), ALU.mult).then_inc(S["prod_ready"], 1)
                    pool.wait_ge(S["ex_ready"], s.n + 1)
                    for i in range(TILES):
                        k = kt[s.u][:, i, :].rearrange("p (c d) -> p c d", d=D)
                        pool.tensor_tensor(k, k, ex[:, i, :].unsqueeze(2).broadcast_to([P, PAIRS, D]),
                                           ALU.mult).then_inc(S["pk_ready"], 1)
                if t:
                    wait_alone(pool, S["slots_ready"], t.n + 1)
                    for i in range(TILES):
                        for k in range(TOP):
                            pool.indirect_dma_start(rows, bass.IndirectOffsetOnAxis(ap=slot[t.u][:, i, k:k + 1], axis=0),
                                                    rowb[t.u][k][:, i, :], None, bounds_check=ZERO_ROW - 1,
                                                    oob_is_err=False).then_inc(scattered[t.u], 16)

            def step_and_free(s, t, n):
                if t and not (isinstance(t.n, int) and t.n == 0):
                    half = t.half if t.u else t.half - 1
                    pool.wait_ge(scattered[1 - t.u], 16 * TOP * TILES * (half + 1))
                    pool.wait_ge(x1_out[1 - t.u], 16 * (half + 1))
                    pool.sem_inc(S["rows_free"], 1)
                step(s, t, n)

            stage_a(pool, step_and_free)

            def scatter(b, q, i):
                wait_alone(pool, S["y_ready"], b + 2)
                for j in range(BR // P):
                    pool.indirect_dma_start(res, bass.IndirectOffsetOnAxis(ap=wd[i][:, j, 1:2].bitcast(I32), axis=0),
                                            yb[i][:, j, :], None, bounds_check=PLACES - 1,
                                            oob_is_err=False).then_inc(y_out[i], 16)

            with pool.Fori(0, BLOCKS // RING) as r:
                for i in range(RING):
                    scatter(r * RING + i, r, i)

        @block.vector
        def _(dve):
            prepare_carrier(dve)
            dve.sem_inc(S["score_free"], WIDE)
            dve.sem_inc(S["pv_free"], 1)
            dve.sem_inc(S["tail_free"], 1)
            dve.sem_inc(S["g_lo"], 2)
            dve.sem_inc(S["y_ready"], 1)
            for u in range(2):
                dve.memset(prob[u][:], 0.0)
            dve.memset(mtot[0][:], 0.0)
            dve.memset(ones_b[:], 1.0)
            dve.memset(ones2[:].bitcast(F32), 1.0)
            dve.wait_ge(S["const_in"], 48)
            dve.tensor_copy(tri[:], kc[:, K_TRI:K_TRI + P])
            dve.wait_ge(S["w_hi"], 2)
            dve.tensor_tensor(wal[:], wa[:], wah[:].bitcast(F32), ALU.subtract)
            dve.scalar_tensor_tensor(bas[:], bah[:].bitcast(F32), kc[0:2, K_NB:K_NB + 1], ba[:],
                                     ALU.mult, ALU.add).then_inc(S["weights_ready"], 1)

            def x_lo(n):
                dve.wait_ge(S["x_hi"], n.n + 1)
                dve.tensor_tensor(xtl[:], xtf[:], xth[:].bitcast(F32), ALU.subtract).then_inc(S["x_lo"], 1)

            x_lo(Seq(0, 0, 0))
            own = Chain(dve, S["dve_a"], 22)
            tail = Chain(dve, S["dve_t"], 27)

            def rstd(chain, v):
                y = nwt[0]
                chain.mark(dve.tensor_scalar(y[:].bitcast(I32), v[:].bitcast(I32), -0.5, 1597463007.0, ALU.mult, ALU.add))
                for i in range(3):
                    a, b, y2 = nwt[3 * i + 1], nwt[3 * i + 2], nwt[3 * i + 3]
                    chain.wait()
                    chain.mark(dve.tensor_tensor(a[:], y[:], y[:], ALU.mult))
                    chain.wait()
                    chain.mark(dve.scalar_tensor_tensor(b[:], a[:], -0.5, v[:], ALU.mult, ALU.mult))
                    chain.wait()
                    chain.mark(dve.scalar_tensor_tensor(y2[:], b[:], 1.5, y[:], ALU.add, ALU.mult))
                    y = y2
                chain.wait()
                return y

            def statistics(chain, h):
                for i in range(TILES):
                    ins = dve.bn_stats(stat[:, i, :], h[:, i, :])
                chain.mark(ins)
                wait_alone(dve, chain.sem, chain.value())
                for i in range(TILES):
                    ins = dve.bn_aggr(mv[:, i, :], stat[:, i, :])
                chain.mark(ins)
                chain.wait()
                chain.mark(dve.tensor_scalar(va[:], mv[:, :, 1], EPS, None, ALU.add))
                chain.wait()
                return rstd(chain, va)

            def window(s, i):
                for h in range(WIDE):
                    wait_alone(dve, S["scores"], 4 * (4 * s.n + i) + (h + 1 if h < 2 else WIDE))
                    if i >= 2 and h == 0:
                        dve.wait_ge(S["p_ready"], 4 * s.n + i - 1)
                    a = WINDOWS[h] if i == 0 else 0
                    dve.tensor_tensor_reduce(
                        scored[i % 2][:, KEY_AT[h] + a:KEY_AT[h] + KEYS[h]], score_at[h][:, a:],
                        kc[:, K_MN + KEY_AT[h] + a:K_MN + KEY_AT[h] + KEYS[h]], 1.0, LOW, ALU.add, ALU.max,
                        top[:, i % 2, h:h + 1]).then_inc(S["score_free"], 1)
                dve.wait_ge(S["score_free"], 4 * (4 * s.n + i) + 2 * WIDE)
                dve.tensor_scalar(ntop[:, i % 2, :], top[:, i % 2, :], -SCALE, None, ALU.mult).then_inc(S["ntop_ready"], 1)

            def narrow_scores(s, i):
                dve.wait_ge(S["prod_ready"], 4 * s.n + i + 1)
                own.mark(dve.tensor_reduce(sc[:, i, :], prod[:, i, :].rearrange("p (c d) -> p c d", d=D), X_AXIS, ALU.add))

            def end(t, i):
                u = t.u
                if i == 0:
                    dve.wait_ge(S["att_hi"], t.n + 1)
                    dve.tensor_tensor(attl[:], b_tail[:], atth[:].bitcast(F32), ALU.subtract).then_inc(S["att_lo"], 1)
                if i == 1:
                    dve.wait_ge(S["projected"], t.n + 1)
                    dve.wait_ge(xres_in[u], 16 * (t.half + 1))
                    dve.tensor_tensor(hid[:].rearrange("p i c -> p (i c)"), b_tail[:],
                                      xres[u][:].rearrange("p i c -> p (i c)"), ALU.add).then_inc(S["hid_ready"], 1)
                    dve.wait_ge(S["hid_ready"], t.n + 1)
                    y = statistics(tail, hid)
                    dve.wait_ge(S["rows_free"], t.n + 1)
                    for k in range(TILES):
                        ins = dve.tensor_scalar(rowb[u][0][:, k, 0:C], hid[:, k, :], mv[:, k, 0:1], y[:, k:k + 1],
                                                ALU.subtract, ALU.mult)
                    ins.then_inc(S["rows_x"], 1)
                    for k in range(TOP):
                        ins = dve.tensor_copy(rowb[u][k][:, :, C + 1:C + 2].bitcast(I32),
                                              place_c[:, bass.ds(4 * t.n + k * SEQS * TILES, TILES)].unsqueeze(2))
                    tail.mark(ins)
                if i == 2:
                    dve.wait_ge(S["x1_hi"], t.n + 1)
                    dve.tensor_tensor(attl[:], b_tail[:], atth[:].bitcast(F32), ALU.subtract).then_inc(S["x1_lo"], 1)
                if i == 3:
                    dve.wait_ge(S["logits_ready"], t.n + 1)
                    tail.mark(dve.tensor_copy(logit[:].rearrange("p i e -> p (i e)"), b_tail[:, 0:TILES * EXPERTS]))
                    wait_alone(dve, tail.sem, tail.value())
                    for k in range(TILES):
                        ins = dve.max(best[:, k, :], logit[:, k, :])
                    tail.mark(ins)
                    wait_alone(dve, tail.sem, tail.value())
                    for k in range(TILES):
                        ins = dve.max_index(ibest[:, k, :], best[:, k, :], logit[:, k, :])
                    tail.mark(ins)
                    dve.tensor_tensor(diff[:], best[:, :, 1], best[:, :, 0], ALU.subtract).then_inc(S["diff_ready"], 1)
                    tail.wait()
                    tail.mark(dve.tensor_copy(ibf[:], ibest[:]))
                    tail.wait()
                    tail.mark(dve.tensor_tensor(oh[:], ibf[:, :, 0:TOP].unsqueeze(3).broadcast_to([P, TILES, TOP, EXPERTS]),
                                                kc[:, K_I8:K_I8 + EXPERTS].unsqueeze(1).unsqueeze(1).broadcast_to([P, TILES, TOP, EXPERTS]),
                                                ALU.is_equal))
                    tail.wait()
                    dve.tensor_tensor(mem[:], oh[:, :, 0, :], oh[:, :, 1, :], ALU.add).then_inc(S["mem_ready"], 1)
                    dve.wait_ge(S["edif_ready"], t.n + 1)
                    tail.mark(dve.tensor_scalar(edif1[:], edif[:], 1.0, None, ALU.add))
                    tail.wait()
                    tail.mark(dve.reciprocal(wtop[:], edif1[:]))
                    tail.wait()
                    tail.mark(dve.tensor_copy(rowb[u][0][:, :, C:C + 1], wtop[:].unsqueeze(2)))
                    tail.mark(dve.tensor_tensor(rowb[u][1][:, :, C:C + 1], wtop[:].unsqueeze(2), edif[:].unsqueeze(2), ALU.mult))
                    dve.wait_ge(S["mem_ready"], t.n + 1)
                    tail.mark(dve.tensor_reduce(memf[:], mem[:].rearrange("p i e -> p e i"), X_AXIS, ALU.add))
                    tail.wait()
                    tail.mark(dve.tensor_tensor(mtot[1 - u][:], mtot[u][:], memf[:], ALU.add))
                if i == 4:
                    dve.wait_ge(S["ranks"], t.n + 1)
                    dve.tensor_tensor(rank[:], b_tail[:, 64:64 + TILES * EXPERTS].rearrange("p (i e) -> p i e", e=EXPERTS),
                                      kc[:, K_EC:K_EC + EXPERTS].unsqueeze(1).broadcast_to([P, TILES, EXPERTS]),
                                      ALU.add).then_inc(S["tail_free"], 1)
                    dve.wait_ge(S["tail_free"], t.n + 2)
                    tail.mark(dve.tensor_tensor(pick[:], oh[:], rank[:].unsqueeze(2).broadcast_to([P, TILES, TOP, EXPERTS]), ALU.mult))
                    tail.wait()
                    dve.wait_ge(S["x1_kept"], t.n + 1)
                    tail.mark(dve.tensor_reduce(slotf[:], pick[:], X_AXIS, ALU.add))
                    tail.wait()
                    dve.tensor_copy(slot[u][:], slotf[:]).then_inc(S["slots_ready"], 1)

            def stacks(n):
                dve.wait_ge(S["khi"], n.n + 1)
                dve.scalar_tensor_tensor(kst[:], hi_k[:].bitcast(F32), kc[:, K_NK:K_NK + 1], b_k[:],
                                         ALU.mult, ALU.add).then_inc(S["kst_ready"], 1)
                dve.wait_ge(S["qhi"], n.n + 1)
                dve.scalar_tensor_tensor(qst[:], hi_q[:].bitcast(F32), kc[:, K_NQ:K_NQ + 1], b_q[:],
                                         ALU.mult, ALU.add).then_inc(S["qst_ready"], 1)

            def step(s, t, n):
                if s:
                    own.round(s.n)
                if t:
                    tail.round(t.n)
                for i in range(TILES):
                    if s:
                        window(s, i)
                        if i == 2:
                            narrow_scores(s, 0)
                            narrow_scores(s, 1)
                        if i == 3:
                            narrow_scores(s, 2)
                    if n and i == 1:
                        x_lo(n)
                    if t and i < 3:
                        end(t, i)
                if s:
                    u = s.u
                    narrow_scores(s, TILES - 1)
                    own.wait()
                    own.mark(dve.tensor_tensor(sc[:, 0, :], sc[:, 0, :], kc[:, K_SM:K_SM + PAIRS], ALU.add))
                    gl = qg[u][:, :, NW:QG]
                    own.mark(dve.tensor_reduce(gmax[:], gl, X_AXIS, ALU.max))
                    own.wait()
                    n4 = OFFS * NARROW
                    by_head = sc[:, :, 0:n4].rearrange("p i (o h) -> p i h o", o=OFFS)
                    own.mark(dve.tensor_reduce(nmax[:], by_head, X_AXIS, ALU.max))
                    own.mark(dve.tensor_reduce(nmax2[:], sc[:, :, n4:PAIRS], X_AXIS, ALU.max))
                    own.mark(dve.tensor_tensor(gd[:], gl, gmax[:].unsqueeze(2).broadcast_to([P, TILES, HEADS]), ALU.subtract))
                    own.wait()
                    own.mark(dve.tensor_tensor(nmax3[:], nmax2[:], nmax[:, :, 0], ALU.max))
                    own.wait()
                    own.mark(dve.tensor_copy(nmax[:, :, 0], nmax3[:]))
                    own.mark(dve.tensor_tensor(scd[:, :, n4:PAIRS], sc[:, :, n4:PAIRS],
                                               nmax3[:].unsqueeze(2).broadcast_to([P, TILES, OFFS]), ALU.subtract))
                    own.wait()
                    for i in range(TILES):
                        ins = dve.tensor_tensor(scd[:, i, 0:n4].rearrange("p (o h) -> p o h", o=OFFS),
                                                sc[:, i, 0:n4].rearrange("p (o h) -> p o h", o=OFFS),
                                                nmax[:, i, :].unsqueeze(1).broadcast_to([P, OFFS, NARROW]), ALU.subtract)
                    ins.then_inc(S["sc_ready"], 1)
                if t:
                    end(t, 3)
                if n:
                    stacks(n)
                if t:
                    end(t, 4)
                if s:
                    dve.wait_ge(S["ex_ready"], s.n + 1)
                    dve.wait_ge(S["p_ready"], 4 * s.n + 4)
                    own.mark(dve.tensor_reduce(sums[u][:, :, WIDE:HEADS], ex[:, :, 0:n4].rearrange("p i (o h) -> p i h o", o=OFFS), X_AXIS, ALU.add))
                    own.mark(dve.tensor_reduce(xsum[:], ex[:, :, n4:PAIRS], X_AXIS, ALU.add))
                    own.mark(dve.tensor_reduce(gsum[:], ge[:], X_AXIS, ALU.add))
                    own.wait()
                    own.mark(dve.tensor_tensor(xsum2[:], xsum[:], sums[u][:, :, WIDE], ALU.add))
                    own.wait()
                    own.mark(dve.tensor_copy(sums[u][:, :, WIDE], xsum2[:]))
                    own.wait()
                    own.mark(dve.tensor_tensor(den[:], sums[u][:], gsum[:].unsqueeze(2).broadcast_to([P, TILES, HEADS]), ALU.mult))
                    own.wait()
                    own.mark(dve.reciprocal(rden[:], den[:]))
                    own.wait()
                    own.mark(dve.tensor_tensor(gn[:], ge[:], rden[:], ALU.mult))
                    dve.wait_ge(S["pk_ready"], 4 * s.n + 4)
                    dve.tensor_reduce(raw[:], kt[u][:, :, 0:OFFS * NW].rearrange("p i (o c) -> p i c o", o=OFFS), X_AXIS, ALU.add)
                    own.mark(dve.tensor_reduce(raw4[:], kt[u][:, :, OFFS * NW:PK].rearrange("p i (o c) -> p i c o", o=OFFS), X_AXIS, ALU.add))
                    own.wait()
                    ins = dve.tensor_tensor(raw5[:], raw4[:], raw[:, :, 0:D], ALU.add)
                    own_last(ins)
                    dve.tensor_tensor(att[:, :, WIDE * D + D:C].rearrange("p i (h d) -> p i h d", d=D),
                                      raw[:, :, D:NW].rearrange("p i (h d) -> p i h d", d=D),
                                      gn[:, :, WIDE + 1:HEADS].unsqueeze(3).broadcast_to([P, TILES, NARROW - 1, D]), ALU.mult)
                    dve.tensor_tensor(att[:, :, WIDE * D:WIDE * D + D], raw5[:],
                                      gn[:, :, WIDE:WIDE + 1].broadcast_to([P, TILES, D]), ALU.mult)
                    dve.wait_ge(S["pv"], 4 * s.n + 4)
                    dve.tensor_tensor(att[:, :, 0:WIDE * D].rearrange("p i (h d) -> p i h d", d=D),
                                      b_pv[:, 0:TILES * WIDE * D].rearrange("p (i h d) -> p i h d", i=TILES, d=D),
                                      gn[:, :, 0:WIDE].unsqueeze(3).broadcast_to([P, TILES, WIDE, D]), ALU.mult).then_inc(S["att_ready"], 1)
                    dve.wait_ge(S["att_ready"], s.n + 1)
                    dve.sem_inc(S["pv_free"], 1)
                    dve.wait_ge(S["w_hi"], s.n + 3)
                    e = bass.ds(s.n, 1)
                    dve.tensor_tensor(w12s[:, e, :, 1, :], w12f[:].rearrange("p (a k f) -> p a k f", a=1, k=2),
                                      w12s[:, e, :, 0, :].bitcast(F32), ALU.subtract).then_inc(S["w_lo"], 1)

            def own_last(ins):
                own.mark(ins)
                own.wait()

            stacks(Seq(0, 0, 0))
            stage_a(dve, step)

            plan = Chain(dve, S["setup_dve"], 0)
            n = EXPERTS
            dve.wait_ge(S["totals"], 1)
            row = lambda a, k: rc[0:1, a:a + k]

            def then(ins):
                plan.mark(ins)
                plan.wait()

            then(dve.tensor_copy(cnt[:], b_tail[0:1, 0:n]))
            then(dve.tensor_tensor(t_fill[:], cnt[:], row(R_EB, n), ALU.add))
            then(dve.tensor_tensor(cmp32[:], cnt[:].unsqueeze(2).broadcast_to([1, n, MOST]),
                                   row(R_M, MOST).unsqueeze(1).broadcast_to([1, n, MOST]), ALU.is_gt))
            then(dve.tensor_reduce(nblk[:], cmp32[:], X_AXIS, ALU.add))
            then(dve.tensor_tensor(cum3[:], nblk[:].unsqueeze(1).broadcast_to([1, n, n]),
                                   row(R_TRI, n * n).rearrange("p (a b) -> p a b", b=n), ALU.mult))
            then(dve.tensor_reduce(cend[:], cum3[:], X_AXIS, ALU.add))
            then(dve.tensor_tensor(shift[:], nblk[:], cend[:], ALU.subtract))
            then(dve.scalar_tensor_tensor(shift2[:], row(R_EB, n), 1.0 / BR, shift[:], ALU.mult, ALU.add))
            wide = [1, BLOCKS, n]
            then(dve.tensor_tensor(bge[:], row(R_B, BLOCKS).unsqueeze(2).broadcast_to(wide),
                                   cend[:].unsqueeze(1).broadcast_to(wide), ALU.is_ge))
            then(dve.tensor_reduce(bexp[:], bge[:], X_AXIS, ALU.add))
            then(dve.tensor_tensor(boh[:], bexp[:].unsqueeze(2).broadcast_to(wide),
                                   row(R_E, n).unsqueeze(1).broadcast_to(wide), ALU.is_equal))
            then(dve.tensor_tensor(boh2[:], boh[:], shift2[:].unsqueeze(1).broadcast_to(wide), ALU.mult))
            then(dve.tensor_reduce(bsh[:], boh2[:], X_AXIS, ALU.add))
            then(dve.tensor_tensor(brow[:], bsh[:], row(R_B, BLOCKS), ALU.add))
            then(dve.tensor_scalar(bun[:], bexp[:], float(n), None, ALU.is_ge))
            then(dve.tensor_scalar(bun2[:], brow[:], -1.0, float(ZERO_ROW // BR), ALU.mult, ALU.add))
            then(dve.tensor_tensor(bun3[:], bun2[:], bun[:], ALU.mult))
            then(dve.tensor_tensor(brow2[:], brow[:], bun3[:], ALU.add))
            then(dve.tensor_scalar(t_row[:], brow2[:], float(BR), None, ALU.mult))
            dve.tensor_scalar(t_exp[:], bexp[:], float(n - 1), None, ALU.min).then_inc(S["plan_ready"], 1)

            px, pyt = bank[4], bank[7]

            def take_weights(e, b, i, product, kept, ready):
                done = S["h_ready"] if product == 0 else S["y_done"]
                if not isinstance(b, int) or b >= 2:
                    dve.wait_ge(done, b - 1 + 2 * product)
                dve.tensor_copy(kept[i % 2][:].unsqueeze(1), w12s[:, bass.ds(e, 1), product, :, :]).then_inc(ready, 1)

            def x_part(b, q, i):
                dve.wait_ge(S["xb_hi"], b + 1)
                dve.tensor_tensor(xbl[i % 2][:], px[:, 0:BR], xbh[i % 2][:].bitcast(F32), ALU.subtract).then_inc(S["xb_lo"], 1)

            def expert_of(b):
                return dve.value_load(t_exp[0:1, bass.ds(b, 1)], min_val=0, max_val=EXPERTS - 1)

            def keep_places(b, q, i):
                dve.wait_ge(block_in[i], 16 * (q + 1))
                if not (isinstance(b, int) and b < RING):
                    dve.wait_ge(y_out[i], 16 * (BR // P) * q)
                dve.tensor_copy(wd[i][:], xb[i][:, :, C:ROW]).then_inc(S["wd_ready"], 1)

            def weigh(b, i):
                k = i % RING
                dve.wait_ge(S["y_turned"], b + 3)
                dve.wait_ge(S["wd_ready"], b + 1)
                for j in range(BR // P):
                    ins = dve.tensor_scalar(yb[k][:, j, :], pyt[:, C * j:C * j + C], wd[k][:, j, 0:1], None, ALU.mult)
                ins.then_inc(S["y_ready"], 1)

            def b_step(b, q, i):
                static = isinstance(b, int)
                if not static or b + 1 < BLOCKS:
                    x_part(b + 1, q + (i + 1) // RING, (i + 1) % RING)
                if not static or b >= 3:
                    weigh(b - 3, i - 3)
                if not static or 1 <= b <= BLOCKS:
                    k = (i - 1) % 2
                    dve.wait_ge(S["g_hi"], b)
                    dve.tensor_tensor(gl[k][:], g[k][:], gh[k][:].bitcast(F32), ALU.subtract).then_inc(S["g_lo"], 1)
                    e = expert_of(b - 1)
                if not static or b + 2 < BLOCKS:
                    e2 = expert_of(b + 2)
                if not static or 1 <= b <= BLOCKS:
                    keep_places(b - 1, (b - 1) // RING if static else q - (i < 1), (i - 1) % RING)
                    take_weights(e, b - 1, i - 1, 1, w2s, S["w2_ready"])
                if not static or b + 2 < BLOCKS:
                    take_weights(e2, b + 2, i, 0, w1s, S["w1_ready"])

            x_part(0, 0, 0)
            for b in range(2):
                take_weights(expert_of(b), b, b, 0, w1s, S["w1_ready"])
            b_loop(dve, b_step)

            fin = Chain(dve, S["dve_c"], 15)

            def last(n, u, half):
                fin.round(n)
                flat = lambda a: a.rearrange("p i c -> p (i c)")
                dve.wait_ge(c_in[u], 16 * (TOP + 1) * (half + 1))
                fin.mark(dve.tensor_tensor(ysum[:], ya[u][0][:], ya[u][1][:], ALU.add))
                fin.wait()
                fin.mark(dve.tensor_tensor(h2[u][:], ysum[:], x1c[u][:], ALU.add))
                fin.wait()
                y = statistics(fin, h2[u])
                if not (isinstance(n, int) and n < 2):
                    dve.wait_ge(c_out[u], 16 * half)
                for k in range(TILES):
                    ins = dve.tensor_scalar(o2[u][:, k, :], h2[u][:, k, :], mv[:, k, 0:1], y[:, k:k + 1],
                                            ALU.subtract, ALU.mult)
                ins.then_inc(S["c_ready"], 1)
                dve.wait_ge(S["c_ready"], n + 1)

            last(0, 0, 0)
            last(1, 1, 0)
            with dve.Fori(1, SEQS // 2) as j:
                last(2 * j, 0, j)
                last(2 * j + 1, 1, j)


def kernel(L0_attn_x, L0_attn_Wqk, L0_attn_bqk, L0_attn_Wgate, L0_attn_bgate, L0_attn_Wproj,
           L0_attn_bproj, L0_ffn_router_w, L0_ffn_w1, L0_ffn_b1, L0_ffn_w2, L0_ffn_b2):
    import numpy as np
    import concourse.bacc as bacc
    from concourse.bass_utils import run_bass_kernel_spmd

    f4 = np.float32
    x = np.asarray(L0_attn_x).reshape(SEQS * T, C)
    wqk, bqk = np.asarray(L0_attn_Wqk), np.asarray(L0_attn_bqk)
    rep = np.array([D * h + d for h in range(WIDE) for _ in range(4) for d in range(D)])
    w_att = np.concatenate([wqk[:, C + rep], wqk[:, rep], wqk[:, C:2 * C], wqk[:, WIDE * D:C],
                            np.asarray(L0_attn_Wgate), np.asarray(L0_attn_Wproj),
                            np.asarray(L0_ffn_router_w).T], axis=1)
    bk = bqk[C:2 * C]
    b_att = np.concatenate([bk[rep], bqk[rep], bk, bqk[WIDE * D:C], np.asarray(L0_attn_bgate), np.asarray(L0_attn_bproj)])
    b_att = np.stack([b_att, b_att])
    w1 = np.asarray(L0_ffn_w1).transpose(2, 0, 1).reshape(C, EXPERTS * F)
    w2 = np.asarray(L0_ffn_w2).reshape(EXPERTS, C, FC, P).transpose(3, 0, 2, 1).reshape(P, EXPERTS * F)
    w12 = np.concatenate([w1.reshape(P, EXPERTS, F), w2.reshape(P, EXPERTS, F)], axis=2).reshape(P, EXPERTS * 2 * F)
    b12 = np.concatenate([np.asarray(L0_ffn_b1).reshape(EXPERTS, FC, P), np.asarray(L0_ffn_b2)[:, None, :]],
                         axis=1).transpose(2, 0, 1).reshape(P, EXPERTS * (FC + 1))

    k = np.zeros((P, K_COLS), f4)
    k[:, K_ID:K_ID + P] = np.eye(P)
    q = np.arange(P)[:, None]
    for h, w in enumerate(WINDOWS):
        key = np.arange(KEYS[h])[None, :] - w
        ok = (key <= q) & (key > q - w)
        k[:, K_MN + KEY_AT[h]:K_MN + KEY_AT[h] + KEYS[h]] = np.where(ok, 0.0, LOW)
    off = np.concatenate([np.repeat(np.arange(OFFS)[::-1], NARROW), np.arange(OFFS, 2 * OFFS)[::-1]])[None, :]
    k[:, K_SM:K_SM + PAIRS] = np.where(off <= q, 0.0, LOW)
    part = (np.arange(P) // D) % 4
    k[:, K_NK] = -(part % 2)
    k[:, K_NQ] = -(part // 2)
    k[1, K_NB] = -1.0
    k[:, K_I8:K_I8 + EXPERTS] = np.arange(EXPERTS)
    k[:, K_EC:K_EC + EXPERTS] = np.arange(EXPERTS) * CAP
    k[:, K_TRI:K_TRI + P] = np.triu(np.ones((P, P)), 1)
    r = np.zeros((1, R_COLS), f4)
    r[0, R_B:R_B + BLOCKS] = np.arange(BLOCKS)
    r[0, R_E:R_E + 8] = np.arange(8)
    r[0, R_M:R_M + MOST] = np.arange(MOST) * BR
    r[0, R_TRI:R_TRI + 64] = np.tril(np.ones((8, 8))).reshape(-1)
    r[0, R_EB:R_EB + 8] = np.arange(8) * CAP
    places = np.arange(PLACES).reshape(TOP * SEQS * TILES, P).T.astype(np.int32)

    nc = bacc.Bacc("TRN2", target_bir_lowering=False, num_devices=1)
    arrays, args = {}, []
    for name, a in (("x", x), ("xt", x.T), ("w_att", w_att), ("b_att", b_att), ("w12", w12),
                    ("b12", b12), ("consts", k), ("rowc", r), ("places", places)):
        a = np.ascontiguousarray(a)
        arrays[name] = a
        args.append(nc.dram_tensor(name, a.shape, mybir.dt.from_np(a.dtype), kind="ExternalInput").ap())
    args.append(nc.dram_tensor("out", (SEQS * T, C), F32, kind="ExternalOutput").ap())
    program(nc, *args)
    got = run_bass_kernel_spmd(nc, [arrays], core_ids=[0])
    return got.results[0]["out"].reshape(SEQS, T, C)
```

```python
from contextlib import ExitStack

import concourse.bass as bass
from concourse import mybir

F32 = mybir.dt.float32
F32R = mybir.dt.float32r
BF16 = mybir.dt.bfloat16
I32 = mybir.dt.int32
U32 = mybir.dt.uint32
ALU = mybir.AluOpType
ACT = mybir.ActivationFunctionType
X_AXIS = mybir.AxisListType.X

P = 128
SEQS, T, C = 8, 512, 128
TILES = T // P
HEADS, D = 16, 8
SCALE = float(D) ** -0.5
EPS = 1e-5
LOW = -3.0e38

WIDE = 4
WINDOWS = [128, 64, 32, 16]
PREV_AT = [0, 0, 64, P - WINDOWS[3]]
KEYS = [w + P for w in WINDOWS]
KEY_AT = [sum(KEYS[:h]) for h in range(WIDE)]
ALL_KEYS = sum(KEYS)
NARROW = HEADS - WIDE
OFFS = 4
NW = NARROW * D
PAIRS = OFFS * NARROW + OFFS
PK = PAIRS * D
EMPTY = 2 * OFFS

W_KREP, W_QREP, W_K, W_QG, W_PROJ, W_R = 0, 128, 256, 384, 496, 624
W_BK, W_BQ = 632, 633
W_COLS = 634
B_KQ, B_PROJ = 0, 240
B_COLS = B_PROJ + 128
QG = NW + HEADS
KQ = C + QG

EXPERTS, F, TOP = 8, 512, 2
FC = F // P
BR = 2 * P
CAP = SEQS * T + BR
ZERO_ROW = EXPERTS * CAP
ROWS = ZERO_ROW + BR
MOST = SEQS * T // BR
ROW = C + 2
PLACES = TOP * SEQS * T
CT = 2 * TILES
PARTS = [(0, CT // 2)] + [(a, CT) for a in range(CT // 2, SEQS * TILES - CT, CT)] + [(SEQS * TILES - CT // 2, CT // 2)]
NOWHERE = 1 << 20
BLOCKS = PLACES // BR + EXPERTS

K_ID, K_MN = 0, 128
K_SM = K_MN + ALL_KEYS
K_NK, K_NQ, K_NB = K_SM + PAIRS, K_SM + PAIRS + 1, K_SM + PAIRS + 2
K_I8 = K_NB + 1
K_EC = K_I8 + EXPERTS
K_TRI = K_EC + EXPERTS
K_COLS = K_TRI + P
R_B, R_E, R_M = 0, BLOCKS, BLOCKS + 8
R_TRI, R_EB = R_M + MOST, R_M + MOST + 64
R_COLS = R_EB + 8


class Seq:

    def __init__(self, n, half, odd):
        self.n, self.half, self.u = n, half, odd


class Chain:

    def __init__(self, eng, sem, per, base=0):
        self.eng, self.sem, self.per, self.start, self.base, self.k = eng, sem, per, base, base, 0

    def round(self, n):
        assert self.k in (0, self.per), (self.k, self.per)
        self.base, self.k = n * self.per + self.start, 0

    def mark(self, ins):
        ins.then_inc(self.sem, 1)
        self.k += 1
        return ins

    def wait(self):
        self.eng.wait_ge(self.sem, self.base + self.k)

    def value(self):
        return self.base + self.k


def program(nc, x, xt, w_att, b_att, w12, b12, consts, rowc, places, out):
    ctx = ExitStack()
    with ctx:
        stage_a_only = ExitStack()
        place = [ctx]

        def sb(name, shape, dt=F32):
            return place[-1].enter_context(nc.sbuf_tensor(name, shape, dt))

        def sem(name):
            return ctx.enter_context(nc.semaphore(name))

        rows = nc.dram_tensor("expert_rows", (ROWS, ROW), F32, kind="Internal").ap()
        x1 = nc.dram_tensor("x1", (SEQS * T, C), F32, kind="Internal").ap()
        res = nc.dram_tensor("expert_results", (PLACES, C), F32, kind="Internal").ap()

        keys = [nc.dram_tensor(f"keys{u}", (EMPTY + T, NW), F32, kind="Internal").ap() for u in range(2)]
        keys4 = [nc.dram_tensor(f"keys4_{u}", (EMPTY + T, D), F32, kind="Internal").ap() for u in range(2)]

        psum = [ctx.enter_context(nc.psum_tensor(f"banks{i}", [P, 1024], F32)) for i in range(4)]
        bank = [psum[i // 2][:, 512 * (i % 2):512 * (i % 2) + 512] for i in range(8)]

        kc = sb("kc", [P, K_COLS])
        rc = sb("rc", [1, R_COLS])
        place_c = sb("place_c", [P, TOP * SEQS * TILES], I32)
        tri = sb("tri", [P, P], BF16)
        ones_b = sb("ones_b", [P, P], BF16)
        ones2 = sb("ones2", [2, T], F32R)
        wah = sb("wah", [P, W_COLS], F32R)
        wal = sb("wal", [P, W_COLS], F32R)
        wr = sb("wr", [P, 2 * EXPERTS], F32R)
        bas = sb("bas", [2, B_COLS], F32R)
        rowb = [[sb(f"row{k}_{u}", [P, TILES, ROW]) for k in range(TOP)] for u in range(2)]
        slot = [sb(f"slot{u}", [P, TILES, TOP], I32) for u in range(2)]
        table = sb("table", [P, 1])
        proj_bias = sb("proj_bias", [P, C])
        zeros = sb("zeros", [EMPTY, NW])
        fill = sb("fill", [P, BR // P, ROW])
        mtot = [sb(f"mtot{u}", [P, EXPERTS], BF16) for u in range(2)]
        stat = sb("stat", [P, TILES, 6])
        mv = sb("mv", [P, TILES, 2])
        va = sb("va", [P, TILES])
        nwt = [sb(f"nwt{i}", [P, TILES]) for i in range(10)]
        w12s = sb("w12s", [P, EXPERTS, 2, 2, F], F32R)
        b12c = sb("b12c", [P, EXPERTS * (FC + 1)])

        place.append(ctx.enter_context(stage_a_only))
        w12f = sb("w12f", [P, 2 * F])
        xtf = sb("xtf", [P, T])
        xres = [sb(f"xres{u}", [P, TILES, C]) for u in range(2)]
        xth = sb("xth", [P, T], F32R)
        xtl = sb("xtl", [P, T], F32R)
        wide_bias = sb("wide_bias", [P, 2])
        less_bias = sb("less_bias", [P, 2])
        hi_k = sb("hi_k", [P, T], F32R)
        hi_q = sb("hi_q", [P, T], F32R)
        kst = sb("kst", [P, T], F32R)
        qst = sb("qst", [P, T], F32R)
        qg = [sb(f"qg{u}", [P, TILES, QG]) for u in range(2)]
        wide_k = [sb(f"wide{u}", [P, TILES, WIDE, 32 + D]) for u in range(2)]
        wide_b = [sb(f"wide_b{u}", [P, TILES - 1, 32]) for u in range(2)]
        key = [sb(f"key{u}", [P, TILES, NW]) for u in range(2)]
        kt = [sb(f"kt{u}", [P, TILES, PK]) for u in range(2)]
        scored = [sb(f"scored{u}", [P, ALL_KEYS]) for u in range(2)]
        top = sb("top", [P, 2, WIDE])
        ntop = sb("ntop", [P, 2, WIDE])
        prob = [sb(f"prob{u}", [P, WIDE, 2 * P]) for u in range(2)]
        joint = [sb(f"joint{u}", [P, P]) for u in range(2)]
        setup_only = ExitStack()
        place.append(ctx.enter_context(setup_only))
        wa = sb("wa", [P, W_COLS])
        ba = sb("ba", [2, B_COLS])
        bah = sb("bah", [2, B_COLS], F32R)
        setup_only.close()
        place.pop()
        pta = [sb(f"pta{u}", [P, WIDE, P]) for u in range(2)]
        ptb = [sb(f"ptb{u}", [P, 2, P]) for u in range(2)]
        pvt = sb("pvt", [WIDE * D, T])
        sums = [sb(f"sums{u}", [P, TILES, HEADS]) for u in range(2)]
        prod = sb("prod", [P, TILES, PK])
        sc = sb("sc", [P, TILES, PAIRS])
        nmax = sb("nmax", [P, TILES, NARROW])
        nmax2 = sb("nmax2", [P, TILES])
        nmax3 = sb("nmax3", [P, TILES])
        scd = sb("scd", [P, TILES, PAIRS])
        ex = sb("ex", [P, TILES, PAIRS])
        gmax = sb("gmax", [P, TILES])
        gd = sb("gd", [P, TILES, HEADS])
        ge = sb("ge", [P, TILES, HEADS])
        gsum = sb("gsum", [P, TILES])
        xsum = sb("xsum", [P, TILES])
        xsum2 = sb("xsum2", [P, TILES])
        den = sb("den", [P, TILES, HEADS])
        rden = sb("rden", [P, TILES, HEADS])
        gn = sb("gn", [P, TILES, HEADS])
        raw = sb("raw", [P, TILES, NW])
        raw4 = sb("raw4", [P, TILES, D])
        raw5 = sb("raw5", [P, TILES, D])
        att = sb("att", [P, TILES, C])
        atth = sb("atth", [P, T], F32R)
        attl = sb("attl", [P, T], F32R)
        hid = sb("hid", [P, TILES, C])
        best = sb("best", [P, TILES, 8])
        logit = sb("logit", [P, TILES, EXPERTS])
        ibest = sb("ibest", [P, TILES, 8], U32)
        ibf = sb("ibf", [P, TILES, 8])
        diff = sb("diff", [P, TILES])
        edif = sb("edif", [P, TILES])
        edif1 = sb("edif1", [P, TILES])
        wtop = sb("wtop", [P, TILES])
        wtop2 = sb("wtop2", [P, TILES])
        oh = sb("oh", [P, TILES, TOP, EXPERTS])
        mem = sb("mem", [P, TILES, EXPERTS], BF16)
        memf = sb("memf", [P, EXPERTS])
        rank = sb("rank", [P, TILES, EXPERTS])
        slotf = sb("slotf", [P, TILES, TOP])
        pick = sb("pick", [P, TILES, TOP, EXPERTS])

        stage_a_only.close()
        place.pop()

        cnt = sb("cnt", [1, EXPERTS])
        cmp32 = sb("cmp32", [1, EXPERTS, MOST])
        nblk = sb("nblk", [1, EXPERTS])
        cum3 = sb("cum3", [1, EXPERTS, EXPERTS])
        cend = sb("cend", [1, EXPERTS])
        shift = sb("shift", [1, EXPERTS])
        shift2 = sb("shift2", [1, EXPERTS])
        bge = sb("bge", [1, BLOCKS, EXPERTS])
        bexp = sb("bexp", [1, BLOCKS])
        boh = sb("boh", [1, BLOCKS, EXPERTS])
        boh2 = sb("boh2", [1, BLOCKS, EXPERTS])
        bsh = sb("bsh", [1, BLOCKS])
        bun = sb("bun", [1, BLOCKS])
        bun2 = sb("bun2", [1, BLOCKS])
        bun3 = sb("bun3", [1, BLOCKS])
        brow = sb("brow", [1, BLOCKS])
        brow2 = sb("brow2", [1, BLOCKS])
        t_row = sb("t_row", [1, BLOCKS], I32)
        t_exp = sb("t_exp", [1, BLOCKS], I32)
        t_fill = sb("t_fill", [1, EXPERTS], I32)

        RING = 4
        xb = [sb(f"xb{i}", [P, BR // P, ROW]) for i in range(RING)]
        wd = [sb(f"wd{i}", [P, BR // P, 2]) for i in range(RING)]
        w1s = [sb(f"w1s{i}", [P, 2, F], F32R) for i in range(2)]
        w2s = [sb(f"w2s{i}", [P, 2, F], F32R) for i in range(2)]
        xbh = [sb(f"xbh{i}", [P, BR], F32R) for i in range(2)]
        xbl = [sb(f"xbl{i}", [P, BR], F32R) for i in range(2)]
        g = [sb(f"g{i}", [P, FC * BR]) for i in range(2)]
        gh = [sb(f"gh{i}", [P, FC * BR], F32R) for i in range(2)]
        gl = [sb(f"gl{i}", [P, FC * BR], F32R) for i in range(2)]
        yt = [sb(f"yt{i}", [P, BR]) for i in range(2)]
        yb = [sb(f"yb{i}", [P, BR // P, C]) for i in range(RING)]
        x1c = sb("x1c", [P, SEQS * TILES, C])
        ya = [sb(f"ya{k}", [P, SEQS * TILES, C]) for k in range(TOP)]
        cstat = sb("cstat", [P, CT, 6])
        cmv = sb("cmv", [P, CT, 2])
        cva = sb("cva", [P, CT])
        cnwt = [sb(f"cnwt{i}", [P, CT]) for i in range(10)]
        cbias = [sb(f"cbias{u}", [P, CT]) for u in range(2)]
        crstd = [sb(f"crstd{u}", [P, CT]) for u in range(2)]

        names = []
        names += "const_in weights_in biases_in".split()
        names += "weights_ready zeros_ready w_hi w_lo".split()
        names += "x_hi x_lo kproj qproj khi qhi kst_ready qst_ready".split()
        names += "kq_done kq_copied keys_out".split()
        names += "scores score_free ntop_ready exps joined turned pta_out ptb_out".split()
        names += "pv pv_out pv_turned pv_free".split()
        names += "prod_ready sc_ready ex_ready pk_ready".split()
        names += "att_ready att_turned att_hi att_lo projected xres_ready hid_ready rows_x".split()
        names += "x1_kept x1_turned x1_hi x1_lo logits_ready".split()
        names += "tail_free diff_ready edif_ready mem_ready ranks slots_ready rows_free".split()
        names += "dve_a dve_m dve_t dve_c setup_dve pool_a".split()
        names += "totals plan_ready fill_at_ready fill_ready rows_filled".split()
        names += "x_turned xb_hi xb_lo wd_ready".split()
        names += "w1_ready w2_ready h_ready g_ready g_hi g_lo y_done y_copied y_turned y_ready".split()
        names += "x1_in summed added c_scale c_ready c_out".split()
        S = {n: sem(n) for n in names}
        xt_in = sem("xt_in")
        keys_in = [sem(f"keys_in{u}") for u in range(2)]
        wide_in = [sem(f"wide_in{u}") for u in range(2)]
        xres_in = [sem(f"xres_in{u}") for u in range(2)]
        expert_in = sem("expert_in")
        x1_out = [sem(f"x1_out{u}") for u in range(2)]
        scattered = [sem(f"scattered{u}") for u in range(2)]
        block_in = [sem(f"block_in{i}") for i in range(RING)]
        y_out = [sem(f"y_out{i}") for i in range(RING)]
        ya_in = [sem(f"ya_in{part}") for part in range(len(PARTS))]

        ident = kc[:, K_ID:K_ID + P]
        b_kp, b_qp = bank[0], bank[1]
        b_k, b_q, b_c, b_pv, b_tail = bank[4], bank[5], bank[6], bank[7], bank[3]
        score_at = [bank[0][:, 0:KEYS[0]], bank[1][:, 0:KEYS[1]], bank[2][:, 0:KEYS[2]],
                    bank[2][:, 256:256 + KEYS[3]]]

        def wait_alone(eng, semaphore, value):
            if not isinstance(value, int):
                eng.reg_mov(carrier[eng.engine], value)
                eng.wait_ge(S["const_in"], 48)
                value = carrier[eng.engine]
            eng.wait_ge(semaphore, value)

        carrier = {}

        def prepare_carrier(eng):
            carrier[eng.engine] = eng.alloc_register("carrier")
            eng.reg_mov(carrier[eng.engine], 0)

        def fill_rows(eng, experts):
            eng.wait_ge(S["fill_at_ready"], 1)
            for e in experts:
                at = eng.value_load(t_fill[0:1, e:e + 1], min_val=0, max_val=ZERO_ROW - BR)
                eng.dma_start(rows[bass.ds(at, BR), :].rearrange("(j p) c -> p j c", p=P), fill[:]).then_inc(S["rows_filled"], 16)

        def stage_a(eng, step):
            step(Seq(0, 0, 0), None, Seq(1, 0, 1))
            with eng.Fori(0, (SEQS - 2) // 2) as j:
                a, b, c, d = Seq(2 * j, j, 0), Seq(2 * j + 1, j, 1), Seq(2 * j + 2, j + 1, 0), Seq(2 * j + 3, j + 1, 1)
                step(b, a, c)
                step(c, b, d)
            last = Seq(SEQS - 1, SEQS // 2 - 1, 1)
            step(last, Seq(SEQS - 2, SEQS // 2 - 1, 0), None)
            step(None, last, None)

        LAST = 3

        def b_loop(eng, b_step):
            for b in range(RING):
                b_step(b, 0, b)
            with eng.Fori(1, BLOCKS // RING - 1) as r:
                for i in range(RING):
                    b_step(r * RING + i, r, i)
            for b in range(BLOCKS - RING, BLOCKS + LAST):
                b_step(b, b // RING, b % RING)

        block = ctx.enter_context(nc.Block())

        @block.sync
        def _(sp):
            sp.dma_start(xtf[:], xt[:, 0:T]).then_inc(xt_in, 16)
            sp.dma_start(wa[:], w_att).then_inc(S["weights_in"], 16)
            sp.dma_start(ba[:], b_att).then_inc(S["weights_in"], 16)
            sp.dma_start(kc[:], consts).then_inc(S["const_in"], 16)
            sp.dma_start(rc[:], rowc).then_inc(S["const_in"], 16)
            sp.dma_start(place_c[:], places).then_inc(S["const_in"], 16)
            sp.dma_start(xres[0][:], x[0:T, :].rearrange("(i p) c -> p i c", p=P)).then_inc(xres_in[0], 16)
            sp.dma_start(proj_bias[:], b_att[0:1, B_PROJ:B_PROJ + C].broadcast_to([P, C])).then_inc(S["biases_in"], 16)
            sp.dma_start(b12c[:], b12).then_inc(S["biases_in"], 16)
            sp.wait_ge(S["zeros_ready"], 2)
            for u in range(2):
                sp.dma_start(keys[u][0:EMPTY, :], zeros[:]).then_inc(S["keys_out"], 16)
                sp.dma_start(keys4[u][0:EMPTY, :], zeros[:, 0:D]).then_inc(S["keys_out"], 16)

            def windows(n):
                sp.wait_ge(S["kq_copied"], 2 * n.n + 3)
                for to, cols in ((keys, NW), (keys4, D)):
                    sp.dma_start(to[n.u][EMPTY:EMPTY + T, :].rearrange("(i p) c -> p i c", p=P),
                                 key[n.u][:, :, 0:cols]).then_inc(S["keys_out"], 16)
                for h in range(1, WIDE):
                    a, w = PREV_AT[h], WINDOWS[h]
                    sp.dma_start(wide_b[n.u][a:a + w, :, D * h:D * h + D],
                                 wide_k[n.u][P - w:P, 0:TILES - 1, h, 0:D]).then_inc(wide_in[n.u], 16)
                sp.wait_ge(S["keys_out"], 32 * n.n + 96)
                w, w4 = OFFS * NW, OFFS * D
                sp.dma_start(kt[n.u][:, :, 0:w],
                             bass.AP(keys[n.u].tensor, (EMPTY - OFFS + 1) * NW, [[NW, P], [NW * P, TILES], [1, w]])).then_inc(keys_in[n.u], 16)
                sp.dma_start(kt[n.u][:, :, w:PK],
                             bass.AP(keys4[n.u].tensor, (EMPTY - 2 * OFFS + 1) * D, [[D, P], [D * P, TILES], [1, w4]])).then_inc(keys_in[n.u], 16)

            windows(Seq(0, 0, 0))

            def step(s, t, n):
                if n:
                    sp.wait_ge(S["x_lo"], s.n + 1)
                    sp.dma_start(xtf[:], xt[:, bass.ds(n.n * T, T)]).then_inc(xt_in, 16)
                if s:
                    if t:
                        sp.wait_ge(S["w_lo"], s.n)
                    sp.dma_start(w12f[:], w12[:, bass.ds(s.n * 2 * F, 2 * F)]).then_inc(expert_in, 16)
                if n:
                    if t:
                        sp.wait_ge(S["hid_ready"], t.n + 1)
                    sp.dma_start(xres[n.u][:], x[bass.ds(n.n * T, T), :].rearrange("(i p) c -> p i c", p=P)).then_inc(xres_in[n.u], 16)
                if t:
                    sp.wait_ge(S["rows_x"], t.n + 1)
                    sp.dma_start(x1[bass.ds(t.n * T, T), :].rearrange("(i p) c -> p i c", p=P),
                                 rowb[t.u][0][:, :, 0:C]).then_inc(x1_out[t.u], 16)
                if n:
                    windows(n)

            stage_a(sp, step)

            sp.wait_ge(S["fill_ready"], 1)
            sp.dma_start(rows[ZERO_ROW:ROWS, :].rearrange("(j p) c -> p j c", p=P), fill[:]).then_inc(S["rows_filled"], 16)
            fill_rows(sp, range(0, EXPERTS // 2))

            def start_of(b):
                return sp.value_load(t_row[0:1, bass.ds(b, 1)], min_val=0, max_val=ZERO_ROW)

            def load_block(b, i, at):
                sp.dma_start(xb[i][:], rows[bass.ds(at, BR), :].rearrange("(j p) c -> p j c", p=P)).then_inc(block_in[i], 16)

            def load_next(b, i):
                sp.wait_ge(S["x_turned"], b - RING + 1)
                sp.wait_ge(S["wd_ready"], b - RING + 1)
                load_block(b, i, start_of(b))

            sp.wait_ge(S["plan_ready"], 1)
            starts = [start_of(b) for b in range(RING)]
            sp.wait_ge(S["rows_filled"], 16 * (EXPERTS + 1))
            for u in range(2):
                sp.wait_ge(scattered[u], 16 * TOP * TILES * SEQS // 2)
            for b in range(RING):
                load_block(b, b, starts[b])
            for u in range(2):
                sp.wait_ge(x1_out[u], 16 * SEQS // 2)
            with sp.Fori(1, SEQS + 1) as r:
                for i in range(RING):
                    load_next(r * RING + i, i)
                sp.dma_start(x1c[:, bass.ds((r - 1) * TILES, TILES), :],
                             x1[bass.ds((r - 1) * T, T), :].rearrange("(i p) c -> p i c", p=P)).then_inc(S["x1_in"], 16)
            for b in range(RING * (SEQS + 1), BLOCKS):
                load_next(b, b % RING)

            for i in range(RING):
                sp.wait_ge(y_out[i], 16 * (BR // P) * (BLOCKS // RING))
            for part, (a, tiles) in enumerate(PARTS):
                at = slice(a, a + tiles)
                for k in range(TOP):
                    lo = (k * SEQS * TILES + a) * P
                    sp.dma_start(ya[k][:, at, :], res[lo:lo + tiles * P, :].rearrange("(i p) c -> p i c", p=P)).then_inc(ya_in[part], 16)
            for part, (a, tiles) in enumerate(PARTS):
                at = slice(a, a + tiles)
                sp.wait_ge(S["c_ready"], part + 1)
                sp.dma_start(out[P * a:P * (a + tiles), :].rearrange("(i p) c -> p i c", p=P), ya[1][:, at, :]).then_inc(S["c_out"], 16)
            sp.wait_ge(S["c_out"], 16 * len(PARTS))

        @block.tensor
        def _(pe):
            def three(out_ap, lh, ll, rh, rl, last_start=False, stop=True):
                pe.matmul(out_ap, lh, rh, start=last_start, stop=False, skip_group_check=True)
                pe.matmul(out_ap, lh, rl, start=False, stop=False, skip_group_check=True)
                return pe.matmul(out_ap, ll, rh, start=False, stop=stop, skip_group_check=True)

            def bias(out_ap, lhs, rhs):
                return pe.matmul(out_ap, lhs, rhs, start=True, stop=False, skip_group_check=True)

            def scores(s, i):
                pe.wait_ge(S["score_free"], WIDE * (4 * s.n + i + 1))
                for k, h in enumerate((2, 0, 1, 3)):
                    if k == WIDE - 1:
                        pe.wait_ge(S["scores"], WIDE * (4 * s.n + i) + 1)
                    r = slice(32 * h, 32 * h + 32)
                    w = WINDOWS[h] if i else 0
                    pe.matmul(score_at[h][:, WINDOWS[h] - w:], qst[r, P * i:P * i + P], kst[r, P * i - w:P * i + P],
                              start=True, stop=True, skip_group_check=True).then_inc(S["scores"], 1)

            def tokens(n, a):
                pe.wait_ge(S["kq_copied"], 2 * n.n + a + 1)
                for i in range(2):
                    t = slice(P * (2 * a + i), P * (2 * a + i) + P)
                    o = b_c[:, KQ * i:KQ * i + KQ]
                    bias(o, ones2[:, 0:P], bas[:, B_KQ:B_KQ + KQ])
                    mm = three(o, xth[:, t], xtl[:, t], wah[:, W_K:W_K + KQ], wal[:, W_K:W_K + KQ])
                mm.then_inc(S["kq_done"], 1)

            def project(n, b, wc, done):
                three(b[:], wah[:, wc:wc + P], wal[:, wc:wc + P], xth[:], xtl[:], last_start=True).then_inc(done, 1)

            def project_wide(n):
                pe.wait_ge(S["score_free"], WIDE * TILES * n.n + WIDE)
                project(n, b_kp, W_KREP, S["kproj"])
                project(n, b_qp, W_QREP, S["qproj"])

            def turn(s, i):
                pe.wait_ge(S["exps"], WIDE * (4 * s.n + i + 1))
                if i >= 1:
                    pe.wait_ge(S["joined"], 3 * s.n + i)
                if i >= 1:
                    pe.wait_ge(S["pta_out"], 4 * s.n + i + 1)
                if i >= 2:
                    pe.wait_ge(S["ptb_out"], 3 * s.n + i)
                pr = prob[i % 2]
                for h in range(WIDE):
                    mm = pe.transpose(b_k[:, P * h:P * h + P], pr[:, h, P:2 * P], ident)
                if i >= 1:
                    mm = pe.transpose(b_q[:, 0:P], pr[:, 0, 0:P], ident)
                    mm = pe.transpose(b_q[:, P:2 * P], joint[i % 2][:], ident)
                mm.then_inc(S["turned"], 1)

            def pv(s, i):
                pe.wait_ge(S["pta_out"], 4 * s.n + i + 2)
                if i == 0:
                    pe.wait_ge(S["pv_free"], s.n + 1)
                    pe.wait_ge(S["kq_copied"], 2 * s.n + 3)
                if i == 1:
                    pe.wait_ge(wide_in[s.u], 16 * (WIDE - 1) * (s.half + 1))
                if i >= 1:
                    pe.wait_ge(S["ptb_out"], 3 * s.n + i + 1)
                o = b_pv[0:WIDE * D, P * i:P * i + P]
                for h in range(WIDE):
                    mm = pe.matmul(o, head(wide_k[s.u], i, h), pta[i % 2][:, h, :],
                                   start=h == 0, stop=i == 0 and h == WIDE - 1, skip_group_check=True)
                if i >= 1:
                    pe.matmul(o, head(wide_k[s.u], i - 1, 0), ptb[i % 2][:, 0, :], start=False, stop=False,
                              skip_group_check=True)
                    mm = pe.matmul(o, wide_b[s.u][:, i - 1, :], ptb[i % 2][:, 1, :], start=False, stop=True,
                                   skip_group_check=True)
                mm.then_inc(S["pv"], 1)

            def head(weights, i, h):
                return weights[:, i].rearrange("p h c -> p (h c)")[:, 32 * h:32 * h + 32]

            def turn_pv(s):
                wait_alone(pe, S["pv_out"], s.n + 1)
                for i in range(TILES):
                    mm = pe.transpose(b_pv[:, WIDE * D * i:WIDE * D * i + WIDE * D], pvt[:, P * i:P * i + P],
                                      ident[0:WIDE * D, 0:WIDE * D])
                mm.then_inc(S["pv_turned"], 1)

            def turn_att(s):
                pe.wait_ge(S["att_ready"], s.n + 1)
                pe.wait_ge(S["tail_free"], s.n + 1)
                for i in range(TILES):
                    mm = pe.transpose(b_tail[:, P * i:P * i + P], att[:, i, :], ident)
                mm.then_inc(S["att_turned"], 1)

            def project_att(s):
                pe.wait_ge(S["att_lo"], s.n + 1)
                for i in range(TILES):
                    t = slice(P * i, P * i + P)
                    mm = three(b_tail[:, t], atth[:, t], attl[:, t], wah[:, W_PROJ:W_PROJ + C],
                               wal[:, W_PROJ:W_PROJ + C], last_start=True)
                mm.then_inc(S["projected"], 1)

            def turn_x1(s):
                pe.wait_ge(S["rows_x"], s.n + 1)
                for i in range(TILES):
                    mm = pe.transpose(b_tail[:, P * i:P * i + P], rowb[s.u][0][:, i, 0:C], ident)
                mm.then_inc(S["x1_turned"], 1)

            def logits(s):
                pe.wait_ge(S["x1_lo"], s.n + 1)
                for i in range(TILES):
                    t = slice(P * i, P * i + P)
                    o = b_tail[:, 2 * EXPERTS * i:2 * EXPERTS * (i + 1)]
                    pe.matmul(o, atth[:, t], wr[:], start=True, stop=False, skip_group_check=True)
                    mm = pe.matmul(o[:, 0:EXPERTS], attl[:, t], wr[:, 0:EXPERTS], start=False, stop=True, skip_group_check=True)
                mm.then_inc(S["logits_ready"], 1)

            def count_ranks(s):
                pe.wait_ge(S["mem_ready"], s.n + 1)
                o = b_tail[:, 64:64 + TILES * EXPERTS].rearrange("p (i e) -> p i e", e=EXPERTS)
                pe.matmul(o, tri[:], mem[:], start=True, stop=False, skip_group_check=True)
                for i in range(TILES - 1):
                    pe.matmul(o[:, i + 1:], ones_b[:], mem[:, i:i + 1, :].broadcast_to([P, TILES - 1 - i, EXPERTS]),
                              start=False, stop=False, skip_group_check=True)
                mm = pe.matmul(o, ones_b[:], mtot[s.u][:].unsqueeze(1).broadcast_to([P, TILES, EXPERTS]),
                               start=False, stop=True, skip_group_check=True)
                mm.then_inc(S["ranks"], 1)

            def first_tile(s):
                pe.wait_ge(S["kst_ready"], s.n + 1)
                pe.wait_ge(S["qst_ready"], s.n + 1)
                scores(s, 0)

            def step(s, t, n):
                if s:
                    scores(s, 1)
                    turn(s, 0)
                    scores(s, 2)
                if t:
                    turn_att(t)
                if s:
                    turn(s, 1)
                    scores(s, 3)
                    pv(s, 0)
                if n:
                    pe.wait_ge(S["x_lo"], n.n + 1)
                    tokens(n, 0)
                if t:
                    project_att(t)
                if s:
                    pv(s, 1)
                if n:
                    tokens(n, 1)
                if s:
                    turn(s, 2)
                if n:
                    project_wide(n)
                if s:
                    turn(s, 3)
                    pv(s, 2)
                if t:
                    turn_x1(t)
                if s:
                    pv(s, 3)
                if n:
                    first_tile(n)
                if t:
                    logits(t)
                if s:
                    turn_pv(s)
                if t:
                    count_ranks(t)

            prepare_carrier(pe)
            pe.wait_ge(S["weights_ready"], 1)
            pe.wait_ge(S["x_lo"], 1)
            first = Seq(0, 0, 0)
            tokens(first, 0)
            project_wide(first)
            tokens(first, 1)
            first_tile(first)
            stage_a(pe, step)

            pe.wait_ge(S["tail_free"], SEQS + 1)
            pe.matmul(b_tail[:, 0:EXPERTS], ones_b[:], mtot[0][:], start=True, stop=True).then_inc(S["totals"], 1)

            ph, px, py, pyt = psum[0:2], bank[4], bank[5:7], bank[7]
            pe.sem_inc(S["y_done"], 2)
            pe.sem_inc(S["y_turned"], 2)

            def turn_x(b, q, i):
                pe.wait_ge(block_in[i], 16 * (q + 1))
                if not (isinstance(b, int) and b == 0):
                    pe.wait_ge(S["xb_lo"], b)
                for j in range(BR // P):
                    mm = pe.transpose(px[:, P * j:P * j + P], xb[i][:, j, 0:C], ident)
                mm.then_inc(S["x_turned"], 1)

            def first_product(b, i):
                pe.wait_ge(S["w1_ready"], b + 1)
                pe.wait_ge(S["xb_lo"], b + 1)
                pe.wait_ge(S["g_ready"], b + 1)
                for c in range(FC):
                    w = w1s[i % 2][:, :, P * c:P * c + P]
                    mm = three(ph[i % 2][:, BR * c:BR * c + BR], w[:, 0], w[:, 1],
                               xbh[i % 2][:], xbl[i % 2][:], last_start=True)
                mm.then_inc(S["h_ready"], 1)

            def second_product(b, i):
                pe.wait_ge(S["w2_ready"], b + 1)
                pe.wait_ge(S["g_lo"], b + 3)
                pe.wait_ge(S["y_copied"], b + 1)
                for c in range(FC):
                    w, r = w2s[i % 2][:, :, C * c:C * c + C], slice(BR * c, BR * c + BR)
                    mm = three(py[i % 2][:, 0:BR], w[:, 0], w[:, 1], gh[i % 2][:, r], gl[i % 2][:, r],
                               last_start=c == 0, stop=c == FC - 1)
                mm.then_inc(S["y_done"], 1)

            def turn_y(b, i):
                pe.wait_ge(S["y_copied"], b + 3)
                pe.wait_ge(S["y_ready"], b + 1)
                for j in range(BR // P):
                    mm = pe.transpose(pyt[:, C * j:C * j + C], yt[i % 2][:, P * j:P * j + P], ident)
                mm.then_inc(S["y_turned"], 1)

            def b_step(b, q, i):
                static = isinstance(b, int)
                if not static or b + 1 < BLOCKS:
                    turn_x(b + 1, q + (i + 1) // RING, (i + 1) % RING)
                if not static or b < BLOCKS:
                    first_product(b, i)
                if not static or b >= 3:
                    turn_y(b - 3, i - 3)
                if not static or 2 <= b < BLOCKS + 2:
                    second_product(b - 2, i - 2)

            pe.wait_ge(S["w_lo"], SEQS)
            pe.wait_ge(S["plan_ready"], 1)
            turn_x(0, 0, 0)
            b_loop(pe, b_step)

        @block.scalar
        def _(act):
            act.sem_inc(S["kq_copied"], 1)
            act.sem_inc(S["pta_out"], 1)
            act.sem_inc(S["ptb_out"], 1)
            act.sem_inc(S["g_ready"], 2)
            act.sem_inc(S["y_copied"], 2)
            act.wait_ge(S["weights_in"], 32)
            act.copy(wah[:], wa[:]).then_inc(S["w_hi"], 1)
            act.copy(wr[:, 0:EXPERTS], wa[:, W_R:W_R + EXPERTS])
            act.copy(bah[:], ba[:]).then_inc(S["w_hi"], 1)

            def split_x(n):
                act.wait_ge(xt_in, 16 * (n.n + 1))
                if not (isinstance(n.n, int) and n.n == 0):
                    act.wait_ge(S["qproj"], n.n)
                act.copy(xth[:], xtf[:]).then_inc(S["x_hi"], 1)

            def copy_tokens(n, a):
                act.wait_ge(S["kq_done"], 2 * n.n + a + 1)
                both = b_c[:, 0:2 * KQ].rearrange("p (i c) -> p i c", i=2)
                act.copy(wide_k[n.u][:, 2 * a:2 * a + 2, :, 0:D], both[:, :, 0:WIDE * D].rearrange("p i (h d) -> p i h d", d=D))
                act.copy(key[n.u][:, 2 * a:2 * a + 2, :], both[:, :, WIDE * D:C])
                act.copy(qg[n.u][:, 2 * a:2 * a + 2, :], both[:, :, C:KQ]).then_inc(S["kq_copied"], 1)

            def keys_hi(n):
                act.wait_ge(S["kproj"], n.n + 1)
                act.activation(hi_k[:], b_kp[:], ACT.Identity, bias=less_bias[:, 0:1], scale=kc[:, K_NK:K_NK + 1]).then_inc(S["khi"], 1)

            def queries_hi(n):
                act.wait_ge(S["qproj"], n.n + 1)
                act.activation(hi_q[:], b_qp[:], ACT.Identity, bias=less_bias[:, 1:2], scale=kc[:, K_NQ:K_NQ + 1]).then_inc(S["qhi"], 1)

            split_x(Seq(0, 0, 0))

            def wide_exp(s, i):
                act.wait_ge(S["ntop_ready"], 4 * s.n + i + 1)
                for k, h in enumerate((1, 2, 3, 0)):
                    w = WINDOWS[h] if i else 0
                    act.activation(prob[i % 2][:, h, P - w:2 * P],
                                   scored[i % 2][:, KEY_AT[h] + WINDOWS[h] - w:KEY_AT[h] + KEYS[h]], ACT.Exp,
                                   bias=ntop[:, i % 2, h:h + 1], scale=SCALE,
                                   accum_out=sums[s.u][:, i, h:h + 1]).then_inc(S["exps"], 1)
                if i:
                    act.wait_ge(S["exps"], WIDE * (4 * s.n + i) + WIDE - 1)
                    for h in range(1, WIDE):
                        w = WINDOWS[h]
                        a = act.copy(joint[i % 2][:, PREV_AT[h]:PREV_AT[h] + w], prob[i % 2][:, h, P - w:P])
                    a.then_inc(S["joined"], 1)

            def copy_turned(s, i):
                act.wait_ge(S["turned"], 4 * s.n + i + 1)
                act.copy(pta[i % 2][:].rearrange("p h q -> p (h q)"), b_k[:]).then_inc(S["pta_out"], 1)
                if i >= 1:
                    act.copy(ptb[i % 2][:].rearrange("p h q -> p (h q)"), b_q[:, 0:2 * P]).then_inc(S["ptb_out"], 1)

            def att_hi(t):
                act.wait_ge(S["att_turned"], t.n + 1)
                act.copy(atth[:], b_tail[:]).then_inc(S["att_hi"], 1)

            def x1_hi(t):
                act.wait_ge(S["x1_turned"], t.n + 1)
                act.copy(atth[:], b_tail[:]).then_inc(S["x1_hi"], 1)

            def second_weight(t):
                act.wait_ge(S["diff_ready"], t.n + 1)
                act.activation(edif[:], diff[:], ACT.Exp).then_inc(S["edif_ready"], 1)

            def narrow_exp(s):
                act.wait_ge(S["sc_ready"], s.n + 1)
                act.activation(ex[:].rearrange("p i c -> p (i c)"), scd[:].rearrange("p i c -> p (i c)"), ACT.Exp, scale=SCALE)
                act.activation(ge[:].rearrange("p i c -> p (i c)"), gd[:].rearrange("p i c -> p (i c)"), ACT.Exp).then_inc(S["ex_ready"], 1)

            def second_rows(t):
                act.wait_ge(S["rows_free"], t.n + 1)
                act.copy(rowb[t.u][1][:, :, 0:C], rowb[t.u][0][:, :, 0:C]).then_inc(S["x1_kept"], 1)

            def step(s, t, n):
                if n:
                    split_x(n)
                if s:
                    wide_exp(s, 1)
                    copy_turned(s, 0)
                if t:
                    att_hi(t)
                if s:
                    wide_exp(s, 2)
                    copy_turned(s, 1)
                    wide_exp(s, 3)
                if n:
                    copy_tokens(n, 0)
                if s:
                    copy_turned(s, 2)
                if n:
                    keys_hi(n)
                    queries_hi(n)
                    copy_tokens(n, 1)
                if s:
                    copy_turned(s, 3)
                    narrow_exp(s)
                if t:
                    x1_hi(t)
                if n:
                    wide_exp(n, 0)
                if s:
                    act.wait_ge(S["pv"], 4 * s.n + 4)
                    act.copy(pvt[:], b_pv[0:WIDE * D, :]).then_inc(S["pv_out"], 1)
                if t:
                    second_weight(t)
                    second_rows(t)
                if s:
                    act.wait_ge(expert_in, 16 * (s.n + 1))
                    act.copy(w12s[:, bass.ds(s.n, 1), :, 0, :], w12f[:].rearrange("p (a k f) -> p a k f", a=1, k=2)).then_inc(S["w_hi"], 1)

            act.wait_ge(S["weights_ready"], 1)
            first = Seq(0, 0, 0)
            copy_tokens(first, 0)
            keys_hi(first)
            copy_tokens(first, 1)
            queries_hi(first)
            wide_exp(first, 0)
            stage_a(act, step)

            ph, px, py = psum[0:2], bank[4], bank[5:7]
            fill_rows(act, range(EXPERTS // 2, EXPERTS))
            act.wait_ge(S["biases_in"], 32)
            act.activation(table[:], b12c[:, 0:1], ACT.Gelu)

            def expert_of(b):
                return act.value_load(t_exp[0:1, bass.ds(b, 1)], min_val=0, max_val=EXPERTS - 1)

            def x_hi(b, i):
                act.wait_ge(S["x_turned"], b + 1)
                act.copy(xbh[i % 2][:], px[:, 0:BR]).then_inc(S["xb_hi"], 1)

            def gelu(b, i):
                e = expert_of(b)
                act.wait_ge(S["h_ready"], b + 1)
                act.wait_ge(S["g_lo"], b + 1)
                for c in range(FC):
                    r = slice(BR * c, BR * c + BR)
                    a = act.activation(g[i % 2][:, r], ph[i % 2][:, r], ACT.Gelu,
                                       bias=b12c[:, bass.ds(e * (FC + 1) + c, 1)])
                a.then_inc(S["g_ready"], 1)

            def g_hi(b, i):
                act.wait_ge(S["g_ready"], b + 3)
                act.wait_ge(S["y_done"], b + 1)
                act.copy(gh[i % 2][:], g[i % 2][:]).then_inc(S["g_hi"], 1)

            def y_copy(b, i):
                e = expert_of(b)
                act.wait_ge(S["y_done"], b + 3)
                act.wait_ge(S["y_turned"], b + 1)
                act.activation(yt[i % 2][:], py[i % 2][:, 0:BR], ACT.Identity,
                               bias=b12c[:, bass.ds(e * (FC + 1) + FC, 1)]).then_inc(S["y_copied"], 1)

            def b_step(b, q, i):
                static = isinstance(b, int)
                if not static or b >= 3:
                    y_copy(b - 3, i - 3)
                if not static or b + 1 < BLOCKS:
                    x_hi(b + 1, i + 1)
                if not static or 1 <= b <= BLOCKS:
                    g_hi(b - 1, i - 1)
                if not static or b < BLOCKS:
                    gelu(b, i)

            x_hi(0, 0)
            b_loop(act, b_step)

            for part, (at, tiles) in enumerate(PARTS):
                act.wait_ge(S["c_scale"], part + 1)
                for k in range(tiles):
                    a = act.activation(ya[1][:, at + k, :], x1c[:, at + k, :], ACT.Identity,
                                       bias=cbias[part % 2][:, k:k + 1], scale=crstd[part % 2][:, k:k + 1])
                a.then_inc(S["c_ready"], 1)

        @block.gpsimd
        def _(pool):
            prepare_carrier(pool)
            pool.memset(zeros[:], 0.0).then_inc(S["zeros_ready"], 1)
            pool.memset(fill[:], 0.0).then_inc(S["pool_a"], 1)
            pool.wait_ge(S["pool_a"], 1)
            pool.memset(fill[:, :, C + 1:C + 2].bitcast(I32), NOWHERE).then_inc(S["fill_ready"], 1)
            pool.sem_inc(S["rows_free"], 2)

            def add_bias(s):
                pool.wait_ge(xres_in[s.u], 16 * (s.half + 1))
                pool.tensor_tensor(xres[s.u][:], xres[s.u][:], proj_bias[:].unsqueeze(1).broadcast_to([P, TILES, C]),
                                   ALU.add).then_inc(S["xres_ready"], 1)

            def expert_lo(s):
                pool.wait_ge(S["w_hi"], s.n + 3)
                e = bass.ds(s.n, 1)
                pool.tensor_tensor(w12s[:, e, :, 1, :], w12f[:].rearrange("p (a k f) -> p a k f", a=1, k=2),
                                  w12s[:, e, :, 0, :].bitcast(F32), ALU.subtract).then_inc(S["w_lo"], 1)

            def products(s):
                pool.wait_ge(keys_in[s.u], 32 * (s.half + 1))
                for i in range(TILES):
                    k, q = kt[s.u][:, i, :], qg[s.u][:, i, 0:NW]
                    pool.tensor_tensor(prod[:, i, 0:OFFS * NW].rearrange("p (o c) -> p o c", o=OFFS),
                                       k[:, 0:OFFS * NW].rearrange("p (o c) -> p o c", o=OFFS),
                                       q.unsqueeze(1).broadcast_to([P, OFFS, NW]), ALU.mult)
                    pool.tensor_tensor(prod[:, i, OFFS * NW:PK].rearrange("p (o c) -> p o c", o=OFFS),
                                       k[:, OFFS * NW:PK].rearrange("p (o c) -> p o c", o=OFFS),
                                       q[:, 0:D].unsqueeze(1).broadcast_to([P, OFFS, D]), ALU.mult).then_inc(S["prod_ready"], 1)

            def step(s, t, n):
                if s:
                    pool.wait_ge(S["ex_ready"], s.n + 1)
                    for i in range(TILES):
                        k = kt[s.u][:, i, :].rearrange("p (c d) -> p c d", d=D)
                        pool.tensor_tensor(k, k, ex[:, i, :].unsqueeze(2).broadcast_to([P, PAIRS, D]),
                                           ALU.mult).then_inc(S["pk_ready"], 1)
                if n:
                    products(n)
                    add_bias(n)
                if t:
                    wait_alone(pool, S["slots_ready"], t.n + 1)
                    for i in range(TILES):
                        for k in range(TOP):
                            pool.indirect_dma_start(rows, bass.IndirectOffsetOnAxis(ap=slot[t.u][:, i, k:k + 1], axis=0),
                                                    rowb[t.u][k][:, i, :], None, bounds_check=ZERO_ROW - 1,
                                                    oob_is_err=False).then_inc(scattered[t.u], 16)
                if s:
                    expert_lo(s)

            def step_and_free(s, t, n):
                if t and not (isinstance(t.n, int) and t.n == 0):
                    half = t.half if t.u else t.half - 1
                    pool.wait_ge(scattered[1 - t.u], 16 * TOP * TILES * (half + 1))
                    pool.wait_ge(x1_out[1 - t.u], 16 * (half + 1))
                    pool.sem_inc(S["rows_free"], 1)
                step(s, t, n)

            pool.wait_ge(S["biases_in"], 32)
            products(Seq(0, 0, 0))
            add_bias(Seq(0, 0, 0))
            stage_a(pool, step_and_free)

            def scatter(b, q, i):
                wait_alone(pool, S["y_ready"], b + 2)
                for j in range(BR // P):
                    pool.indirect_dma_start(res, bass.IndirectOffsetOnAxis(ap=wd[i][:, j, 1:2].bitcast(I32), axis=0),
                                            yb[i][:, j, :], None, bounds_check=PLACES - 1,
                                            oob_is_err=False).then_inc(y_out[i], 16)

            with pool.Fori(0, BLOCKS // RING) as r:
                for i in range(RING):
                    scatter(r * RING + i, r, i)

            pool.wait_ge(S["x1_in"], 16 * SEQS)
            for part, (a, tiles) in enumerate(PARTS):
                at = slice(a, a + tiles)
                pool.wait_ge(ya_in[part], 16 * TOP)
                pool.tensor_tensor(ya[0][:, at, :], ya[0][:, at, :], ya[1][:, at, :], ALU.add).then_inc(S["summed"], 1)
                pool.wait_ge(S["summed"], part + 1)
                pool.tensor_tensor(x1c[:, at, :], x1c[:, at, :], ya[0][:, at, :], ALU.add).then_inc(S["added"], 1)

        @block.vector
        def _(dve):
            prepare_carrier(dve)
            dve.sem_inc(S["score_free"], WIDE)
            dve.sem_inc(S["pv_free"], 1)
            dve.sem_inc(S["tail_free"], 1)
            dve.sem_inc(S["g_lo"], 2)
            dve.sem_inc(S["y_ready"], 1)
            for u in range(2):
                dve.memset(prob[u][:], 0.0)
                dve.memset(joint[u][:], 0.0)
                dve.memset(wide_k[u][:], 0.0)
                ins = dve.memset(wide_b[u][:], 0.0)
            ins.then_inc(S["zeros_ready"], 1)
            dve.memset(mtot[0][:], 0.0)
            dve.memset(ones_b[:], 1.0)
            dve.memset(ones2[:].bitcast(F32), 1.0)
            dve.wait_ge(S["const_in"], 48)
            dve.tensor_copy(tri[:], kc[:, K_TRI:K_TRI + P])
            dve.wait_ge(S["w_hi"], 2)
            dve.tensor_tensor(wal[:], wa[:], wah[:].bitcast(F32), ALU.subtract)
            dve.tensor_copy(wide_bias[:], wa[:, W_BK:W_COLS])
            dve.tensor_tensor(less_bias[:], wa[:, W_BK:W_COLS], kc[:, K_NK:K_NK + 2], ALU.mult)
            dve.tensor_tensor(wr[:, EXPERTS:], wa[:, W_R:W_R + EXPERTS], wr[:, 0:EXPERTS].bitcast(F32), ALU.subtract)
            dve.scalar_tensor_tensor(bas[:], bah[:].bitcast(F32), kc[0:2, K_NB:K_NB + 1], ba[:],
                                     ALU.mult, ALU.add).then_inc(S["weights_ready"], 1)

            def x_lo(n):
                dve.wait_ge(S["x_hi"], n.n + 1)
                dve.tensor_tensor(xtl[:], xtf[:], xth[:].bitcast(F32), ALU.subtract).then_inc(S["x_lo"], 1)

            x_lo(Seq(0, 0, 0))
            own = Chain(dve, S["dve_a"], 20)
            n4 = OFFS * NARROW
            mix = Chain(dve, S["dve_m"], 2)
            tail = Chain(dve, S["dve_t"], 27)

            def newton(chain, v, nwt, i):
                y, a, b, y2 = nwt[3 * i:3 * i + 4]
                chain.wait()
                chain.mark(dve.tensor_tensor(a[:], y[:], y[:], ALU.mult))
                chain.wait()
                chain.mark(dve.scalar_tensor_tensor(b[:], a[:], -0.5, v[:], ALU.mult, ALU.mult))
                chain.wait()
                chain.mark(dve.scalar_tensor_tensor(y2[:], b[:], 1.5, y[:], ALU.add, ALU.mult))

            def variances(chain, h, stat, mv):
                tiles = h.shape[1]
                for i in range(tiles):
                    ins = dve.bn_stats(stat[:, i, :], h[:, i, :])
                chain.mark(ins)
                wait_alone(dve, chain.sem, chain.value())
                for i in range(tiles):
                    ins = dve.bn_aggr(mv[:, i, :], stat[:, i, :])
                chain.mark(ins)

            def guess(chain, mv, va, nwt):
                chain.wait()
                chain.mark(dve.tensor_scalar(va[:], mv[:, :, 1], EPS, None, ALU.add))
                chain.wait()
                chain.mark(dve.tensor_scalar(nwt[0][:].bitcast(I32), va[:].bitcast(I32), -0.5, 1597463007.0, ALU.mult, ALU.add))

            def statistics(chain, h, stat, mv, va, nwt):
                variances(chain, h, stat, mv)
                guess(chain, mv, va, nwt)
                for i in range(3):
                    newton(chain, va, nwt, i)
                chain.wait()
                return nwt[9]

            def window(s, i):
                for h in range(WIDE):
                    wait_alone(dve, S["scores"], WIDE * (4 * s.n + i) + (h + 2 if h < 2 else WIDE))
                    if i >= 2 and h == 0:
                        dve.wait_ge(S["exps"], WIDE * (4 * s.n + i - 1))
                    a = WINDOWS[h] if i == 0 else 0
                    dve.tensor_tensor_reduce(
                        scored[i % 2][:, KEY_AT[h] + a:KEY_AT[h] + KEYS[h]], score_at[h][:, a:],
                        kc[:, K_MN + KEY_AT[h] + a:K_MN + KEY_AT[h] + KEYS[h]], 1.0, LOW, ALU.add, ALU.max,
                        top[:, i % 2, h:h + 1]).then_inc(S["score_free"], 1)
                dve.wait_ge(S["score_free"], 4 * (4 * s.n + i) + 2 * WIDE)
                dve.tensor_scalar(ntop[:, i % 2, :], top[:, i % 2, :], -SCALE, None, ALU.mult).then_inc(S["ntop_ready"], 1)

            def narrow_scores(s, i):
                dve.wait_ge(S["prod_ready"], 4 * s.n + i + 1)
                own.mark(dve.tensor_reduce(sc[:, i, :], prod[:, i, :].rearrange("p (c d) -> p c d", d=D), X_AXIS, ALU.add))

            def att_lo(t):
                dve.wait_ge(S["att_hi"], t.n + 1)
                dve.tensor_tensor(attl[:], b_tail[:], atth[:].bitcast(F32), ALU.subtract).then_inc(S["att_lo"], 1)

            def x1_lo(t):
                dve.wait_ge(S["x1_hi"], t.n + 1)
                dve.tensor_tensor(attl[:], b_tail[:], atth[:].bitcast(F32), ALU.subtract).then_inc(S["x1_lo"], 1)

            def residual(t):
                u = t.u
                dve.wait_ge(S["projected"], t.n + 1)
                dve.wait_ge(S["xres_ready"], t.n + 1)
                dve.tensor_tensor(hid[:].rearrange("p i c -> p (i c)"), b_tail[:],
                                  xres[u][:].rearrange("p i c -> p (i c)"), ALU.add).then_inc(S["hid_ready"], 1)
                dve.wait_ge(S["hid_ready"], t.n + 1)
                variances(tail, hid, stat, mv)

            def first_norm(t):
                u = t.u
                tail.wait()
                dve.wait_ge(S["rows_free"], t.n + 1)
                for k in range(TILES):
                    ins = dve.tensor_scalar(rowb[u][0][:, k, 0:C], hid[:, k, :], mv[:, k, 0:1], nwt[9][:, k:k + 1],
                                            ALU.subtract, ALU.mult)
                ins.then_inc(S["rows_x"], 1)
                for k in range(TOP):
                    ins = dve.tensor_copy(rowb[u][k][:, :, C + 1:C + 2].bitcast(I32),
                                          place_c[:, bass.ds(4 * t.n + k * SEQS * TILES, TILES)].unsqueeze(2))
                tail.mark(ins)

            def router_logits(t):
                dve.wait_ge(S["logits_ready"], t.n + 1)
                both = b_tail[:, 0:TILES * 2 * EXPERTS].rearrange("p (i k e) -> p i e k", k=2, e=EXPERTS)
                tail.mark(dve.tensor_reduce(logit[:], both, X_AXIS, ALU.add))

            def router_best(t):
                wait_alone(dve, tail.sem, tail.value())
                for k in range(TILES):
                    ins = dve.max(best[:, k, :], logit[:, k, :])
                tail.mark(ins)

            def router_experts(t):
                wait_alone(dve, tail.sem, tail.value())
                for k in range(TILES):
                    ins = dve.max_index(ibest[:, k, :], best[:, k, :], logit[:, k, :])
                tail.mark(ins)
                dve.tensor_tensor(diff[:], best[:, :, 1], best[:, :, 0], ALU.subtract).then_inc(S["diff_ready"], 1)

            def router_numbers(t):
                tail.wait()
                tail.mark(dve.tensor_copy(ibf[:], ibest[:]))

            def router_one_hot(t):
                tail.wait()
                tail.mark(dve.tensor_tensor(oh[:], ibf[:, :, 0:TOP].unsqueeze(3).broadcast_to([P, TILES, TOP, EXPERTS]),
                                            kc[:, K_I8:K_I8 + EXPERTS].unsqueeze(1).unsqueeze(1).broadcast_to([P, TILES, TOP, EXPERTS]),
                                            ALU.is_equal))

            def router_members(t):
                tail.wait()
                dve.tensor_tensor(mem[:], oh[:, :, 0, :], oh[:, :, 1, :], ALU.add).then_inc(S["mem_ready"], 1)

            def weights_sum(t):
                dve.wait_ge(S["edif_ready"], t.n + 1)
                tail.mark(dve.tensor_scalar(edif1[:], edif[:], 1.0, None, ALU.add))

            def weights_first(t):
                dve.wait_ge(S["mem_ready"], t.n + 1)
                tail.mark(dve.tensor_reduce(memf[:], mem[:].rearrange("p i e -> p e i"), X_AXIS, ALU.add))
                tail.wait()
                tail.mark(dve.reciprocal(wtop[:], edif1[:]))
                tail.mark(dve.tensor_tensor(mtot[1 - t.u][:], mtot[t.u][:], memf[:], ALU.add))

            def weights_both(t):
                u = t.u
                tail.wait()
                tail.mark(dve.tensor_copy(rowb[u][0][:, :, C:C + 1], wtop[:].unsqueeze(2)))
                tail.mark(dve.tensor_tensor(rowb[u][1][:, :, C:C + 1], wtop[:].unsqueeze(2), edif[:].unsqueeze(2), ALU.mult))

            def slots(t):
                u = t.u
                dve.wait_ge(S["ranks"], t.n + 1)
                dve.tensor_tensor(rank[:], b_tail[:, 64:64 + TILES * EXPERTS].rearrange("p (i e) -> p i e", e=EXPERTS),
                                  kc[:, K_EC:K_EC + EXPERTS].unsqueeze(1).broadcast_to([P, TILES, EXPERTS]),
                                  ALU.add).then_inc(S["tail_free"], 1)
                dve.wait_ge(S["tail_free"], t.n + 2)
                tail.mark(dve.tensor_tensor(pick[:], oh[:], rank[:].unsqueeze(2).broadcast_to([P, TILES, TOP, EXPERTS]), ALU.mult))
                tail.wait()
                dve.wait_ge(S["x1_kept"], t.n + 1)
                tail.mark(dve.tensor_reduce(slotf[:], pick[:], X_AXIS, ALU.add))
                tail.wait()
                dve.tensor_copy(slot[u][:], slotf[:]).then_inc(S["slots_ready"], 1)

            def stacks(n):
                dve.wait_ge(S["khi"], n.n + 1)
                dve.scalar_tensor_tensor(kst[:], b_kp[:], wide_bias[:, 0:1], hi_k[:].bitcast(F32),
                                         ALU.add, ALU.add).then_inc(S["kst_ready"], 1)
                dve.wait_ge(S["qhi"], n.n + 1)
                dve.scalar_tensor_tensor(qst[:], b_qp[:], wide_bias[:, 1:2], hi_q[:].bitcast(F32),
                                         ALU.add, ALU.add).then_inc(S["qst_ready"], 1)

            def combine(t):
                mix.round(t.n)
                dve.wait_ge(S["pk_ready"], 4 * t.n + 4)
                dve.tensor_reduce(raw[:], kt[t.u][:, :, 0:OFFS * NW].rearrange("p i (o c) -> p i c o", o=OFFS), X_AXIS, ALU.add)
                mix.mark(dve.tensor_reduce(raw4[:], kt[t.u][:, :, OFFS * NW:PK].rearrange("p i (o c) -> p i c o", o=OFFS), X_AXIS, ALU.add))
                mix.wait()
                ins = dve.tensor_tensor(raw5[:], raw4[:], raw[:, :, 0:D], ALU.add)
                mix.mark(ins)
                mix.wait()
                dve.tensor_tensor(att[:, :, WIDE * D + D:C].rearrange("p i (h d) -> p i h d", d=D),
                                  raw[:, :, D:NW].rearrange("p i (h d) -> p i h d", d=D),
                                  gn[:, :, WIDE + 1:HEADS].unsqueeze(3).broadcast_to([P, TILES, NARROW - 1, D]), ALU.mult)
                dve.tensor_tensor(att[:, :, WIDE * D:WIDE * D + D], raw5[:],
                                  gn[:, :, WIDE:WIDE + 1].broadcast_to([P, TILES, D]), ALU.mult)
                dve.wait_ge(S["pv_turned"], t.n + 1)
                dve.tensor_tensor(att[:, :, 0:WIDE * D].rearrange("p i (h d) -> p i h d", d=D),
                                  b_pv[:, 0:TILES * WIDE * D].rearrange("p (i h d) -> p i h d", i=TILES, d=D),
                                  gn[:, :, 0:WIDE].unsqueeze(3).broadcast_to([P, TILES, WIDE, D]), ALU.mult).then_inc(S["att_ready"], 1)
                dve.wait_ge(S["att_ready"], t.n + 1)
                dve.sem_inc(S["pv_free"], 1)

            def narrow_mask(s):
                own.wait()
                own.mark(dve.tensor_tensor(sc[:, 0, :], sc[:, 0, :], kc[:, K_SM:K_SM + PAIRS], ALU.add))
                own.mark(dve.tensor_reduce(gmax[:], qg[s.u][:, :, NW:QG], X_AXIS, ALU.max))

            def narrow_max(s):
                own.wait()
                by_head = sc[:, :, 0:n4].rearrange("p i (o h) -> p i h o", o=OFFS)
                own.mark(dve.tensor_reduce(nmax[:], by_head, X_AXIS, ALU.max))
                own.mark(dve.tensor_reduce(nmax2[:], sc[:, :, n4:PAIRS], X_AXIS, ALU.max))
                own.mark(dve.tensor_tensor(gd[:], qg[s.u][:, :, NW:QG], gmax[:].unsqueeze(2).broadcast_to([P, TILES, HEADS]), ALU.subtract))

            def narrow_max4(s):
                own.wait()
                own.mark(dve.tensor_tensor(nmax3[:], nmax2[:], nmax[:, :, 0], ALU.max))

            def narrow_less4(s):
                own.wait()
                own.mark(dve.tensor_copy(nmax[:, :, 0], nmax3[:]))
                own.mark(dve.tensor_tensor(scd[:, :, n4:PAIRS], sc[:, :, n4:PAIRS],
                                           nmax3[:].unsqueeze(2).broadcast_to([P, TILES, OFFS]), ALU.subtract))

            def narrow_less(s):
                own.wait()
                for i in range(TILES):
                    ins = dve.tensor_tensor(scd[:, i, 0:n4].rearrange("p (o h) -> p o h", o=OFFS),
                                            sc[:, i, 0:n4].rearrange("p (o h) -> p o h", o=OFFS),
                                            nmax[:, i, :].unsqueeze(1).broadcast_to([P, OFFS, NARROW]), ALU.subtract)
                ins.then_inc(S["sc_ready"], 1)

            def sums_narrow(s):
                dve.wait_ge(S["ex_ready"], s.n + 1)
                own.mark(dve.tensor_reduce(sums[s.u][:, :, WIDE:HEADS], ex[:, :, 0:n4].rearrange("p i (o h) -> p i h o", o=OFFS), X_AXIS, ALU.add))
                own.mark(dve.tensor_reduce(xsum[:], ex[:, :, n4:PAIRS], X_AXIS, ALU.add))
                own.mark(dve.tensor_reduce(gsum[:], ge[:], X_AXIS, ALU.add))

            def sums_4(s):
                own.wait()
                own.mark(dve.tensor_tensor(xsum2[:], xsum[:], sums[s.u][:, :, WIDE], ALU.add))

            def sums_4_kept(s):
                own.wait()
                own.mark(dve.tensor_copy(sums[s.u][:, :, WIDE], xsum2[:]))

            def sums_gated(s):
                own.wait()
                dve.wait_ge(S["exps"], WIDE * (4 * s.n + 4))
                own.mark(dve.tensor_tensor(den[:], sums[s.u][:], gsum[:].unsqueeze(2).broadcast_to([P, TILES, HEADS]), ALU.mult))

            def sums_turned_over(s):
                own.wait()
                own.mark(dve.reciprocal(rden[:], den[:]))

            def gates(s):
                own.wait()
                own.mark(dve.tensor_tensor(gn[:], ge[:], rden[:], ALU.mult))

            def step(s, t, n):
                if s:
                    own.round(s.n)
                    window(s, 1)
                if t:
                    tail.round(t.n)
                    combine(t)
                if s:
                    window(s, 2)
                if n:
                    x_lo(n)
                if s:
                    narrow_scores(s, 0)
                    narrow_scores(s, 1)
                if t:
                    att_lo(t)
                if s:
                    window(s, 3)
                    narrow_scores(s, 2)
                    narrow_scores(s, 3)
                    narrow_mask(s)
                if t:
                    residual(t)
                if s:
                    narrow_max(s)
                if t:
                    guess(tail, mv, va, nwt)
                if s:
                    narrow_max4(s)
                if t:
                    newton(tail, va, nwt, 0)
                if s:
                    narrow_less4(s)
                if t:
                    newton(tail, va, nwt, 1)
                if s:
                    narrow_less(s)
                if t:
                    newton(tail, va, nwt, 2)
                    first_norm(t)
                if n:
                    stacks(n)
                if t:
                    x1_lo(t)
                if n:
                    window(n, 0)
                if s:
                    sums_narrow(s)
                if t:
                    router_logits(t)
                if s:
                    sums_4(s)
                if t:
                    router_best(t)
                if s:
                    sums_4_kept(s)
                if t:
                    router_experts(t)
                if s:
                    sums_gated(s)
                if t:
                    router_numbers(t)
                if s:
                    sums_turned_over(s)
                if t:
                    router_one_hot(t)
                if s:
                    gates(s)
                if t:
                    router_members(t)
                    weights_sum(t)
                    weights_first(t)
                if t:
                    weights_both(t)
                    slots(t)

            stacks(Seq(0, 0, 0))
            window(Seq(0, 0, 0), 0)
            stage_a(dve, step)

            plan = Chain(dve, S["setup_dve"], 0)
            n = EXPERTS
            dve.wait_ge(S["totals"], 1)
            dve.wait_ge(S["w_lo"], SEQS)
            row = lambda a, k: rc[0:1, a:a + k]

            def then(ins):
                plan.mark(ins)
                plan.wait()

            then(dve.tensor_copy(cnt[:], b_tail[0:1, 0:n]))
            dve.tensor_tensor(t_fill[:], cnt[:], row(R_EB, n), ALU.add).then_inc(S["fill_at_ready"], 1)
            then(dve.tensor_tensor(cmp32[:], cnt[:].unsqueeze(2).broadcast_to([1, n, MOST]),
                                   row(R_M, MOST).unsqueeze(1).broadcast_to([1, n, MOST]), ALU.is_gt))
            then(dve.tensor_reduce(nblk[:], cmp32[:], X_AXIS, ALU.add))
            then(dve.tensor_tensor(cum3[:], nblk[:].unsqueeze(1).broadcast_to([1, n, n]),
                                   row(R_TRI, n * n).rearrange("p (a b) -> p a b", b=n), ALU.mult))
            then(dve.tensor_reduce(cend[:], cum3[:], X_AXIS, ALU.add))
            then(dve.tensor_tensor(shift[:], nblk[:], cend[:], ALU.subtract))
            then(dve.scalar_tensor_tensor(shift2[:], row(R_EB, n), 1.0 / BR, shift[:], ALU.mult, ALU.add))
            table = [1, BLOCKS, n]
            then(dve.tensor_tensor(bge[:], row(R_B, BLOCKS).unsqueeze(2).broadcast_to(table),
                                   cend[:].unsqueeze(1).broadcast_to(table), ALU.is_ge))
            then(dve.tensor_reduce(bexp[:], bge[:], X_AXIS, ALU.add))
            then(dve.tensor_tensor(boh[:], bexp[:].unsqueeze(2).broadcast_to(table),
                                   row(R_E, n).unsqueeze(1).broadcast_to(table), ALU.is_equal))
            then(dve.tensor_tensor(boh2[:], boh[:], shift2[:].unsqueeze(1).broadcast_to(table), ALU.mult))
            then(dve.tensor_reduce(bsh[:], boh2[:], X_AXIS, ALU.add))
            then(dve.tensor_tensor(brow[:], bsh[:], row(R_B, BLOCKS), ALU.add))
            then(dve.tensor_scalar(bun[:], bexp[:], float(n), None, ALU.is_ge))
            then(dve.tensor_scalar(bun2[:], brow[:], -1.0, float(ZERO_ROW // BR), ALU.mult, ALU.add))
            then(dve.tensor_tensor(bun3[:], bun2[:], bun[:], ALU.mult))
            then(dve.tensor_tensor(brow2[:], brow[:], bun3[:], ALU.add))
            then(dve.tensor_scalar(t_row[:], brow2[:], float(BR), None, ALU.mult))
            dve.tensor_scalar(t_exp[:], bexp[:], float(n - 1), None, ALU.min).then_inc(S["plan_ready"], 1)

            px, pyt = bank[4], bank[7]

            def take_weights(e, b, i, product, kept, ready):
                done = S["h_ready"] if product == 0 else S["y_done"]
                if not isinstance(b, int) or b >= 2:
                    dve.wait_ge(done, b - 1 + 2 * product)
                dve.tensor_copy(kept[i % 2][:].unsqueeze(1), w12s[:, bass.ds(e, 1), product, :, :]).then_inc(ready, 1)

            def x_part(b, q, i):
                dve.wait_ge(S["xb_hi"], b + 1)
                dve.tensor_tensor(xbl[i % 2][:], px[:, 0:BR], xbh[i % 2][:].bitcast(F32), ALU.subtract).then_inc(S["xb_lo"], 1)

            def expert_of(b):
                return dve.value_load(t_exp[0:1, bass.ds(b, 1)], min_val=0, max_val=EXPERTS - 1)

            def keep_places(b, q, i):
                dve.wait_ge(block_in[i], 16 * (q + 1))
                if not (isinstance(b, int) and b < RING):
                    dve.wait_ge(y_out[i], 16 * (BR // P) * q)
                dve.tensor_copy(wd[i][:], xb[i][:, :, C:ROW]).then_inc(S["wd_ready"], 1)

            def weigh(b, i):
                k = i % RING
                dve.wait_ge(S["y_turned"], b + 3)
                dve.wait_ge(S["wd_ready"], b + 1)
                for j in range(BR // P):
                    ins = dve.tensor_scalar(yb[k][:, j, :], pyt[:, C * j:C * j + C], wd[k][:, j, 0:1], None, ALU.mult)
                ins.then_inc(S["y_ready"], 1)

            def b_step(b, q, i):
                static = isinstance(b, int)
                if not static or b + 1 < BLOCKS:
                    x_part(b + 1, q + (i + 1) // RING, (i + 1) % RING)
                if not static or b >= 3:
                    weigh(b - 3, i - 3)
                if not static or 1 <= b <= BLOCKS:
                    k = (i - 1) % 2
                    dve.wait_ge(S["g_hi"], b)
                    dve.tensor_tensor(gl[k][:], g[k][:], gh[k][:].bitcast(F32), ALU.subtract).then_inc(S["g_lo"], 1)
                    e = expert_of(b - 1)
                if not static or b + 2 < BLOCKS:
                    e2 = expert_of(b + 2)
                if not static or 1 <= b <= BLOCKS:
                    keep_places(b - 1, (b - 1) // RING if static else q - (i < 1), (i - 1) % RING)
                    take_weights(e, b - 1, i - 1, 1, w2s, S["w2_ready"])
                if not static or b + 2 < BLOCKS:
                    take_weights(e2, b + 2, i, 0, w1s, S["w1_ready"])

            x_part(0, 0, 0)
            for b in range(2):
                take_weights(expert_of(b), b, b, 0, w1s, S["w1_ready"])
            b_loop(dve, b_step)

            fin = Chain(dve, S["dve_c"], 14)
            for part, (a, tiles) in enumerate(PARTS):
                h = x1c[:, a:a + tiles, :]
                fin.round(part)
                dve.wait_ge(S["added"], part + 1)
                y = statistics(fin, h, cstat[:, 0:tiles], cmv[:, 0:tiles], cva[:, 0:tiles], [t[:, 0:tiles] for t in cnwt])
                if part >= 2:
                    dve.wait_ge(S["c_ready"], part - 1)
                fin.mark(dve.tensor_copy(crstd[part % 2][:, 0:tiles], y[:]))
                dve.scalar_tensor_tensor(cbias[part % 2][:, 0:tiles], cmv[:, 0:tiles, 0], -1.0, y[:], ALU.mult, ALU.mult).then_inc(S["c_scale"], 1)
                fin.wait()
                dve.wait_ge(S["c_scale"], part + 1)


def kernel(L0_attn_x, L0_attn_Wqk, L0_attn_bqk, L0_attn_Wgate, L0_attn_bgate, L0_attn_Wproj,
           L0_attn_bproj, L0_ffn_router_w, L0_ffn_w1, L0_ffn_b1, L0_ffn_w2, L0_ffn_b2):
    import numpy as np
    import concourse.bacc as bacc
    from concourse.bass_utils import run_bass_kernel_spmd

    f4 = np.float32
    x = np.asarray(L0_attn_x).reshape(SEQS * T, C)
    wqk, bqk = np.asarray(L0_attn_Wqk), np.asarray(L0_attn_bqk)
    rep = np.array([D * h + d for h in range(WIDE) for _ in range(4) for d in range(D)])
    bk = bqk[C:2 * C]
    w_att = np.concatenate([wqk[:, C + rep], wqk[:, rep], wqk[:, C:2 * C], wqk[:, WIDE * D:C],
                            np.asarray(L0_attn_Wgate), np.asarray(L0_attn_Wproj),
                            np.asarray(L0_ffn_router_w).T, bk[rep][:, None], bqk[rep][:, None]], axis=1)
    b_att = np.concatenate([bk, bqk[WIDE * D:C], np.asarray(L0_attn_bgate), np.asarray(L0_attn_bproj)])
    b_att = np.stack([b_att, b_att])
    w1 = np.asarray(L0_ffn_w1).transpose(2, 0, 1).reshape(C, EXPERTS * F)
    w2 = np.asarray(L0_ffn_w2).reshape(EXPERTS, C, FC, P).transpose(3, 0, 2, 1).reshape(P, EXPERTS * F)
    w12 = np.concatenate([w1.reshape(P, EXPERTS, F), w2.reshape(P, EXPERTS, F)], axis=2).reshape(P, EXPERTS * 2 * F)
    b12 = np.concatenate([np.asarray(L0_ffn_b1).reshape(EXPERTS, FC, P), np.asarray(L0_ffn_b2)[:, None, :]],
                         axis=1).transpose(2, 0, 1).reshape(P, EXPERTS * (FC + 1))

    k = np.zeros((P, K_COLS), f4)
    k[:, K_ID:K_ID + P] = np.eye(P)
    q = np.arange(P)[:, None]
    for h, w in enumerate(WINDOWS):
        key = np.arange(KEYS[h])[None, :] - w
        ok = (key <= q) & (key > q - w)
        k[:, K_MN + KEY_AT[h]:K_MN + KEY_AT[h] + KEYS[h]] = np.where(ok, 0.0, LOW)
    off = np.concatenate([np.repeat(np.arange(OFFS)[::-1], NARROW), np.arange(OFFS, 2 * OFFS)[::-1]])[None, :]
    k[:, K_SM:K_SM + PAIRS] = np.where(off <= q, 0.0, LOW)
    part = (np.arange(P) // D) % 4
    k[:, K_NK] = -(part % 2)
    k[:, K_NQ] = -(part // 2)
    k[1, K_NB] = -1.0
    k[:, K_I8:K_I8 + EXPERTS] = np.arange(EXPERTS)
    k[:, K_EC:K_EC + EXPERTS] = np.arange(EXPERTS) * CAP
    k[:, K_TRI:K_TRI + P] = np.triu(np.ones((P, P)), 1)
    r = np.zeros((1, R_COLS), f4)
    r[0, R_B:R_B + BLOCKS] = np.arange(BLOCKS)
    r[0, R_E:R_E + 8] = np.arange(8)
    r[0, R_M:R_M + MOST] = np.arange(MOST) * BR
    r[0, R_TRI:R_TRI + 64] = np.tril(np.ones((8, 8))).reshape(-1)
    r[0, R_EB:R_EB + 8] = np.arange(8) * CAP
    places = np.arange(PLACES).reshape(TOP * SEQS * TILES, P).T.astype(np.int32)

    nc = bacc.Bacc("TRN2", target_bir_lowering=False, num_devices=1)
    arrays, args = {}, []
    for name, a in (("x", x), ("xt", x.T), ("w_att", w_att), ("b_att", b_att), ("w12", w12),
                    ("b12", b12), ("consts", k), ("rowc", r), ("places", places)):
        a = np.ascontiguousarray(a)
        arrays[name] = a
        args.append(nc.dram_tensor(name, a.shape, mybir.dt.from_np(a.dtype), kind="ExternalInput").ap())
    args.append(nc.dram_tensor("out", (SEQS * T, C), F32, kind="ExternalOutput").ap())
    program(nc, *args)
    got = run_bass_kernel_spmd(nc, [arrays], core_ids=[0])
    return got.results[0]["out"].reshape(SEQS, T, C)
```
